# Optimizing a Trainium2 kernel written in Bass

```python
import numpy as np
import jax
import jax.numpy as jnp

def _softmax(x, axis=-1):
    return jax.nn.softmax(x, axis=axis)

def _gelu(x):
    return jax.nn.gelu(x, approximate=True)

def _silu(x):
    return jax.nn.silu(x)

def _sigmoid(x):
    return jax.nn.sigmoid(x)

def _layernorm(x, axis=-1, eps=1e-05):
    m = jnp.mean(x, axis=axis, keepdims=True)
    v = jnp.var(x, axis=axis, keepdims=True)
    return (x - m) / jnp.sqrt(v + eps)

def _scatter_add(tgt, idx, src, axis=0):
    return tgt.at[idx].add(src)

def _segment_sum(src, seg, n):
    return jax.ops.segment_sum(src, seg, n)
kernel_name = 'mk_flamingo_gated_d4_seqx_r4_e01fea'

def setup_inputs(seed: int=0):
    np.random.seed(seed)
    _w = jnp.asarray

    def _rec_inputs():
        import jax
        import jax.numpy as jnp
        _rk = jax.random.key(seed)
        x = 7.22e-05 + 1 * jax.random.normal(jax.random.fold_in(_rk, 1), (4, 512, 256), jnp.float32)
        _lenS = 512 - jax.random.randint(jax.random.fold_in(_rk, 7), (4,), 0, max(1, 512 // 4) + 1, jnp.int32)
        _lenS2 = 512 - jax.random.randint(jax.random.fold_in(_rk, 8), (4,), 0, max(1, 512 // 4) + 1, jnp.int32)
        _ctx_1024P = jax.random.normal(jax.random.fold_in(_rk, 11), (4, 16, 256), jnp.float32)
        _ctx_1024c = jax.random.dirichlet(jax.random.fold_in(_rk, 511), 0.3 * jnp.ones((16,), jnp.float32), (4, 512))
        _ctx_1024t = jnp.einsum('bsk,bkd->bsd', _ctx_1024c, _ctx_1024P)
        _ctx_1024t = _ctx_1024t * jax.lax.rsqrt(jnp.mean(jnp.square(_ctx_1024t)) + 1e-12) * 0.953939
        ctx_1024 = -0.000514642 + 1.00011 * (_ctx_1024t + 0.3 * jax.random.normal(jax.random.fold_in(_rk, 611), (4, 512, 256), jnp.float32))
        itok_BxS_0_511 = jax.random.randint(jax.random.fold_in(_rk, 12), (4, 512), 0, 128, jnp.int32)
        _validS = jnp.arange(512)[None, :] < _lenS[:, None]
        _validS2 = jnp.arange(512)[None, :] < _lenS2[:, None]
        _causal = jnp.tril(jnp.ones((512, 512), dtype=bool))
        mask_BxS2_ik0 = jnp.where(jnp.broadcast_to(_validS2[:, :], (4, 512)), 0, 1).astype(jnp.int32)
        _g = jax.random.normal(jax.random.fold_in(_rk, 9001), (2, 4), jnp.float32)
        _g = jnp.sign(_g) * jnp.maximum(jnp.abs(_g), 1.0) + (_g == 0) * 1.0
        g_xattn = _g[0]
        g_ffn = _g[1]
        return (x, ctx_1024, itok_BxS_0_511, mask_BxS2_ik0, g_xattn, g_ffn)
    x, ctx_1024, itok_BxS_0_511, mask_BxS2_ik0, g_xattn, g_ffn = _rec_inputs()

    def _L0_xattn_setup():
        import jax, jax.numpy as jnp
        import numpy as np
        Q_DIM, KV_DIM = (256, 256)
        H, HD, KVC, QC, R = (16, 64, 64, 96, 64)
        LOOKBACK = 2
        B, LQ, LK = (4, 512, 128)

        def _rope(x, pos):
            r = x.shape[-1]
            half = r // 2
            inv = 1.0 / 10000.0 ** (jnp.arange(half, dtype=jnp.float32) / half)
            ang = pos[..., None].astype(jnp.float32) * inv
            cos, sin = (jnp.cos(ang), jnp.sin(ang))
            x1, x2 = (x[..., :half], x[..., half:])
            return jnp.concatenate([x1 * cos - x2 * sin, x1 * sin + x2 * cos], axis=-1)
        key = jax.random.key(seed)
        ks = jax.random.split(key, 11)
        w = lambda k, shape: jax.random.normal(k, shape, jnp.float32) / np.sqrt(shape[0]).astype(np.float32)
        return {'q': jax.random.normal(ks[0], (B, LQ, Q_DIM), jnp.float32), 'kv': jax.random.normal(ks[1], (B, LK, KV_DIM), jnp.float32), 'seg_id': jnp.sort(jax.random.randint(ks[2], (B, LQ), 0, LK), axis=-1), 'w_kv_comp': w(ks[3], (KV_DIM, KVC)), 'w_q_down': w(ks[4], (Q_DIM, QC)), 'w_q_up': w(ks[5], (QC, H * HD)), 'w_q_rope': w(ks[6], (QC, H * R)), 'w_k_up': w(ks[7], (KVC, H * HD)), 'w_k_rope': w(ks[8], (KVC, R)), 'w_v_up': w(ks[9], (KVC, H * HD)), 'w_out': w(ks[10], (H * HD, Q_DIM))}
    _L0_xattn_all = _L0_xattn_setup()
    _L0_xattn_in = {k: v for k, v in _L0_xattn_all.items() if k in ('w_kv_comp', 'w_q_down', 'w_q_up', 'w_q_rope', 'w_k_up', 'w_k_rope', 'w_v_up', 'w_out')}
    del _L0_xattn_all

    def _L0_ffn_setup():
        import jax, jax.numpy as jnp
        import numpy as np
        H = 256
        I = 512
        E = 8
        B, S = (2, 1024)
        EPS = 1e-05
        INIT = 0.02

        def _layernorm(x, w, b):
            mu = jnp.mean(x, axis=-1, keepdims=True)
            var = jnp.mean(jnp.square(x - mu), axis=-1, keepdims=True)
            return (x - mu) * jax.lax.rsqrt(var + EPS) * w + b
        key = jax.random.key(seed)
        ks = jax.random.split(key, 9)
        return {'hidden_states': jax.random.normal(ks[0], (B, S, H), jnp.float32), 'ln_w': jnp.ones((H,), jnp.float32), 'ln_b': jnp.zeros((H,), jnp.float32), 'router_w': jax.random.normal(ks[1], (H, E), jnp.float32) * INIT, 'gate_w': jax.random.normal(ks[2], (E, H, I), jnp.float32) * INIT, 'up_w': jax.random.normal(ks[3], (E, H, I), jnp.float32) * INIT, 'down_w': jax.random.normal(ks[4], (E, I, H), jnp.float32) * INIT, 'sh_gate': jax.random.normal(ks[5], (H, I), jnp.float32) * INIT, 'sh_up': jax.random.normal(ks[6], (H, I), jnp.float32) * INIT, 'sh_down': jax.random.normal(ks[7], (I, H), jnp.float32) * INIT}
    _L0_ffn_all = _L0_ffn_setup()
    _L0_ffn_in = {k: v for k, v in _L0_ffn_all.items() if k in ('ln_w', 'ln_b', 'router_w', 'gate_w', 'up_w', 'down_w', 'sh_gate', 'sh_up', 'sh_down')}
    del _L0_ffn_all

    def _L1_xattn_setup():
        import jax, jax.numpy as jnp
        import numpy as np
        B, C_LEN, Q_LEN, D = (8, 512, 128, 256)
        key = jax.random.key(seed)
        ks = jax.random.split(key, 10)
        scale = 1.0 / np.sqrt(D)
        return {'c': jax.random.normal(ks[0], (B, C_LEN, D), dtype=jnp.float32), 'q': jax.random.normal(ks[1], (B, Q_LEN, D), dtype=jnp.float32), 'w_cq': jax.random.normal(ks[2], (D,), dtype=jnp.float32) * scale, 'b_cq': jax.random.normal(ks[3], (), dtype=jnp.float32) * scale, 'w_c': jax.random.normal(ks[4], (D,), dtype=jnp.float32) * scale, 'b_c': jax.random.normal(ks[5], (), dtype=jnp.float32) * scale, 'w_q': jax.random.normal(ks[6], (D,), dtype=jnp.float32) * scale, 'b_q': jax.random.normal(ks[7], (), dtype=jnp.float32) * scale, 'W_l': jax.random.normal(ks[8], (D, 4 * D), dtype=jnp.float32) * (1.0 / np.sqrt(4 * D)), 'b_l': jax.random.normal(ks[9], (D,), dtype=jnp.float32) * (1.0 / np.sqrt(4 * D))}
    _L1_xattn_all = _L1_xattn_setup()
    _L1_xattn_in = {k: v for k, v in _L1_xattn_all.items() if k in ('w_cq', 'b_cq', 'w_c', 'b_c', 'w_q', 'b_q', 'W_l', 'b_l')}
    del _L1_xattn_all

    def _L1_ffn_setup():
        import jax, jax.numpy as jnp
        import numpy as np
        CAPACITY_FACTOR = 0.5
        NUM_HEADS = 16
        key = jax.random.key(seed)
        ks = jax.random.split(key, 6)
        B, N, D = (4, 1024, 256)
        s = 1.0 / np.sqrt(D)
        return {'token_inputs': jax.random.normal(ks[0], (B, N, D), jnp.float32), 'Wg': jax.random.normal(ks[1], (D, 1), jnp.float32) * s, 'Wq': jax.random.normal(ks[2], (D, D), jnp.float32) * s, 'Wk': jax.random.normal(ks[3], (D, D), jnp.float32) * s, 'Wv': jax.random.normal(ks[4], (D, D), jnp.float32) * s, 'Wo': jax.random.normal(ks[5], (D, D), jnp.float32) * s}
    _L1_ffn_all = _L1_ffn_setup()
    _L1_ffn_in = {k: v for k, v in _L1_ffn_all.items() if k in ('Wg', 'Wq', 'Wk', 'Wv', 'Wo')}
    del _L1_ffn_all

    def _L2_xattn_setup():
        import jax, jax.numpy as jnp
        import numpy as np
        B, S, D = (4, 512, 256)
        H = 16
        DH = D // H
        HID = 64
        NEG = 1e+18
        key = jax.random.key(seed)
        ks = jax.random.split(key, 12)
        inp = {'query': jax.random.normal(ks[0], (B, S, D), dtype=jnp.float32), 'key': jax.random.normal(ks[1], (B, S, D), dtype=jnp.float32), 'value': jax.random.normal(ks[2], (B, S, D), dtype=jnp.float32), 'key_mask': jax.random.randint(ks[3], (B, S), 0, 2, dtype=jnp.int32), 'Wq': jax.random.normal(ks[4], (H, DH, HID), dtype=jnp.float32) * 0.05, 'bq': jnp.zeros((H, HID), dtype=jnp.float32), 'Wk': jax.random.normal(ks[5], (H, DH, HID), dtype=jnp.float32) * 0.05, 'bk': jnp.zeros((H, HID), dtype=jnp.float32), 'Wv': jax.random.normal(ks[6], (H, DH, HID), dtype=jnp.float32) * 0.05, 'bv': jnp.zeros((H, HID), dtype=jnp.float32), 'Wo': jax.random.normal(ks[7], (H * HID, D), dtype=jnp.float32) * 0.05, 'bo': jnp.zeros((D,), dtype=jnp.float32)}
        return inp
    _L2_xattn_all = _L2_xattn_setup()
    _L2_xattn_in = {k: v for k, v in _L2_xattn_all.items() if k in ('Wq', 'bq', 'Wk', 'bk', 'Wv', 'bv', 'Wo', 'bo')}
    del _L2_xattn_all

    def _L2_ffn_setup():
        import math
        import jax, jax.numpy as jnp
        import numpy as np
        D_MODEL = 256
        D_FF = 1024
        N_EXPERTS = 8
        CAPACITY_FACTOR = 1.25
        L, B = (128, 8)

        def _route(tokens, router_w):
            T = tokens.shape[0]
            E = router_w.shape[0]
            capacity = int(math.ceil(T / E * CAPACITY_FACTOR))
            logits = tokens @ router_w.T
            probs = jax.nn.softmax(logits, axis=-1)
            top1_idx = jnp.argmax(probs, axis=-1)
            top1_prob = jnp.max(probs, axis=-1)
            order = jnp.lexsort((-top1_prob, top1_idx))
            sorted_e = top1_idx[order]
            counts = jnp.bincount(top1_idx, length=E)
            start = jnp.cumsum(counts) - counts
            pos_in_group = jnp.arange(T) - start[sorted_e]
            keep_sorted = pos_in_group < capacity
            keep = jnp.zeros((T,), bool).at[order].set(keep_sorted)
            return jnp.where(keep, top1_idx, 0).astype(jnp.int32)
        key = jax.random.key(seed)
        ks = jax.random.split(key, 6)
        s_in = 1.0 / math.sqrt(D_MODEL)
        s_ff = 1.0 / math.sqrt(D_FF)
        return {'x': jax.random.normal(ks[0], (L, B, D_MODEL), dtype=jnp.float32), 'router_w': jax.random.uniform(ks[1], (N_EXPERTS, D_MODEL), minval=-s_in, maxval=s_in), 'W1': jax.random.uniform(ks[2], (N_EXPERTS, D_MODEL, D_FF), minval=-s_in, maxval=s_in), 'b1': jax.random.uniform(ks[3], (N_EXPERTS, D_FF), minval=-s_in, maxval=s_in), 'W2': jax.random.uniform(ks[4], (N_EXPERTS, D_FF, D_MODEL), minval=-s_ff, maxval=s_ff), 'b2': jax.random.uniform(ks[5], (N_EXPERTS, D_MODEL), minval=-s_ff, maxval=s_ff)}
    _L2_ffn_all = _L2_ffn_setup()
    _L2_ffn_in = {k: v for k, v in _L2_ffn_all.items() if k in ('router_w', 'W1', 'b1', 'W2', 'b2')}
    del _L2_ffn_all

    def _L3_xattn_setup():
        import jax, jax.numpy as jnp
        import numpy as np
        B, S, D, H, W = (2, 1024, 256, 16, 16)
        HD = D // H
        key = jax.random.key(seed)
        ks = jax.random.split(key, 10)
        std = 0.02
        mk_w = lambda k: jax.random.normal(k, (D, D), jnp.float32) * std
        mk_b = lambda k: jax.random.normal(k, (D,), jnp.float32) * std
        return {'query': jax.random.normal(ks[0], (B, S, D), jnp.float32), 'kv': jax.random.normal(ks[1], (B, S, D), jnp.float32), 'Wq': mk_w(ks[2]), 'bq': mk_b(ks[3]), 'Wk': mk_w(ks[4]), 'bk': mk_b(ks[5]), 'Wv': mk_w(ks[6]), 'bv': mk_b(ks[7]), 'Wo': mk_w(ks[8]), 'bo': mk_b(ks[9]), 'is_causal': 1}
    _L3_xattn_all = _L3_xattn_setup()
    _L3_xattn_in = {k: v for k, v in _L3_xattn_all.items() if k in ('Wq', 'bq', 'Wk', 'bk', 'Wv', 'bv', 'Wo', 'bo')}
    del _L3_xattn_all

    def _L3_ffn_setup():
        import jax, jax.numpy as jnp
        import numpy as np
        EMB = 256
        FF = 4 * EMB

        def _ternary(w):
            scale = jnp.maximum(jnp.mean(jnp.abs(w)), 1e-08)
            w_t = jnp.clip(jnp.round(w / scale), -1.0, 1.0)
            return w + jax.lax.stop_gradient(w_t - w)
        key = jax.random.key(seed)
        kx, k1, k2, kb1, kb2 = jax.random.split(key, 5)
        x = jax.random.normal(kx, (4, 512, EMB), dtype=jnp.float32)
        lim1 = 1.0 / np.sqrt(EMB)
        lim2 = 1.0 / np.sqrt(FF)
        W1 = jax.random.uniform(k1, (FF, EMB), jnp.float32, -lim1, lim1)
        b1 = jax.random.uniform(kb1, (FF,), jnp.float32, -lim1, lim1)
        W2 = jax.random.uniform(k2, (EMB, FF), jnp.float32, -lim2, lim2)
        b2 = jax.random.uniform(kb2, (EMB,), jnp.float32, -lim2, lim2)
        return {'x': x, 'W1': W1, 'b1': b1, 'W2': W2, 'b2': b2}
    _L3_ffn_all = _L3_ffn_setup()
    _L3_ffn_in = {k: v for k, v in _L3_ffn_all.items() if k in ('W1', 'b1', 'W2', 'b2')}
    del _L3_ffn_all
    return {'x': x, 'ctx_1024': ctx_1024, 'itok_BxS_0_511': itok_BxS_0_511, 'mask_BxS2_ik0': mask_BxS2_ik0, 'g_xattn': g_xattn, 'g_ffn': g_ffn, 'L0_xattn_w_kv_comp': _L0_xattn_in['w_kv_comp'], 'L0_xattn_w_q_down': _L0_xattn_in['w_q_down'], 'L0_xattn_w_q_up': _L0_xattn_in['w_q_up'], 'L0_xattn_w_q_rope': _L0_xattn_in['w_q_rope'], 'L0_xattn_w_k_up': _L0_xattn_in['w_k_up'], 'L0_xattn_w_k_rope': _L0_xattn_in['w_k_rope'], 'L0_xattn_w_v_up': _L0_xattn_in['w_v_up'], 'L0_xattn_w_out': _L0_xattn_in['w_out'], 'L0_ffn_ln_w': _L0_ffn_in['ln_w'], 'L0_ffn_ln_b': _L0_ffn_in['ln_b'], 'L0_ffn_router_w': _L0_ffn_in['router_w'], 'L0_ffn_gate_w': _L0_ffn_in['gate_w'], 'L0_ffn_up_w': _L0_ffn_in['up_w'], 'L0_ffn_down_w': _L0_ffn_in['down_w'], 'L0_ffn_sh_gate': _L0_ffn_in['sh_gate'], 'L0_ffn_sh_up': _L0_ffn_in['sh_up'], 'L0_ffn_sh_down': _L0_ffn_in['sh_down'], 'L1_xattn_w_cq': _L1_xattn_in['w_cq'], 'L1_xattn_b_cq': _L1_xattn_in['b_cq'], 'L1_xattn_w_c': _L1_xattn_in['w_c'], 'L1_xattn_b_c': _L1_xattn_in['b_c'], 'L1_xattn_w_q': _L1_xattn_in['w_q'], 'L1_xattn_b_q': _L1_xattn_in['b_q'], 'L1_xattn_W_l': _L1_xattn_in['W_l'], 'L1_xattn_b_l': _L1_xattn_in['b_l'], 'L1_ffn_Wg': _L1_ffn_in['Wg'], 'L1_ffn_Wq': _L1_ffn_in['Wq'], 'L1_ffn_Wk': _L1_ffn_in['Wk'], 'L1_ffn_Wv': _L1_ffn_in['Wv'], 'L1_ffn_Wo': _L1_ffn_in['Wo'], 'L2_xattn_Wq': _L2_xattn_in['Wq'], 'L2_xattn_bq': _L2_xattn_in['bq'], 'L2_xattn_Wk': _L2_xattn_in['Wk'], 'L2_xattn_bk': _L2_xattn_in['bk'], 'L2_xattn_Wv': _L2_xattn_in['Wv'], 'L2_xattn_bv': _L2_xattn_in['bv'], 'L2_xattn_Wo': _L2_xattn_in['Wo'], 'L2_xattn_bo': _L2_xattn_in['bo'], 'L2_ffn_router_w': _L2_ffn_in['router_w'], 'L2_ffn_W1': _L2_ffn_in['W1'], 'L2_ffn_b1': _L2_ffn_in['b1'], 'L2_ffn_W2': _L2_ffn_in['W2'], 'L2_ffn_b2': _L2_ffn_in['b2'], 'L3_xattn_Wq': _L3_xattn_in['Wq'], 'L3_xattn_bq': _L3_xattn_in['bq'], 'L3_xattn_Wk': _L3_xattn_in['Wk'], 'L3_xattn_bk': _L3_xattn_in['bk'], 'L3_xattn_Wv': _L3_xattn_in['Wv'], 'L3_xattn_bv': _L3_xattn_in['bv'], 'L3_xattn_Wo': _L3_xattn_in['Wo'], 'L3_xattn_bo': _L3_xattn_in['bo'], 'L3_ffn_W1': _L3_ffn_in['W1'], 'L3_ffn_b1': _L3_ffn_in['b1'], 'L3_ffn_W2': _L3_ffn_in['W2'], 'L3_ffn_b2': _L3_ffn_in['b2']}

def reference(x, ctx_1024, itok_BxS_0_511, mask_BxS2_ik0, g_xattn, g_ffn, L0_xattn_w_kv_comp, L0_xattn_w_q_down, L0_xattn_w_q_up, L0_xattn_w_q_rope, L0_xattn_w_k_up, L0_xattn_w_k_rope, L0_xattn_w_v_up, L0_xattn_w_out, L0_ffn_ln_w, L0_ffn_ln_b, L0_ffn_router_w, L0_ffn_gate_w, L0_ffn_up_w, L0_ffn_down_w, L0_ffn_sh_gate, L0_ffn_sh_up, L0_ffn_sh_down, L1_xattn_w_cq, L1_xattn_b_cq, L1_xattn_w_c, L1_xattn_b_c, L1_xattn_w_q, L1_xattn_b_q, L1_xattn_W_l, L1_xattn_b_l, L1_ffn_Wg, L1_ffn_Wq, L1_ffn_Wk, L1_ffn_Wv, L1_ffn_Wo, L2_xattn_Wq, L2_xattn_bq, L2_xattn_Wk, L2_xattn_bk, L2_xattn_Wv, L2_xattn_bv, L2_xattn_Wo, L2_xattn_bo, L2_ffn_router_w, L2_ffn_W1, L2_ffn_b1, L2_ffn_W2, L2_ffn_b2, L3_xattn_Wq, L3_xattn_bq, L3_xattn_Wk, L3_xattn_bk, L3_xattn_Wv, L3_xattn_bv, L3_xattn_Wo, L3_xattn_bo, L3_ffn_W1, L3_ffn_b1, L3_ffn_W2, L3_ffn_b2):
    import jax
    import jax.numpy as jnp

    def _L0_xattn_ref(q, kv, seg_id, w_kv_comp, w_q_down, w_q_up, w_q_rope, w_k_up, w_k_rope, w_v_up, w_out):
        import jax, jax.numpy as jnp
        import numpy as np
        Q_DIM, KV_DIM = (256, 256)
        H, HD, KVC, QC, R = (16, 64, 64, 96, 64)
        LOOKBACK = 2
        B, LQ, LK = (4, 512, 128)

        def _rope(x, pos):
            r = x.shape[-1]
            half = r // 2
            inv = 1.0 / 10000.0 ** (jnp.arange(half, dtype=jnp.float32) / half)
            ang = pos[..., None].astype(jnp.float32) * inv
            cos, sin = (jnp.cos(ang), jnp.sin(ang))
            x1, x2 = (x[..., :half], x[..., half:])
            return jnp.concatenate([x1 * cos - x2 * sin, x1 * sin + x2 * cos], axis=-1)
        b, lq, _ = q.shape
        lk = kv.shape[1]
        kv_c = kv @ w_kv_comp
        qc = q @ w_q_down
        q_nope = (qc @ w_q_up).reshape(b, lq, H, HD)
        q_rope = (qc @ w_q_rope).reshape(b, lq, H, R)
        q_rope = _rope(q_rope, jnp.arange(lq)[None, :, None])
        k_nope = (kv_c @ w_k_up).reshape(b, lk, H, HD)
        k_rope = _rope(kv_c @ w_k_rope, jnp.arange(lk)[None, :])
        v = (kv_c @ w_v_up).reshape(b, lk, H, HD)
        scale = 1.0 / np.sqrt(HD + R).astype(np.float32)
        scores = (jnp.einsum('bqhd,bkhd->bhqk', q_nope, k_nope) + jnp.einsum('bqhr,bkr->bhqk', q_rope, k_rope)) * scale
        k_idx = jnp.arange(lk)[None, None, :]
        q_seg = seg_id[:, :, None]
        good = (k_idx <= q_seg) & (k_idx >= q_seg - LOOKBACK)
        neg = jnp.finfo(scores.dtype).min
        scores = jnp.where(good[:, None, :, :], scores, neg)
        attn = jax.nn.softmax(scores, axis=-1)
        out = jnp.einsum('bhqk,bkhd->bqhd', attn, v).reshape(b, lq, H * HD)
        return out @ w_out

    def _L0_ffn_ref(hidden_states, ln_w, ln_b, router_w, gate_w, up_w, down_w, sh_gate, sh_up, sh_down):
        import jax, jax.numpy as jnp
        import numpy as np
        H = 256
        I = 512
        E = 8
        B, S = (2, 1024)
        EPS = 1e-05
        INIT = 0.02

        def _layernorm(x, w, b):
            mu = jnp.mean(x, axis=-1, keepdims=True)
            var = jnp.mean(jnp.square(x - mu), axis=-1, keepdims=True)
            return (x - mu) * jax.lax.rsqrt(var + EPS) * w + b
        b, s, h = hidden_states.shape
        normed = _layernorm(hidden_states, ln_w, ln_b)
        xf = normed.reshape(-1, h)
        logits = xf @ router_w
        top_idx = jnp.argmax(logits, axis=-1)
        top_score = jax.nn.sigmoid(jnp.max(logits, axis=-1))

        def body(acc, ew):
            g, u, d, e = ew
            w = jnp.where(top_idx == e, top_score, 0.0)[:, None]
            xe = xf * w
            hmid = jax.nn.silu(xe @ g) * (xe @ u)
            return (acc + hmid @ d, None)
        routed, _ = jax.lax.scan(body, jnp.zeros_like(xf), (gate_w, up_w, down_w, jnp.arange(E)))
        shared = jax.nn.silu(xf @ sh_gate) * (xf @ sh_up) @ sh_down
        moe_out = (routed + shared).reshape(b, s, h)
        return hidden_states + moe_out

    def _L1_xattn_ref(c, q, w_cq, b_cq, w_c, b_c, w_q, b_q, W_l, b_l):
        import jax, jax.numpy as jnp
        import numpy as np
        B, C_LEN, Q_LEN, D = (8, 512, 128, 256)
        cq = jnp.einsum('bcd,bqd,d->bcq', c, q, w_cq) + b_cq
        s = (c @ w_c + b_c)[:, :, None] + (q @ w_q + b_q)[:, None, :] + cq
        a = jax.nn.softmax(s, axis=2)
        c2q_att = jnp.einsum('bcq,bqd->bcd', a, q)
        b_att = jax.nn.softmax(jnp.max(s, axis=2), axis=1)
        q2c_att = jnp.einsum('bc,bcd->bd', b_att, c)[:, None, :]
        x = jnp.concatenate([c, c2q_att, c * c2q_att, c * q2c_att], axis=-1)
        z = x @ W_l.T + b_l
        return z

    def _L1_ffn_ref(token_inputs, Wg, Wq, Wk, Wv, Wo):
        import jax, jax.numpy as jnp
        import numpy as np
        CAPACITY_FACTOR = 0.5
        NUM_HEADS = 16
        B, N, D = token_inputs.shape
        C = int(N * CAPACITY_FACTOR)
        H = NUM_HEADS
        dh = D // H
        gate = jax.nn.sigmoid((token_inputs @ Wg)[..., 0])
        _, idx = jax.lax.top_k(gate, C)
        attn_in = jnp.take_along_axis(token_inputs, idx[..., None], axis=1)
        q = (attn_in @ Wq).reshape(B, C, H, dh)
        k = (attn_in @ Wk).reshape(B, C, H, dh)
        v = (attn_in @ Wv).reshape(B, C, H, dh)
        scores = jnp.einsum('bqhd,bkhd->bhqk', q, k) / jnp.sqrt(jnp.float32(dh))
        attn = jax.nn.softmax(scores, axis=-1)
        o = jnp.einsum('bhqk,bkhd->bqhd', attn, v).reshape(B, C, D) @ Wo
        gate_sel = jnp.take_along_axis(gate, idx, axis=1)
        out = jnp.zeros_like(token_inputs)
        out = out.at[jnp.arange(B)[:, None], idx].set(o * gate_sel[..., None])
        return out

    def _L2_xattn_ref(query, key, value, key_mask, Wq, bq, Wk, bk, Wv, bv, Wo, bo):
        import jax, jax.numpy as jnp
        import numpy as np
        B, S, D = (4, 512, 256)
        H = 16
        DH = D // H
        HID = 64
        NEG = 1e+18
        b, s, d = query.shape
        q = query.reshape(b, s, H, DH)
        k = key.reshape(b, s, H, DH)
        v = value.reshape(b, s, H, DH)
        qh = jnp.einsum('bshd,hde->bhse', q, Wq) + bq[None, :, None, :]
        kh = jnp.einsum('bshd,hde->bhse', k, Wk) + bk[None, :, None, :]
        vh = jnp.einsum('bshd,hde->bhse', v, Wv) + bv[None, :, None, :]
        scores = jnp.einsum('bhse,bhte->bhst', qh, kh)
        scores = scores - (1.0 - key_mask.astype(jnp.float32))[:, None, None, :] * NEG
        causal = (1.0 - jnp.tril(jnp.ones((s, s), dtype=jnp.float32))) * NEG
        scores = scores - causal[None, None, :, :]
        attn = jax.nn.softmax(scores, axis=-1)
        out = jnp.einsum('bhst,bhte->bhse', attn, vh)
        concat = out.transpose(0, 2, 1, 3).reshape(b, s, H * HID)
        return concat @ Wo + bo

    def _L2_ffn_ref(x, router_w, W1, b1, W2, b2):
        import math
        import jax, jax.numpy as jnp
        import numpy as np
        D_MODEL = 256
        D_FF = 1024
        N_EXPERTS = 8
        CAPACITY_FACTOR = 1.25
        L, B = (128, 8)

        def _route(tokens, router_w):
            T = tokens.shape[0]
            E = router_w.shape[0]
            capacity = int(math.ceil(T / E * CAPACITY_FACTOR))
            logits = tokens @ router_w.T
            probs = jax.nn.softmax(logits, axis=-1)
            top1_idx = jnp.argmax(probs, axis=-1)
            top1_prob = jnp.max(probs, axis=-1)
            order = jnp.lexsort((-top1_prob, top1_idx))
            sorted_e = top1_idx[order]
            counts = jnp.bincount(top1_idx, length=E)
            start = jnp.cumsum(counts) - counts
            pos_in_group = jnp.arange(T) - start[sorted_e]
            keep_sorted = pos_in_group < capacity
            keep = jnp.zeros((T,), bool).at[order].set(keep_sorted)
            return jnp.where(keep, top1_idx, 0).astype(jnp.int32)
        Lx, Bx, D = x.shape
        T = Lx * Bx
        E = router_w.shape[0]
        tokens = x.reshape(T, D)
        final_e = _route(tokens, router_w)
        out = jnp.zeros_like(tokens)
        for e in range(E):
            h = jax.nn.relu(tokens @ W1[e] + b1[e])
            y = h @ W2[e] + b2[e]
            out = out + jnp.where((final_e == e)[:, None], y, 0.0)
        return out.reshape(Lx, Bx, D)

    def _L3_xattn_ref(query, kv, Wq, bq, Wk, bk, Wv, bv, Wo, bo, is_causal):
        import jax, jax.numpy as jnp
        import numpy as np
        B, S, D, H, W = (2, 1024, 256, 16, 16)
        HD = D // H
        b, s, d = query.shape

        def split_heads(x):
            return x.reshape(b, s, H, HD).transpose(0, 2, 1, 3)
        Q = split_heads(query @ Wq.T + bq)
        K = split_heads(kv @ Wk.T + bk)
        V = split_heads(kv @ Wv.T + bv)
        pad = W - 1
        Kp = jnp.pad(K, ((0, 0), (0, 0), (pad, 0), (0, 0)))
        Vp = jnp.pad(V, ((0, 0), (0, 0), (pad, 0), (0, 0)))
        idx = jnp.arange(s)[:, None] + jnp.arange(W)[None, :]
        Kw = Kp[:, :, idx]
        Vw = Vp[:, :, idx]
        scores = jnp.einsum('bhsd,bhswd->bhsw', Q, Kw) / np.sqrt(HD).astype(np.float32)
        if is_causal:
            mask = jnp.arange(W)[None, :] <= jnp.arange(s)[:, None]
            scores = jnp.where(mask[None, None], scores, -jnp.inf)
        attn = jax.nn.softmax(scores, axis=-1)
        out = jnp.einsum('bhsw,bhswd->bhsd', attn, Vw)
        out = out.transpose(0, 2, 1, 3).reshape(b, s, d)
        return out @ Wo.T + bo

    def _L3_ffn_ref(x, W1, b1, W2, b2):
        import jax, jax.numpy as jnp
        import numpy as np
        EMB = 256
        FF = 4 * EMB

        def _ternary(w):
            scale = jnp.maximum(jnp.mean(jnp.abs(w)), 1e-08)
            w_t = jnp.clip(jnp.round(w / scale), -1.0, 1.0)
            return w + jax.lax.stop_gradient(w_t - w)
        h = jnp.einsum('bsd,fd->bsf', x, _ternary(W1)) + b1
        h = jax.nn.gelu(h, approximate=False)
        out = jnp.einsum('bsf,df->bsd', h, _ternary(W2)) + b2
        return out
    x = x + jnp.tanh(g_xattn[0]) * _L0_xattn_ref(_layernorm(x, axis=-1), ctx_1024, itok_BxS_0_511, L0_xattn_w_kv_comp, L0_xattn_w_q_down, L0_xattn_w_q_up, L0_xattn_w_q_rope, L0_xattn_w_k_up, L0_xattn_w_k_rope, L0_xattn_w_v_up, L0_xattn_w_out)
    x = x + jnp.tanh(g_ffn[0]) * _L0_ffn_ref(_layernorm(x, axis=-1), L0_ffn_ln_w, L0_ffn_ln_b, L0_ffn_router_w, L0_ffn_gate_w, L0_ffn_up_w, L0_ffn_down_w, L0_ffn_sh_gate, L0_ffn_sh_up, L0_ffn_sh_down)
    x = x + jnp.tanh(g_xattn[1]) * _L1_xattn_ref(_layernorm(x, axis=-1), ctx_1024, L1_xattn_w_cq, L1_xattn_b_cq, L1_xattn_w_c, L1_xattn_b_c, L1_xattn_w_q, L1_xattn_b_q, L1_xattn_W_l, L1_xattn_b_l)
    x = x + jnp.tanh(g_ffn[1]) * _L1_ffn_ref(_layernorm(x, axis=-1), L1_ffn_Wg, L1_ffn_Wq, L1_ffn_Wk, L1_ffn_Wv, L1_ffn_Wo)
    x = x + jnp.tanh(g_xattn[2]) * _L2_xattn_ref(_layernorm(x, axis=-1), ctx_1024, ctx_1024, mask_BxS2_ik0, L2_xattn_Wq, L2_xattn_bq, L2_xattn_Wk, L2_xattn_bk, L2_xattn_Wv, L2_xattn_bv, L2_xattn_Wo, L2_xattn_bo)
    x = x + jnp.tanh(g_ffn[2]) * _L2_ffn_ref(_layernorm(x, axis=-1), L2_ffn_router_w, L2_ffn_W1, L2_ffn_b1, L2_ffn_W2, L2_ffn_b2)
    x = x + jnp.tanh(g_xattn[3]) * _L3_xattn_ref(_layernorm(x, axis=-1), ctx_1024, L3_xattn_Wq, L3_xattn_bq, L3_xattn_Wk, L3_xattn_bk, L3_xattn_Wv, L3_xattn_bv, L3_xattn_Wo, L3_xattn_bo, 1)
    x = x + jnp.tanh(g_ffn[3]) * _L3_ffn_ref(_layernorm(x, axis=-1), L3_ffn_W1, L3_ffn_b1, L3_ffn_W2, L3_ffn_b2)
    return x

_drawn_inputs = setup_inputs


def setup_inputs(seed=0):
    import zlib

    import numpy as np

    out = dict(_drawn_inputs(seed))
    spreads = {'L0_ffn_ln_w': (1.0, 0.2),
     'L0_ffn_ln_b': (0.0, 0.1),
     'L2_xattn_bq': (0.0, 0.8),
     'L2_xattn_bk': (0.0, 2.0),
     'L2_xattn_bv': (0.0, 0.1),
     'L2_xattn_bo': (0.0, 0.1)}
    factors = {'L2_xattn_Wq': 2.898,
     'L2_xattn_Wk': 3.309,
     'L2_ffn_b1': 4.165,
     'L2_ffn_b2': 3.264,
     'L3_xattn_Wq': 8.0,
     'L3_xattn_bq': 57.295,
     'L3_xattn_Wk': 8.0,
     'L3_xattn_bk': 64.0,
     'L3_xattn_bv': 8.0,
     'L3_xattn_bo': 2.974,
     'L3_ffn_b1': 23.128,
     'L3_ffn_b2': 64.0}
    for name, (base, spread) in spreads.items():
        noise = np.random.default_rng([zlib.crc32(name.encode()), seed]).standard_normal(out[name].shape)
        drawn = base * np.exp(spread * noise) if base else spread * noise
        out[name] = jnp.asarray(drawn.astype(out[name].dtype))
    for name, factor in factors.items():
        out[name] = (out[name] * factor).astype(out[name].dtype)
    return out
```

```python
from contextlib import ExitStack

import numpy as np
import concourse.bass as bass
from concourse import mybir

F32 = mybir.dt.float32
BF16 = mybir.dt.bfloat16
I32 = mybir.dt.int32
U32 = mybir.dt.uint32
ALU = mybir.AluOpType
ACT = mybir.ActivationFunctionType
X_AXIS = mybir.AxisListType.X

P = 128
B, S, D = 4, 512, 256
T = B * S
NT = T // P
QT_B = S // P
DK = D // P
H = 16
EPS = 1e-5
F32_MIN = float(np.finfo(np.float32).min)


class Tally:

    def __init__(self, sem):
        self.sem = sem
        self.n = 0

    def mark(self, ins):
        ins.then_inc(self.sem, 1)
        self.n += 1
        return self.n


class Core:

    def __init__(self, nc, ctx):
        self.nc = nc
        self.ctx = ctx
        self.stage_sems = []
        self.soft_sems = {k: ctx.enter_context(nc.semaphore(k)) for n in ("f0", "f2") for k in (
            n + "_d_cleared", n + "_d_sent", *(f"{n}_c_got{t}" for t in range(4)))}
        self.X = self.sb(ctx, "resid", [P, NT, D])
        self.XN = self.XNT = None
        self.ident = self.sb(ctx, "ident", [P, P])
        self.ones = self.sb(ctx, "ones", [P, P])
        self.tg = self.sb(ctx, "tanh_gates", [P, 8])
        self.PS = ctx.enter_context(nc.psum_tensor("PS", [P, 8, 512], F32))

    def sb(self, ctx, name, shape, dt=F32):
        return ctx.enter_context(self.nc.sbuf_tensor(name, shape, dt))

    def sem(self, name):
        held = self.nc.semaphore(name)
        s = held.__enter__()
        self.stage_sems.append((held, s))
        return s

    def end_stage(self):
        with self.nc.Block() as block:
            @block.gpsimd
            def _(pool):
                for _, s in self.stage_sems:
                    pool.sem_clear(s)
        for held, _ in reversed(self.stage_sems):
            held.__exit__(None, None, None)
        self.stage_sems = []


def prologue(c, x, ctx_in, g_xattn, g_ffn):
    loaded, gates_in, built = c.sem("x_loaded"), c.sem("gates_loaded"), c.sem("ident_built")
    with c.nc.Block() as block:
        @block.sync
        def _(sp):
            sp.dma_start(c.tg[:, 0:4], g_xattn.partition_broadcast(P)).then_inc(gates_in, 16)
            sp.dma_start(c.tg[:, 4:8], g_ffn.partition_broadcast(P)).then_inc(gates_in, 16)
            sp.dma_start(c.X[:, :, :], x.rearrange("b (t p) d -> p (b t) d", p=P)).then_inc(loaded, 16)
            sp.wait_ge(loaded, 16)

        @block.gpsimd
        def _(pool):
            pool.memset(c.ident[:, :], 0.0).then_inc(built, 1)
            pool.memset(c.ones[:, :], 1.0).then_inc(built, 1)
            pool.wait_ge(built, 2)
            pool.affine_select(out=c.ident[:, :], in_=c.ident[:, :], compare_op=ALU.not_equal, fill=1.0,
                               base=0, pattern=[[-1, P]], channel_multiplier=1).then_inc(built, 1)

        @block.scalar
        def _(act):
            act.wait_ge(gates_in, 32)
            act.activation(c.tg[:, :], c.tg[:, :], ACT.Tanh)


def transpose_tokens(c, name, src, dst, evac_scale=None):
    turned, out_a, out_d = c.sem(name + "_turned"), c.sem(name + "_out_a"), c.sem(name + "_out_d")
    pairs = NT // 2
    with c.nc.Block() as block:
        @block.tensor
        def _(pe):
            for i in range(pairs):
                bank = c.PS[:, i, :].rearrange("p (k q) -> p k q", k=DK)
                for t in range(2):
                    for k in range(DK):
                        last = pe.transpose(bank[:, k, t * P:(t + 1) * P], src[:, 2 * i + t, k * P:(k + 1) * P],
                                            c.ident[:, :])
                last.then_inc(turned, 1)

        def evacuate(eng, i, copy, sem):
            eng.wait_ge(turned, i + 1)
            copy(dst[:, :, 2 * i * P:2 * (i + 1) * P],
                 c.PS[:, i, :].rearrange("p (k q) -> p k q", k=DK)).then_inc(sem, 1)

        @block.scalar
        def _(act):
            for i in range(0, pairs, 2):
                evacuate(act, i, act.copy, out_a)

        @block.vector
        def _(dve):
            for i in range(1, pairs, 2):
                evacuate(dve, i, dve.tensor_copy, out_d)


def layernorm(c, scope, name, keep_rows=False):
    c.XNT = c.sb(scope, name + "_XNT", [P, DK, T])
    with ExitStack() as own:
        c.XN = c.sb(scope if keep_rows else own, name + "_XN", [P, NT, D])
        normalise(c, name, c.X, c.XN)
        transpose_tokens(c, name + "_t", c.XN, c.XNT)


def normalise(c, name, src, dst, affine=None):
    nc = c.nc
    with ExitStack() as ctx:
        stats = c.sb(ctx, name + "_stats", [P, NT, 6])
        mv = c.sb(ctx, name + "_mv", [P, NT, 2])
        std = c.sb(ctx, name + "_std", [P, NT])
        rstd = c.sb(ctx, name + "_rstd", [P, NT])
        step = Tally(c.sem(name + "_dve"))
        root = c.sem(name + "_root")
        pool_out = c.sem(name + "_pool")
        with nc.Block() as block:
            var_ready = [0]

            @block.vector
            def _(dve):
                for t in range(NT):
                    step.mark(dve.bn_stats(stats[:, t, :], src[:, t, :]))
                for t in range(NT):
                    dve.wait_ge(step.sem, t + 1)
                    step.mark(dve.bn_aggr(mv[:, t, :], stats[:, t, :]))
                dve.wait_ge(step.sem, step.n)
                var_ready[0] = step.mark(dve.tensor_scalar(std[:, :], mv[:, :, 1], EPS, None, ALU.add))
                dve.wait_ge(root, 1)
                dve.wait_ge(step.sem, var_ready[0])
                r = step.mark(dve.reciprocal(rstd[:, :], std[:, :]))
                dve.wait_ge(step.sem, r)
                for t in range(NT):
                    step.mark(dve.tensor_scalar(dst[:, t, :], src[:, t, :], mv[:, t, 0:1], rstd[:, t:t + 1],
                                                ALU.subtract, ALU.mult))
                if affine:
                    w, b = affine
                    for t in range(NT):
                        dve.wait_ge(step.sem, r + t + 1)
                        step.mark(dve.tensor_tensor(dst[:, t, :], dst[:, t, :], w[:, :], ALU.mult))
                    for t in range(NT):
                        dve.wait_ge(step.sem, r + NT + t + 1)
                        step.mark(dve.tensor_tensor(dst[:, t, :], dst[:, t, :], b[:, :], ALU.add))

            @block.scalar
            def _(act):
                act.wait_ge(step.sem, var_ready[0])
                act.activation(std[:, :], std[:, :], ACT.Sqrt).then_inc(root, 1)


def add_scaled(eng, c, gate, tile_ap, delta):
    return eng.scalar_tensor_tensor(out=tile_ap, in0=delta, scalar=c.tg[:, gate:gate + 1], in1=tile_ap,
                                    op0=ALU.mult, op1=ALU.add)


class Attention:

    RING = 4

    def __init__(self, c, ctx, name, nk, wide, masked, q_tiles=QT_B):
        self.c, self.name, self.nk, self.wide, self.masked, self.q_tiles = c, name, nk, wide, masked, q_tiles
        self.kt = nk // P
        self.probs = c.sb(ctx, name + "_probs", [P, self.RING, nk])
        self.probsT = c.sb(ctx, name + "_probsT", [P, 8, self.kt, P])
        self.neg_max = c.sb(ctx, name + "_negmax", [P, 8])
        if wide:
            self.heads = c.sb(ctx, name + "_heads", [P, 2, H // 2, P])
            self.rsum = c.sb(ctx, name + "_rsum", [64, 4, P])
        else:
            self.heads = c.sb(ctx, name + "_heads", [P, 2, 4, P])
            self.rsum = c.sb(ctx, name + "_rsum", [P, 4 * P])
        names = ["scores", "neg_max", "probs", "turned", "copied_a", "copied_d", "heads", "heads_out",
                 "sums", "rsum", "normed", "projected", "added"]
        self.s = {k: c.sem(name + "_" + k) for k in names}

    def clear(self):
        with self.c.nc.Block() as block:
            @block.gpsimd
            def _(pool):
                for s in self.s.values():
                    pool.sem_clear(s)

    def run(self, scores, mask, values, w_out, bias_row, emit, sel=None):
        c, s, kt = self.c, self.s, self.kt
        PS = c.PS
        n_heads = self.q_tiles * H
        units = n_heads // 4

        def PT(n):
            return PS[:, 4 + n % 2, 0:self.nk].rearrange("p (k q) -> p k q", k=kt)

        tail = 16
        with c.nc.Block() as block:
            @block.tensor
            def _(pe):
                def score(n):
                    if n >= 4:
                        pe.wait_ge(s["neg_max"], n - 3)
                        if not self.masked:
                            pe.wait_ge(s["probs"], n - 3)
                    parts = scores(n // H, n % H)
                    for cols, lhsT, rhs in parts:
                        last = pe.matmul(PS[:, n % 4, cols], lhsT, rhs, start=True, stop=True)
                    last.then_inc(s["scores"], 1)

                def turn(n):
                    pe.wait_ge(s["probs"], n + 1)
                    if n >= 2:
                        pe.wait_ge(s["copied_a"] if n % 2 == 0 else s["copied_d"], n // 2)
                    for k in range(kt):
                        last = pe.transpose(PT(n)[:, k, :], self.probs[:, n % self.RING, k * P:(k + 1) * P],
                                            c.ident[:, :])
                    last.then_inc(s["turned"], 1)

                def attend(u):
                    pe.wait_ge(s["copied_a"], 2 * u + 2)
                    pe.wait_ge(s["copied_d"], 2 * u + 2)
                    if u >= 1:
                        pe.wait_ge(s["heads_out"], u)
                    base = 4 * (u % 2)
                    for k in range(kt):
                        if self.wide:
                            last = pe.matmul(PS[:, 6, :].rearrange("p (j q) -> p j q", j=4), values(u // 4, 0, k),
                                             self.probsT[:, base:base + 4, k, :], start=(k == 0), stop=(k == kt - 1))
                        else:
                            for j in range(4):
                                last = pe.matmul(PS[32 * j:32 * j + 32, 6, 0:P], values(u // 4, 4 * (u % 4) + j, k),
                                                 self.probsT[:, base + j, k, :], start=(k == 0), stop=(k == kt - 1))
                    last.then_inc(s["heads"], 1)

                def sums(qt):
                    pe.wait_ge(s["heads_out"], 4 * qt + 4)
                    if qt >= 1:
                        pe.wait_ge(s["added"], qt)
                    pe.matmul(PS[:, 7, :], sel, self.heads[:, qt % 2, :, :].rearrange("p g q -> p (g q)"),
                              start=True, stop=True).then_inc(s["sums"], 1)

                def project(qt):
                    if self.wide:
                        pe.wait_ge(s["heads_out"], 4 * qt + 4)
                        if qt >= 1:
                            pe.wait_ge(s["added"], qt)
                    else:
                        pe.wait_ge(s["normed"], qt + 1)
                    groups = H // 2 if self.wide else 4
                    for g in range(groups):
                        last = pe.matmul(PS[:, 7, 0:D], self.heads[:, qt % 2, g, :], w_out[:, g, :], start=(g == 0),
                                         stop=(g == groups - 1 and bias_row is None))
                    if bias_row is not None:
                        last = pe.matmul(PS[:, 7, 0:D], c.ones[0:1, :], bias_row, start=False, stop=True)
                    last.then_inc(s["projected"], 1)

                for n in range(4):
                    score(n)
                for n in range(n_heads + tail):
                    if n < n_heads:
                        turn(n)
                    if n + 4 < n_heads:
                        score(n + 4)
                    if n % 4 == 1 and 0 <= n // 4 - 1 < units:
                        attend(n // 4 - 1)
                    if n % 16 == 4 and 0 <= n // 16 - 1 < self.q_tiles and not self.wide:
                        sums(n // 16 - 1)
                    if n % 16 == 9 and 0 <= n // 16 - 1 < self.q_tiles:
                        project(n // 16 - 1)

            @block.vector
            def _(dve):
                def row_max(n):
                    dve.wait_ge(s["scores"], n + 1)
                    if n >= 8:
                        dve.wait_ge(s["probs"], n - 7)
                    if self.masked:
                        if n >= self.RING:
                            dve.wait_ge(s["turned"], n - self.RING + 1)
                        dve.tensor_tensor_reduce(self.probs[:, n % self.RING, :], PS[:, n % 4, 0:self.nk],
                                                 mask(n // H), 1.0, -F32_MIN, ALU.add, ALU.min,
                                                 self.neg_max[:, n % 8:n % 8 + 1]).then_inc(s["neg_max"], 1)
                    else:
                        dve.tensor_reduce(self.neg_max[:, n % 8:n % 8 + 1], PS[:, n % 4, 0:self.nk], X_AXIS,
                                          ALU.min).then_inc(s["neg_max"], 1)

                def copy_turned(n):
                    dve.wait_ge(s["turned"], n + 1)
                    if n >= 8:
                        dve.wait_ge(s["heads"], n // 4 - 1)
                    dve.tensor_copy(self.probsT[:, n % 8, :, :], PT(n)).then_inc(s["copied_d"], 1)

                def wide_heads(u):
                    dve.wait_ge(s["heads"], u + 1)
                    if u >= 8 and u % 4 == 0:
                        dve.wait_ge(s["projected"], u // 4 - 1)
                    dve.reciprocal(self.rsum[:, :, :],
                                   PS[64:128, 6, :].rearrange("p (j q) -> p j q", j=4)).then_inc(s["rsum"], 1)
                    dve.wait_ge(s["rsum"], u + 1)
                    O = PS[0:64, 6, :].rearrange("p (j q) -> p j q", j=4)
                    g, half = u % 4, u // 4 % 2
                    dve.tensor_tensor(self.heads[0:64, half, 2 * g:2 * g + 2, :], O[:, 0:4:2, :], self.rsum[:, 0:4:2, :],
                                      ALU.mult).then_inc(s["normed"], 1)
                    dve.tensor_tensor(self.heads[64:128, half, 2 * g:2 * g + 2, :], O[:, 1:4:2, :], self.rsum[:, 1:4:2, :],
                                      ALU.mult).then_inc(s["heads_out"], 1)
                    dve.wait_ge(s["heads_out"], u + 1)
                    dve.wait_ge(s["normed"], u + 1)

                for n in range(n_heads + tail):
                    if n < n_heads:
                        row_max(n)
                    if 0 <= n - 3 < n_heads and (n - 3) % 2 == 1:
                        copy_turned(n - 3)
                    if self.wide and n % 4 == 3 and 0 <= n // 4 - 1 < units:
                        wide_heads(n // 4 - 1)
                    if not self.wide and n % 16 == 6 and 0 <= n // 16 - 1 < self.q_tiles:
                        qt = n // 16 - 1
                        dve.wait_ge(s["sums"], qt + 1)
                        if qt >= 1:
                            dve.wait_ge(s["normed"], qt)
                        dve.reciprocal(self.rsum[:, :], PS[:, 7, :]).then_inc(s["rsum"], 1)
                    if n % 16 == 11 and 0 <= n // 16 - 1 < self.q_tiles:
                        qt = n // 16 - 1
                        dve.wait_ge(s["projected"], qt + 1)
                        emit(dve, qt, PS[:, 7, 0:D]).then_inc(s["added"], 1)

            @block.scalar
            def _(act):
                def exponent(n):
                    act.wait_ge(s["neg_max"], n + 1)
                    if not self.masked and n >= self.RING:
                        act.wait_ge(s["turned"], n - self.RING + 1)
                    src = self.probs[:, n % self.RING, :] if self.masked else PS[:, n % 4, 0:self.nk]
                    act.activation(self.probs[:, n % self.RING, :], src, ACT.Exp, scale=-1.0,
                                   bias=self.neg_max[:, n % 8:n % 8 + 1]).then_inc(s["probs"], 1)

                def copy_turned(n):
                    act.wait_ge(s["turned"], n + 1)
                    if n >= 8:
                        act.wait_ge(s["heads"], n // 4 - 1)
                    act.copy(self.probsT[:, n % 8, :, :], PT(n)).then_inc(s["copied_a"], 1)

                for n in range(n_heads + tail):
                    if n < n_heads:
                        exponent(n)
                    if 0 <= n - 2 < n_heads and (n - 2) % 2 == 0:
                        copy_turned(n - 2)
                    if not self.wide and n % 4 == 3 and 0 <= n // 4 - 1 < units:
                        u = n // 4 - 1
                        act.wait_ge(s["heads"], u + 1)
                        if u >= 8 and u % 4 == 0:
                            act.wait_ge(s["projected"], u // 4 - 1)
                        act.copy(self.heads[:, u // 4 % 2, u % 4, :], PS[:, 6, 0:P]).then_inc(s["heads_out"], 1)

            if not self.wide:
                @block.gpsimd
                def _(pool):
                    for qt in range(self.q_tiles):
                        pool.wait_ge(s["rsum"], qt + 1)
                        h2 = self.heads[:, qt % 2, :, :].rearrange("p g q -> p (g q)")
                        pool.tensor_tensor(h2, h2, self.rsum[:, :], ALU.mult).then_inc(s["normed"], 1)


def project_columns(c, name, jobs):
    made, out_a, out_d = c.sem(name + "_made"), c.sem(name + "_out_a"), c.sem(name + "_out_d")
    with c.nc.Block() as block:
        @block.tensor
        def _(pe):
            for i, (view, steps, _) in enumerate(jobs):
                if i >= 8:
                    pe.wait_ge(out_a if i % 2 == 0 else out_d, i // 2 - 3)
                for n, (lhsT, rhs) in enumerate(steps):
                    last = pe.matmul(view(c.PS[:, i % 8, :]), lhsT, rhs, start=(n == 0), stop=(n == len(steps) - 1))
                last.then_inc(made, 1)

        @block.scalar
        def _(act):
            for i in range(0, len(jobs), 2):
                view, _, dst = jobs[i]
                act.wait_ge(made, i + 1)
                act.copy(dst, view(c.PS[:, i % 8, :])).then_inc(out_a, 1)

        @block.vector
        def _(dve):
            for i in range(1, len(jobs), 2):
                view, _, dst = jobs[i]
                dve.wait_ge(made, i + 1)
                dve.tensor_copy(dst, view(c.PS[:, i % 8, :])).then_inc(out_d, 1)


def columns(parts, n, first=0):
    return lambda bank: bank[first:first + parts, 0:n]


def load_all(c, name, pairs):
    in_sp, in_act = c.sem(name + "_in_sp"), c.sem(name + "_in_act")
    with c.nc.Block() as block:
        for get, sem, mine in ((block.sync, in_sp, pairs[0::2]), (block.scalar, in_act, pairs[1::2])):
            @get
            def _(eng, sem=sem, mine=mine):
                for dst, src in mine:
                    eng.dma_start(dst, src).then_inc(sem, 16)
                if mine:
                    eng.wait_ge(sem, 16 * len(mine))



LAT, QLAT, HD = 64, 96, 64


def layer0_attention(c, ctx_T, seg, w, rope):
    nc = c.nc
    with ExitStack() as ctx:
        sb = lambda n, shape, dt=F32: c.sb(ctx, "a0_" + n, shape, dt)
        QW, QS = sb("QW", [QLAT, H, P]), sb("QS", [QLAT, H, P])
        KW, KS = sb("KW", [LAT, P]), sb("KS", [LAT, P])
        WVO = sb("WVO", [P, H // 2, D])
        V = sb("V", [P, NT, P])
        K = sb("K", [P, T])
        qcT = sb("qcT", [QLAT, T])
        tabs = sb("tabs", [P, 4, S])
        segs = sb("segs", [P, NT], I32)
        with ExitStack() as early:
            tb = lambda n, shape, dt=F32: c.sb(early, "a0_" + n, shape, dt)
            wkc, wqd = tb("wkc", [P, DK, LAT]), tb("wqd", [P, DK, QLAT])
            wqr, wkr = tb("wqr", [QLAT, H, HD]), tb("wkr", [LAT, HD])
            wo = tb("wo", [HD, H, D])
            wquT, wkuT, wvuT = tb("wquT", [HD, H, QLAT]), tb("wkuT", [HD, H, LAT]), tb("wvuT", [HD, H, LAT])
            kcT = tb("kcT", [LAT, T])
            ctxT = tb("ctxT", [P, DK, T])
            load_all(c, "a0", [
                (wkc[:, :, :], w["w_kv_comp"].rearrange("(k p) n -> p k n", p=P)),
                (wqd[:, :, :], w["w_q_down"].rearrange("(k p) n -> p k n", p=P)),
                (wqr[:, :, :], w["w_q_rope"].rearrange("c (h e) -> c h e", h=H)),
                (wkr[:, :], w["w_k_rope"]),
                (wquT[:, :, :], w["w_q_up_T"]), (wkuT[:, :, :], w["w_k_up_T"]), (wvuT[:, :, :], w["w_v_up_T"]),
                (wo[:, :, :], w["w_out"].rearrange("(h e) n -> e h n", h=H)),
                (tabs[:, :, :], rope), (segs[:, :], seg), (ctxT[:, :, :], ctx_T),
            ])
            with nc.Block() as block:
                @block.gpsimd
                def _(pool):
                    half = HD // 2
                    pool.memset(QS[:, :, 0:LAT], 0.0)
                    pool.memset(KS[:, 0:LAT], 0.0)
                    pool.tensor_copy(KW[:, 0:LAT], c.ident[0:LAT, 0:LAT])
                    for dst, src in ((QW[:, :, LAT:P], wqr[:, :, :]), (QS[:, :, LAT:LAT + half], wqr[:, :, half:HD]),
                                     (QS[:, :, LAT + half:P], wqr[:, :, 0:half]), (KW[:, LAT:P], wkr[:, :]),
                                     (KS[:, LAT:LAT + half], wkr[:, half:HD]), (KS[:, LAT + half:P], wkr[:, 0:half])):
                        pool.tensor_copy(dst, src)
                    pool.memset(V[:, :, LAT:P], 1.0)
            absorbed = c.sem("a0_absorbed")
            with nc.Block() as block:
                @block.tensor
                def _(pe):
                    for h in range(H):
                        mm = pe.matmul(c.PS[0:QLAT, h // 8, (h % 8) * LAT:(h % 8 + 1) * LAT], wquT[:, h, :],
                                       wkuT[:, h, :], start=True, stop=True)
                    mm.then_inc(absorbed, 1)
                    for h in range(H):
                        r = 64 * (h % 2)
                        mm = pe.matmul(c.PS[r:r + 64, 2 + h // 4, D * (h // 2 % 2):D * (h // 2 % 2 + 1)],
                                       wvuT[:, h, :], wo[:, h, :], start=True, stop=True)
                    mm.then_inc(absorbed, 1)

                @block.vector
                def _(dve):
                    dve.wait_ge(absorbed, 1)
                    for i in range(2):
                        dve.tensor_copy(QW[:, 8 * i:8 * i + 8, 0:LAT],
                                        c.PS[0:QLAT, i, :].rearrange("p (h n) -> p h n", h=8))

                @block.scalar
                def _(act):
                    act.wait_ge(absorbed, 2)
                    for i in range(4):
                        act.copy(WVO[:, 2 * i:2 * i + 2, :], c.PS[:, 2 + i, :].rearrange("p (h n) -> p h n", h=2))
            chunk = lambda b: slice(b * S, (b + 1) * S)
            layernorm(c, early, "a0_ln")
            project_columns(c, "a0_down", [
                (columns(LAT, S), [(wkc[:, k, :], ctxT[:, k, chunk(b)]) for k in range(DK)], kcT[:, chunk(b)])
                for b in range(B)] + [
                (columns(QLAT, S), [(wqd[:, k, :], c.XNT[:, k, chunk(b)]) for k in range(DK)], qcT[:, chunk(b)])
                for b in range(B)])
            made, rot, vt, vout = c.sem("a0_k_made"), c.sem("a0_k_rot"), c.sem("a0_v_turned"), c.sem("a0_v_out")
            other = tb("k_sin", [P, T])
            with nc.Block() as block:
                @block.tensor
                def _(pe):
                    for b in range(B):
                        pe.matmul(c.PS[:, b, :], KW[:, :], kcT[:, chunk(b)], start=True, stop=True)
                        if b >= 2:
                            pe.wait_ge(rot, 3 * (b - 2) + 3)
                        pe.matmul(c.PS[:, 4 + b % 2, :], KS[:, :], kcT[:, chunk(b)], start=True, stop=True)\
                            .then_inc(made, 1)
                    for t in range(NT):
                        mm = pe.transpose(c.PS[:, 6 + t // 8, (t % 8) * LAT:(t % 8 + 1) * LAT],
                                          kcT[:, t * P:(t + 1) * P], c.ident[0:LAT, 0:LAT])
                    mm.then_inc(vt, 1)

                @block.vector
                def _(dve):
                    for b in range(B):
                        dve.wait_ge(made, b + 1)
                        dve.tensor_tensor(K[:, chunk(b)], c.PS[:, b, :], tabs[:, 2, :], ALU.mult).then_inc(rot, 1)
                        dve.tensor_tensor(other[:, chunk(b)], c.PS[:, 4 + b % 2, :], tabs[:, 3, :], ALU.mult)\
                            .then_inc(rot, 1)
                        dve.wait_ge(rot, 3 * b + 2)
                        dve.tensor_tensor(K[:, chunk(b)], K[:, chunk(b)], other[:, chunk(b)], ALU.add)\
                            .then_inc(rot, 1)

                @block.scalar
                def _(act):
                    act.wait_ge(vt, 1)
                    for i in range(2):
                        act.copy(V[:, 8 * i:8 * i + 8, 0:LAT], c.PS[:, 6 + i, :].rearrange("p (t n) -> p t n", t=8))\
                            .then_inc(vout, 1)
        att = Attention(c, ctx, "a0_att", S, True, True)
        QB = sb("QB", [P, H, S])
        VB = sb("VB", [P, QT_B, P])
        mask = sb("mask", [P, QT_B, S])
        keys = sb("key_index", [P, S])
        segf = sb("segf", [P, 2, NT])
        segB = sb("segB", [P, 2, QT_B])
        sinp = sb("q_sin", [P, 2, S])
        idx = sb("idx", [P, S], I32)
        prep = c.sem("a0_prep")
        with nc.Block() as block:
            @block.gpsimd
            def _(pool):
                pool.iota(idx[:, :], pattern=[[1, S]], base=0, channel_multiplier=0).then_inc(prep, 1)

            @block.vector
            def _(dve):
                dve.wait_ge(prep, 1)
                dve.tensor_copy(keys[:, :], idx[:, :])
                dve.tensor_copy(segf[:, 0, :], segs[:, :]).then_inc(prep, 1)
                dve.wait_ge(prep, 2)
                dve.tensor_scalar(segf[:, 1, :], segf[:, 0, :], -2.0, None, ALU.add)
        q = {k: c.sem("a0_q_" + k) for k in ("made", "cos", "sin", "sum", "mask", "copied")}
        with nc.Fori(0, B) as b:
            with nc.Block() as block:
                @block.tensor
                def _(pe):
                    for h in range(H):
                        if h >= 4:
                            pe.wait_ge(q["cos"], h - 3)
                            pe.wait_ge(q["sin"], h - 3)
                        for bank, W in ((h % 4, QW), (4 + h % 4, QS)):
                            mm = pe.matmul(c.PS[:, bank, :], W[:, h, :], qcT[:, bass.ds(b * S, S)], start=True,
                                           stop=True)
                        mm.then_inc(q["made"], 1)

                @block.vector
                def _(dve):
                    for h in range(H):
                        dve.wait_ge(q["made"], h + 1)
                        dve.tensor_tensor(QB[:, h, :], c.PS[:, h % 4, :], tabs[:, 0, :], ALU.mult)\
                            .then_inc(q["cos"], 1)
                        if h >= 2:
                            dve.wait_ge(q["sum"], h - 1)
                        dve.tensor_tensor(sinp[:, h % 2, :], c.PS[:, 4 + h % 4, :], tabs[:, 1, :], ALU.mult)\
                            .then_inc(q["sin"], 1)
                    dve.wait_ge(q["copied"], 2)
                    for t in range(QT_B):
                        m = mask[:, t, :]
                        dve.tensor_scalar(m, keys[:, :], segB[:, 1, t:t + 1], None, ALU.is_ge)\
                            .then_inc(q["mask"], 1)
                        dve.wait_ge(q["mask"], 3 * t + 1)
                        dve.scalar_tensor_tensor(out=m, in0=keys[:, :], scalar=segB[:, 0, t:t + 1], in1=m,
                                                 op0=ALU.is_le, op1=ALU.mult).then_inc(q["mask"], 1)
                        dve.wait_ge(q["mask"], 3 * t + 2)
                        dve.tensor_scalar(m, m, -1.0, F32_MIN, ALU.add, ALU.mult).then_inc(q["mask"], 1)

                @block.gpsimd
                def _(pool):
                    pool.tensor_copy(segB[:, :, :], segf[:, :, bass.ds(b * QT_B, QT_B)]).then_inc(q["copied"], 1)
                    pool.tensor_copy(VB[:, :, :], V[:, bass.ds(b * QT_B, QT_B), :]).then_inc(q["copied"], 1)
                    for h in range(H):
                        pool.wait_ge(q["cos"], h + 1)
                        pool.wait_ge(q["sin"], h + 1)
                        pool.tensor_tensor(QB[:, h, :], QB[:, h, :], sinp[:, h % 2, :], ALU.add)\
                            .then_inc(q["sum"], 1)

            with nc.Block() as block:
                @block.gpsimd
                def _(pool):
                    for sm in q.values():
                        pool.sem_clear(sm)
            whole = slice(0, S)
            att.run(lambda qt, h: [(whole, QB[:, h, qt * P:(qt + 1) * P], K[:, bass.ds(b * S, S)])],
                    lambda qt: mask[:, qt, :], lambda qt, h, k: VB[:, k, :], WVO, None,
                    lambda dve, qt, delta: add_scaled(dve, c, 0, c.X[:, bass.ds(b * QT_B + qt, 1), :]
                                                      .rearrange("p a d -> p (a d)"), delta))
            att.clear()



Q_PARTS = (0, 0, 1, 1, 0, 2)
K_PARTS = (0, 1, 0, 1, 2, 0)
DH = D // H
PACKED = 6 * DH
SLOT = 32


def split_and_pack(c, name, jobs, pack, parts_of, scratch, chunk_w, rows=P, scale=1.0, lead=None, ring=3):
    nc = c.nc
    nk = len(jobs[0])
    flat = [(n, k) for n in range(len(jobs)) for k in range(nk)]
    with ExitStack() as ctx:
        whole = c.sb(ctx, name + "_whole", [rows, 2, chunk_w])
        rest = c.sb(ctx, name + "_rest", [rows, 2, chunk_w])
        parts = c.sb(ctx, name + "_parts", [rows, ring, 3, chunk_w], BF16)
        s = {k: c.sem(name + "_" + k) for k in ("made", "whole", "high", "rest", "middle", "low", "packed")}
        saved = [c.sem(f"{name}_saved{i}") for i in range(ring)]
        with nc.Block() as block:
            @block.tensor
            def _(pe):
                for i, (n, k) in enumerate(flat):
                    steps = jobs[n][k][0]
                    if steps is None:
                        continue
                    if i >= 8:
                        pe.wait_ge(s["whole"], i - 7)
                    for m, (lhsT, rhs) in enumerate(steps):
                        last = pe.matmul(c.PS[0:rows, i % 8, 0:chunk_w], lhsT, rhs, start=(m == 0),
                                         stop=(m == len(steps) - 1))
                    last.then_inc(s["made"], 1)

            @block.scalar
            def _(act):
                for i, (n, k) in enumerate(flat):
                    steps, bias, src = jobs[n][k]
                    if steps is not None:
                        act.wait_ge(s["made"], i + 1)
                        src = c.PS[0:rows, i % 8, 0:chunk_w]
                    if i >= 2:
                        act.wait_ge(s["rest"], i - 1)
                    if bias is None:
                        act.activation(whole[:, i % 2, :], src, ACT.Copy, scale=scale).then_inc(s["whole"], 1)
                    else:
                        act.activation(whole[:, i % 2, :], src, ACT.Identity, bias=bias, scale=scale)\
                           .then_inc(s["whole"], 1)
                    act.wait_ge(s["whole"], i + 1)
                    if i >= ring:
                        act.wait_ge(saved[i % ring], 16 * (i // ring))
                    act.copy(parts[:, i % ring, 0, :], whole[:, i % 2, :]).then_inc(s["high"], 1)

            @block.vector
            def _(dve):
                for i in range(len(flat)):
                    p = parts[:, i % ring, :, :]
                    dve.wait_ge(s["high"], i + 1)
                    if i >= 2:
                        dve.wait_ge(s["low"], i - 1)
                    dve.tensor_tensor(rest[:, i % 2, :], whole[:, i % 2, :], p[:, 0, :], ALU.subtract)\
                        .then_inc(s["rest"], 1)
                    dve.wait_ge(s["rest"], i + 1)
                    dve.tensor_copy(p[:, 1, :], rest[:, i % 2, :]).then_inc(s["middle"], 1)
                    dve.wait_ge(s["middle"], i + 1)
                    dve.tensor_tensor(p[:, 2, :], rest[:, i % 2, :], p[:, 1, :], ALU.subtract).then_inc(s["low"], 1)

            @block.sync
            def _(sp):
                loads = 0
                for i, (n, k) in enumerate(flat):
                    cols = slice(n * chunk_w, (n + 1) * chunk_w)
                    sp.wait_ge(s["low"], i + 1)
                    sp.dma_start(scratch[:, k * P:k * P + rows, cols].rearrange("a r t -> r a t"),
                                 parts[:, i % ring, :, :]).then_inc(saved[i % ring], 16)
                    if k == nk - 1:
                        for m in range(i - nk + 1, i + 1):
                            sp.wait_ge(saved[m % ring], 16 * (m // ring + 1))
                        if lead is None:
                            for a, part in enumerate(parts_of):
                                sp.dma_start(pack[DH * a:DH * (a + 1), :, cols],
                                             scratch[part, 0:D, cols].rearrange("(h d) t -> d h t", d=DH))\
                                  .then_inc(s["packed"], 16)
                                loads += 1
                        else:
                            sp.dma_start(pack[lead:lead + 3, :, cols], scratch[:, 0:H, cols]).then_inc(s["packed"], 16)
                            loads += 1
                sp.wait_ge(s["packed"], 16 * loads)




def layer1_attention(c, ctx_T, ctx_rows, w):
    nc = c.nc
    kt = S // P
    with ExitStack() as ctx:
        sb = lambda n, shape, dt=F32: c.sb(ctx, "a1_" + n, shape, dt)
        layernorm(c, ctx, "a1_ln", keep_rows=True)
        R, rows = sb("R", [P, DK, T]), sb("rows", [P, NT, D])
        W, W14 = sb("W", [P, 4, DK, D]), sb("W14", [P, B, DK, D])
        vecs = sb("vecs", [P, 3, DK])
        biases, bl, row_term = sb("biases", [1, 3]), sb("bl", [1, D]), sb("row_term", [1, T])
        bias = sb("bias", [1, 1])
        attT, prod = sb("attT", [P, DK, T]), sb("prod", [P, DK, T])
        probs, probsT = sb("probs", [P, 2, S]), sb("probsT", [P, 2, kt, S])
        nmax, sums, rsum = sb("nmax", [P, NT]), sb("sums", [P, NT]), sb("rsum", [P, NT])
        with ExitStack() as early:
            ctxT = c.sb(early, "a1_ctxT", [P, DK, T])
            one = lambda v: v.rearrange("(a n) -> a n", a=1)
            load_all(c, "a1", [(ctxT[:, :, :], ctx_T), (rows[:, :, :], ctx_rows), (W[:, :, :, :], w["W_l_T"]),
                               (vecs[:, :, :], w["vecs"]), (bl[:, :], one(w["b_l"])),
                               (biases[:, 0:1], one(w["b_cq"])), (biases[:, 1:2], one(w["b_c"])),
                               (biases[:, 2:3], one(w["b_q"]))])
            termed, bsum = c.sem("a1_termed"), c.sem("a1_bsum")
            with nc.Block() as block:
                @block.tensor
                def _(pe):
                    for b in range(B):
                        for k in range(DK):
                            mm = pe.matmul(c.PS[0:1, b, :], vecs[:, 2, k:k + 1], ctxT[:, k, b * S:(b + 1) * S],
                                           start=(k == 0), stop=(k == DK - 1))
                        mm.then_inc(termed, 1)

                @block.vector
                def _(dve):
                    dve.reduce_sum(bias[:, :], biases[:, :], X_AXIS).then_inc(bsum, 1)
                    for k in range(DK):
                        dve.tensor_scalar(R[:, k, :], ctxT[:, k, :], vecs[:, 0, k:k + 1], vecs[:, 1, k:k + 1],
                                          ALU.mult, ALU.add)
                    dve.wait_ge(bsum, 1)
                    for b in range(B):
                        dve.wait_ge(termed, b + 1)
                        dve.tensor_scalar(row_term[:, b * S:(b + 1) * S], c.PS[0:1, b, :], bias[:, 0:1], None,
                                          ALU.add)
        s = {k: c.sem("a1_" + k) for k in ("scores", "max", "probs", "rsum", "scaled", "turned", "copied", "att",
                                           "att_out")}
        with nc.Block() as block:
            @block.tensor
            def _(pe):
                def score(t):
                    if t >= 2:
                        pe.wait_ge(s["probs"], t - 1)
                    b = t // kt
                    for k in range(DK):
                        pe.matmul(c.PS[:, t % 2, :], c.XNT[:, k, t * P:(t + 1) * P], R[:, k, b * S:(b + 1) * S],
                                  start=(k == 0), stop=False)
                    pe.matmul(c.PS[:, t % 2, :], c.ones[0:1, :], row_term[:, b * S:(b + 1) * S], start=False,
                              stop=True).then_inc(s["scores"], 1)

                def turn(t):
                    pe.wait_ge(s["scaled"], t + 1)
                    if t >= 2:
                        pe.wait_ge(s["copied"], t - 1)
                    for k in range(kt):
                        mm = pe.transpose(c.PS[:, 2 + t % 2, k * P:(k + 1) * P], probs[:, t % 2, k * P:(k + 1) * P],
                                          c.ident[:, :])
                    mm.then_inc(s["turned"], 1)

                def attend(b):
                    pe.wait_ge(s["copied"], kt * (b + 1))
                    if b >= 2:
                        pe.wait_ge(s["att_out"], b - 1)
                    for half in range(DK):
                        for k in range(kt):
                            mm = pe.matmul(c.PS[:, 4 + 2 * (b % 2) + half, :],
                                           rows[:, b * kt + k, half * P:(half + 1) * P], probsT[:, b % 2, k, :],
                                           start=(k == 0), stop=(k == kt - 1))
                    mm.then_inc(s["att"], 1)
                score(0)
                score(1)
                for t in range(NT):
                    turn(t)
                    if t + 2 < NT:
                        score(t + 2)
                    if t % kt == 1 and t >= kt:
                        attend(t // kt - 1)
                attend(B - 1)

            @block.vector
            def _(dve):
                for t in range(NT + 2):
                    if t < NT:
                        dve.wait_ge(s["scores"], t + 1)
                        dve.tensor_reduce(nmax[:, t:t + 1], c.PS[:, t % 2, :], X_AXIS, ALU.max, negate=True)\
                            .then_inc(s["max"], 1)
                    if t >= 1 and t - 1 < NT:
                        n = t - 1
                        dve.wait_ge(s["probs"], n + 1)
                        dve.reciprocal(rsum[:, n:n + 1], sums[:, n:n + 1]).then_inc(s["rsum"], 1)
                        dve.wait_ge(s["rsum"], n + 1)
                        dve.tensor_scalar(probs[:, n % 2, :], probs[:, n % 2, :], rsum[:, n:n + 1], None, ALU.mult)\
                            .then_inc(s["scaled"], 1)

            @block.gpsimd
            def _(pool):
                for b in range(B):
                    pool.wait_ge(s["att_out"], b + 1)
                    for k in range(DK):
                        cols = slice(b * S, (b + 1) * S)
                        pool.tensor_tensor(prod[:, k, cols], attT[:, k, cols], c.XNT[:, k, cols], ALU.mult)

            @block.scalar
            def _(act):
                def out(b):
                    act.wait_ge(s["att"], b + 1)
                    act.copy(attT[:, :, b * S:(b + 1) * S], c.PS[:, 4 + 2 * (b % 2):6 + 2 * (b % 2), :])\
                       .then_inc(s["att_out"], 1)
                for t in range(NT + 2):
                    if t < NT:
                        act.wait_ge(s["max"], t + 1)
                        if t >= 2:
                            act.wait_ge(s["turned"], t - 1)
                        act.activation(probs[:, t % 2, :], c.PS[:, t % 2, :], ACT.Exp, bias=nmax[:, t:t + 1],
                                       accum_out=sums[:, t:t + 1]).then_inc(s["probs"], 1)
                    if 1 <= t and t - 1 < NT:
                        n = t - 1
                        b, l = n // kt, n % kt
                        act.wait_ge(s["turned"], n + 1)
                        if b >= 2:
                            act.wait_ge(s["att"], b - 1)
                        act.copy(probsT[:, b % 2, :, l * P:(l + 1) * P],
                                 c.PS[:, 2 + n % 2, :].rearrange("p (k q) -> p k q", k=kt)).then_inc(s["copied"], 1)
                    if t >= kt + 3 and (t - 3) % kt == 0:
                        out((t - 3) // kt - 1)
                out(B - 1)
        bmin, bmin_all = sb("bmin", [P, B]), sb("bmin_all", [P, B])
        e, tot, mean = sb("e", [P, NT]), sb("tot", [P, B]), sb("mean", [P, B, DK])
        v, allr, exped, meant = Tally(c.sem("a1_m_dve")), c.sem("a1_allr"), c.sem("a1_exped"), c.sem("a1_meant")
        neg = sb("neg", [P, B])
        with nc.Block() as block:
            @block.vector
            def _(dve):
                def then(ins):
                    dve.wait_ge(v.sem, v.mark(ins))
                then(dve.tensor_reduce(bmin[:, :], nmax[:, :].rearrange("p (b t) -> p b t", b=B), X_AXIS, ALU.min))
                then(dve.tensor_scalar(neg[:, :], bmin[:, :], -1.0, None, ALU.mult))
                dve.wait_ge(meant, 1)
                then(dve.tensor_reduce(tot[:, :], c.PS[:, 0, 0:NT].rearrange("p (b t) -> p b t", b=B), X_AXIS,
                                       ALU.add))
                then(dve.reciprocal(tot[:, :], tot[:, :]))
                for b in range(B):
                    then(dve.tensor_scalar(mean[:, b, :], c.PS[:, 1, 2 * b:2 * b + 2], tot[:, b:b + 1], None,
                                           ALU.mult))
                    for k in range(DK):
                        then(dve.scalar_tensor_tensor(out=W14[:, b, k, :], in0=W[:, 3, k, :],
                                                      scalar=mean[:, b, k:k + 1], in1=W[:, 0, k, :],
                                                      op0=ALU.mult, op1=ALU.add))

            @block.gpsimd
            def _(pool):
                pool.wait_ge(v.sem, 2)
                pool.partition_all_reduce(bmin_all[:, :], neg[:, :], P, bass.bass_isa.ReduceOp.max).then_inc(allr, 1)
                pool.wait_ge(allr, 1)
                pool.tensor_scalar(neg[:, :], bmin_all[:, :], -1.0, None, ALU.mult).then_inc(allr, 1)

            @block.scalar
            def _(act):
                act.wait_ge(allr, 2)
                for b in range(B):
                    act.activation(e[:, b * kt:(b + 1) * kt], nmax[:, b * kt:(b + 1) * kt], ACT.Exp, scale=-1.0,
                                   bias=neg[:, b:b + 1]).then_inc(exped, 1)

            @block.tensor
            def _(pe):
                pe.wait_ge(exped, B)
                pe.matmul(c.PS[:, 0, 0:NT], c.ones[:, :], e[:, :], start=True, stop=True)
                for b in range(B):
                    for half in range(DK):
                        for k in range(kt):
                            t = b * kt + k
                            mm = pe.matmul(c.PS[:, 1, 2 * b + half:2 * b + half + 1],
                                           c.XN[:, t, half * P:(half + 1) * P], e[:, t:t + 1], start=(k == 0),
                                           stop=(k == kt - 1))
                mm.then_inc(meant, 1)
        out, added = c.sem("a1_out"), c.sem("a1_added")
        with nc.Block() as block:
            @block.tensor
            def _(pe):
                for t in range(NT):
                    if t >= 8:
                        pe.wait_ge(added, t - 7)
                    z, cols = c.PS[:, t % 8, 0:D], slice(t * P, (t + 1) * P)
                    for k in range(DK):
                        pe.matmul(z, c.XNT[:, k, cols], W14[:, t // kt, k, :], start=(k == 0), stop=False)
                        pe.matmul(z, attT[:, k, cols], W[:, 1, k, :], start=False, stop=False)
                        pe.matmul(z, prod[:, k, cols], W[:, 2, k, :], start=False, stop=False)
                    pe.matmul(z, c.ones[0:1, :], bl[:, :], start=False, stop=True).then_inc(out, 1)

            @block.vector
            def _(dve):
                for t in range(NT):
                    dve.wait_ge(out, t + 1)
                    add_scaled(dve, c, 1, c.X[:, t, :], c.PS[:, t % 8, 0:D]).then_inc(added, 1)



KEEP = S // 2
NK_T = B * KEEP // P


def rows_of_columns(c, name, scope, cols, out):
    wide = c.sb(scope, name + "_wide", [P, NT, P])
    spread, turned, copied = c.sem(name + "_spread"), c.sem(name + "_turned"), c.sem(name + "_copied")
    with c.nc.Block() as block:
        @block.vector
        def _(dve):
            for t in range(NT):
                dve.tensor_scalar(wide[:, t, :], c.ones[:, :], cols[:, t:t + 1], None, ALU.mult).then_inc(spread, 1)

        @block.tensor
        def _(pe):
            for t in range(NT):
                pe.wait_ge(spread, t + 1)
                mm = pe.transpose(c.PS[:, t // 4, (t % 4) * P:(t % 4 + 1) * P], wide[:, t, :], c.ident[:, :])
                if t % 4 == 3:
                    mm.then_inc(turned, 1)

        @block.scalar
        def _(act):
            for i in range(NT // 4):
                act.wait_ge(turned, i + 1)
                act.copy(out[:, 4 * i * P:4 * (i + 1) * P], c.PS[:, i, :]).then_inc(copied, 1)


def token_logits(c, name, weights, n, out):
    made = c.sem(name + "_made")
    with c.nc.Block() as block:
        @block.tensor
        def _(pe):
            for t in range(NT):
                for k in range(DK):
                    mm = pe.matmul(c.PS[:, 0, t * n:(t + 1) * n], c.XNT[:, k, t * P:(t + 1) * P], weights[:, k, :],
                                   start=(k == 0), stop=(k == DK - 1))
            mm.then_inc(made, 1)

        @block.vector
        def _(dve):
            dve.wait_ge(made, 1)
            dve.tensor_copy(out, c.PS[:, 0, 0:NT * n].rearrange("p (t n) -> p t n", t=NT))


def rank_within(c, name, scope, key_cols, key_rows, rank, spans, earlier):
    span = max(b - a for a, b in spans) * P
    part = c.sb(scope, name + "_part", [P, NT, 4])
    junk = c.sb(scope, name + "_junk", [P, 4, span], BF16)
    zeroed, step = c.sem(name + "_zeroed"), Tally(c.sem(name + "_step"))
    with c.nc.Block() as block:
        @block.vector
        def _(dve):
            def spare(w):
                if step.n >= 4:
                    dve.wait_ge(step.sem, step.n - 3)
                return junk[:, step.n % 4, 0:w]
            dve.memset(part[:, :, :], 0.0).then_inc(zeroed, 1)
            dve.wait_ge(zeroed, 1)
            for t in range(NT):
                a, b = spans[t]
                key = key_cols[:, t:t + 1]
                for i, (lo, hi, op) in enumerate(((a, t, ALU.is_ge), (t, b, ALU.is_gt))):
                    if lo < hi:
                        step.mark(dve.tensor_scalar(spare((hi - lo) * P), key_rows[:, lo * P:hi * P], key, None, op,
                                                    ALU.add, accum_out=part[:, t, i:i + 1]))
                step.mark(dve.scalar_tensor_tensor(out=spare(P), in0=key_rows[:, t * P:(t + 1) * P], scalar=key,
                                                   in1=earlier[:, :], op0=ALU.is_equal, op1=ALU.mult,
                                                   accum_out=part[:, t, 2:3]))
            dve.wait_ge(step.sem, step.n)
            dve.tensor_reduce(rank, part[:, :, :], X_AXIS, ALU.add)


def layer1_ffn(c, w, consts, scratch):
    nc = c.nc
    TK = B * KEEP
    tile = lambda t: slice(t * P, (t + 1) * P)
    with ExitStack() as ctx:
        sb = lambda n, shape, dt=F32: c.sb(ctx, "f1_" + n, shape, dt)
        WOUT, sel, gate = sb("WOUT", [P, 4, D]), sb("sel", [P, P]), sb("gate", [P, NT])
        pickT = sb("pickT", [P, 2, T])
        QP, KP = sb("QP", [PACKED, H, TK], BF16), sb("KP", [PACKED, H, TK], BF16)
        V, Y = sb("V", [P, NK_T, D]), sb("Y", [P, NK_T, D])
        W = {n: sb("W" + n, [P, DK, D]) for n in "qkv"}
        kept = sb("kept", [P, DK, TK])
        with ExitStack() as early:
            tb = lambda n, shape, dt=F32: c.sb(early, "f1_" + n, shape, dt)
            Wg, earlier = tb("Wg", [P, DK, 1]), tb("earlier", [P, P])
            slots_i, slots = tb("slots_i", [P, KEEP], I32), tb("slots", [P, KEEP])
            rank, gate_rows, pick = tb("rank", [P, NT]), tb("gate_rows", [P, T]), tb("pick", [P, NT, KEEP])
            layernorm(c, early, "f1_ln", keep_rows=True)
            load_all(c, "f1", [(Wg[:, :, :], w["Wg_cols"]),
                               (WOUT[:, :, :], w["Wo_slots"]), (sel[:, :], consts["sum_rows"]),
                               (earlier[:, :], consts["earlier"])]
                     + [(W[n][:, :, :], w["W" + n].rearrange("(k p) n -> p k n", p=P)) for n in "qkv"])
            token_logits(c, "f1_gate", Wg, 1, gate[:, :].rearrange("p (t n) -> p t n", n=1))
            with nc.Block() as block:
                @block.scalar
                def _(act):
                    act.activation(gate[:, :], gate[:, :], ACT.Sigmoid)

                @block.gpsimd
                def _(pool):
                    pool.iota(slots_i[:, :], pattern=[[1, KEEP]], base=0, channel_multiplier=0)
            with ExitStack() as tmp:
                rows_of_columns(c, "f1_rows", tmp, gate, gate_rows)
                rank_within(c, "f1_rank", tmp, gate, gate_rows, rank[:, :],
                            [(t // QT_B * QT_B, t // QT_B * QT_B + QT_B) for t in range(NT)], earlier)
            ready, picked, turned, out_a, kept_made, kept_out = (c.sem("f1_" + k) for k in (
                "slots_ready", "picked", "pick_turned", "pick_out", "kept_made", "kept_out"))
            with nc.Block() as block:
                @block.vector
                def _(dve):
                    dve.tensor_copy(slots[:, :], slots_i[:, :]).then_inc(ready, 1)
                    dve.wait_ge(ready, 1)
                    for t in range(NT):
                        dve.tensor_scalar(pick[:, t, :], slots[:, :], rank[:, t:t + 1], None, ALU.is_equal)\
                            .then_inc(picked, 1)
                    for b in range(B):
                        dve.wait_ge(kept_made, b + 1)
                        dve.tensor_copy(kept[:, :, b * KEEP:(b + 1) * KEEP],
                                        c.PS[:, b, :].rearrange("p (k n) -> p k n", k=DK)).then_inc(kept_out, 1)

                @block.tensor
                def _(pe):
                    for b in range(B):
                        pe.wait_ge(picked, QT_B * (b + 1))
                        for half in range(DK):
                            for l in range(QT_B):
                                t = b * QT_B + l
                                mm = pe.matmul(c.PS[:, b, half * KEEP:(half + 1) * KEEP],
                                               c.XN[:, t, half * P:(half + 1) * P], pick[:, t, :], start=(l == 0),
                                               stop=(l == QT_B - 1))
                        mm.then_inc(kept_made, 1)
                    for i in range(NT // 2):
                        if i >= 4:
                            pe.wait_ge(out_a, i - 3)
                        for l in range(2):
                            for hf in range(2):
                                mm = pe.transpose(c.PS[:, 4 + i % 4, hf * D + l * P:hf * D + (l + 1) * P],
                                                  pick[:, 2 * i + l, hf * P:(hf + 1) * P], c.ident[:, :])
                        mm.then_inc(turned, 1)

                @block.scalar
                def _(act):
                    for i in range(NT // 2):
                        act.wait_ge(turned, i + 1)
                        act.copy(pickT[:, :, 2 * i * P:2 * (i + 1) * P],
                                 c.PS[:, 4 + i % 4, :].rearrange("p (s n) -> p s n", s=2)).then_inc(out_a, 1)
        half_chunk = lambda n: slice(n * S, (n + 1) * S)
        for n, pack, parts, scale in (("q", QP, Q_PARTS, -0.25), ("k", KP, K_PARTS, 1.0)):
            split_and_pack(c, f"f1_{n}s", [[([(W[n][:, i, tile(k)], kept[:, i, half_chunk(m)]) for i in range(DK)],
                                             None, None) for k in range(DK)] for m in range(TK // S)],
                           pack, parts, scratch, S, scale=scale)
        project_columns(c, "f1_v", [
            (columns(P, D), [(kept[:, i, tile(t)], W["v"][:, i, :]) for i in range(DK)], V[:, t, :])
            for t in range(NK_T)])
        att = Attention(c, ctx, "f1_att", KEEP, False, False, q_tiles=KEEP // P)
        VB = sb("VB", [P, KEEP // P, H, SLOT])
        vset = c.sem("f1_vset")
        with nc.Block() as block:
            @block.gpsimd
            def _(pool):
                pool.memset(VB[:, :, :, :], 0.0).then_inc(vset, 1)
                pool.wait_ge(vset, 1)
                pool.memset(VB[:, :, :, DH:DH + 1], 1.0)
        per = KEEP // P
        with nc.Fori(0, B) as b:
            with nc.Block() as block:
                @block.gpsimd
                def _(pool):
                    pool.tensor_copy(VB[:, :, :, 0:DH],
                                     V[:, bass.ds(b * per, per), :].rearrange("p t (h d) -> p t h d", h=H))
            att.run(lambda qt, h: [(slice(0, KEEP), QP[:, h, bass.ds(b * KEEP + qt * P, P)],
                                    KP[:, h, bass.ds(b * KEEP, KEEP)])],
                    None, lambda qt, h, k: VB[:, k, h, :], WOUT, None,
                    lambda dve, qt, delta: dve.tensor_copy(Y[:, bass.ds(b * per + qt, 1), :]
                                                           .rearrange("p a d -> p (a d)"), delta), sel=sel[:, :])
            att.clear()
        placed, added, gated = c.sem("f1_placed"), c.sem("f1_added"), c.sem("f1_gated")
        with nc.Block() as block:
            @block.vector
            def _(dve):
                dve.tensor_scalar(gate[:, :], gate[:, :], c.tg[:, 5:6], None, ALU.mult).then_inc(gated, 1)
                dve.wait_ge(gated, 1)
                for t in range(NT):
                    dve.wait_ge(placed, t + 1)
                    dve.scalar_tensor_tensor(out=c.X[:, t, :], in0=c.PS[:, t % 8, 0:D], scalar=gate[:, t:t + 1],
                                             in1=c.X[:, t, :], op0=ALU.mult, op1=ALU.add).then_inc(added, 1)

            @block.tensor
            def _(pe):
                for t in range(NT):
                    if t >= 8:
                        pe.wait_ge(added, t - 7)
                    for hf in range(2):
                        mm = pe.matmul(c.PS[:, t % 8, 0:D], pickT[:, hf, tile(t)], Y[:, t // QT_B * per + hf, :],
                                       start=(hf == 0), stop=(hf == 1))
                    mm.then_inc(placed, 1)



HID = 64
NEG = 1e18


def layer2_attention(c, ctx_T, ctx_rows, key_mask, w, consts, scratch):
    nc = c.nc
    chunk = lambda b: slice(b * S, (b + 1) * S)
    with ExitStack() as ctx:
        sb = lambda n, shape, dt=F32: c.sb(ctx, "a2_" + n, shape, dt)
        rows = PACKED + 3
        WOUT, brow, sel = sb("WOUT", [P, 4, D]), sb("brow", [1, D]), sb("sel", [P, P])
        G, CW = sb("G", [P, DK, P]), sb("CW", [P, DK, H])
        g, cc = sb("g", [P, 2, DK]), sb("cc", [H, 1])
        with ExitStack() as early:
            tb = lambda n, shape, dt=F32: c.sb(early, "a2_" + n, shape, dt)
            WqT, WkT = tb("WqT", [HID, D]), tb("WkT", [HID, D])
            Wq, Wk = tb("Wq", [P, DK, HID]), tb("Wk", [P, DK, HID])
            bqr, bkr = tb("bqr", [P, DK, HID]), tb("bkr", [P, DK, HID])
            bq, bk = tb("bq", [H, HID]), tb("bk", [H, HID])
            Z, Wo, bvT, bo = tb("Z", [HID, H, P]), tb("Wo", [HID, H, D]), tb("bvT", [HID, H]), tb("bo", [1, D])
            blocks, heads = tb("blocks", [P, P]), tb("heads", [P, DK, H])
            junk = tb("junk", [P, HID])
            load_all(c, "a2", [
                (WqT[:, :], w["WqT"]), (WkT[:, :], w["WkT"]), (Wq[:, :, :], w["Wq_rows"]), (Wk[:, :, :], w["Wk_rows"]),
                (bqr[:, :, :], w["bq_rows"]), (bkr[:, :, :], w["bk_rows"]), (bq[:, :], w["bq"]), (bk[:, :], w["bk"]),
                (Z[:, :, :], w["Wv_slots"]), (Wo[:, :, :], w["Wo"].rearrange("(h e) n -> e h n", h=H)),
                (bvT[:, :], w["bvT"]), (bo[:, :], w["bo"].rearrange("(a n) -> a n", a=1)),
                (blocks[:, :], consts["blocks"]), (heads[:, :, :], consts["heads"]), (sel[:, :], consts["sum_rows"]),
            ])
            made, v = c.sem("a2_w_made"), Tally(c.sem("a2_w_dve"))
            with nc.Block() as block:
                @block.tensor
                def _(pe):
                    for k in range(DK):
                        mm = pe.matmul(c.PS[:, 0, k * P:(k + 1) * P], WqT[:, k * P:(k + 1) * P],
                                       WkT[:, k * P:(k + 1) * P], start=True, stop=True)
                    mm.then_inc(made, 1)
                    for q in range(4):
                        for j in range(4):
                            mm = pe.matmul(c.PS[:, 1 + q // 2, (q % 2) * D:(q % 2 + 1) * D], Z[:, 4 * q + j, :],
                                           Wo[:, 4 * q + j, :], start=(j == 0), stop=(j == 3))
                    mm.then_inc(made, 1)
                    for h in range(H):
                        mm = pe.matmul(c.PS[0:1, 3, 0:D], bvT[:, h:h + 1], Wo[:, h, :], start=(h == 0),
                                       stop=(h == H - 1))
                    mm.then_inc(made, 1)

                @block.vector
                def _(dve):
                    def dots(out, a, b_):
                        n = v.mark(dve.tensor_tensor_reduce(junk[0:a.shape[0], :], a, b_, 1.0, 0.0, ALU.mult, ALU.add,
                                                            out))
                        dve.wait_ge(v.sem, n)
                    for k in range(DK):
                        dots(g[:, 0, k:k + 1], Wk[:, k, :], bqr[:, k, :])
                        dots(g[:, 1, k:k + 1], Wq[:, k, :], bkr[:, k, :])
                    dots(cc[:, :], bq[:, :], bk[:, :])
                    v.mark(dve.tensor_scalar(g[:, 0, :], g[:, 0, :], -1.0, None, ALU.mult))
                    v.mark(dve.tensor_scalar(cc[:, :], cc[:, :], -1.0, None, ALU.mult))
                    for k in range(DK):
                        v.mark(dve.tensor_scalar(CW[:, k, :], heads[:, k, :], g[:, 1, k:k + 1], None, ALU.mult))
                    dve.wait_ge(made, 3)
                    for k in range(DK):
                        v.mark(dve.tensor_tensor(G[:, k, :], c.PS[:, 0, k * P:(k + 1) * P], blocks[:, :], ALU.mult))
                    for i in range(2):
                        v.mark(dve.tensor_copy(WOUT[:, 2 * i:2 * i + 2, :],
                                               c.PS[:, 1 + i, :].rearrange("p (g n) -> p g n", g=2)))
                    v.mark(dve.tensor_tensor(brow[:, :], c.PS[0:1, 3, 0:D], bo[:, :], ALU.add))

        QP, KP = sb("QP", [rows, H, T], BF16), sb("KP", [rows, H, T], BF16)
        with nc.Block() as block:
            @block.gpsimd
            def _(pool):
                pool.memset(KP[PACKED:PACKED + 3, :, :], 1.0)
        with ExitStack() as early:
            ctxT = c.sb(early, "a2_ctxT", [P, DK, T])
            load_all(c, "a2_ctx", [(ctxT[:, :, :], ctx_T)])
            split_and_pack(c, "a2_ks", [[(None, None, ctxT[:, k, chunk(n)]) for k in range(DK)] for n in range(B)],
                           KP, K_PARTS, scratch, S)
        with ExitStack() as early:
            layernorm(c, early, "a2_ln")
            split_and_pack(c, "a2_qs", [[([(G[:, k, :], c.XNT[:, k, chunk(n)])], g[:, 0, k:k + 1], None)
                                         for k in range(DK)] for n in range(B)], QP, Q_PARTS, scratch, S, scale=-1.0)
            split_and_pack(c, "a2_cs", [[([(CW[:, k, :], c.XNT[:, k, chunk(n)]) for k in range(DK)], cc[:, :], None)]
                                        for n in range(B)], QP, None, scratch, S, rows=H, scale=-1.0, lead=PACKED)
        att = Attention(c, ctx, "a2_att", S, False, True)
        crow = att.probs[:, 0:2, :].rearrange("p a (t d) -> p (a t) d", t=2)
        pen, mrow = att.probs[:, 2, :], att.probs[:, 3, :].bitcast(I32)
        VB = sb("VB", [P, QT_B, H, SLOT])
        later, mask = sb("later", [P, QT_B, S], BF16), sb("mask", [P, QT_B, S])
        set_, q = c.sem("a2_set"), {k: c.sem("a2_b_" + k) for k in ("rows", "mask", "pen")}
        with nc.Block() as block:
            @block.gpsimd
            def _(pool):
                pool.memset(VB[:, :, :, DH:SLOT], 0.0).then_inc(set_, 1)
                pool.memset(later[:, :, :], 0.0).then_inc(set_, 1)
                pool.wait_ge(set_, 2)
                pool.memset(VB[:, :, :, DH:DH + 1], 1.0)
                for t in range(QT_B):
                    pool.affine_select(out=later[:, t, :], in_=later[:, t, :], compare_op=ALU.is_ge, fill=1.0,
                                       base=t * P, pattern=[[-1, S]], channel_multiplier=1)
        with nc.Fori(0, B) as b:
            with nc.Block() as block:
                @block.sync
                def _(sp):
                    sp.dma_start(crow, ctx_rows[:, bass.ds(b * QT_B, QT_B), :]).then_inc(q["rows"], 16)
                    sp.dma_start(mrow, key_mask[bass.ds(b, 1), :].rearrange("a s -> (a s)").partition_broadcast(P))\
                      .then_inc(q["mask"], 16)

                @block.gpsimd
                def _(pool):
                    pool.wait_ge(q["rows"], 16)
                    pool.tensor_copy(VB[:, :, :, 0:DH], crow.rearrange("p t (h d) -> p t h d", h=H))

                @block.vector
                def _(dve):
                    dve.wait_ge(q["mask"], 16)
                    dve.tensor_scalar(pen, mrow, -1.0, -NEG, ALU.add, ALU.mult).then_inc(q["pen"], 1)
                    dve.wait_ge(q["pen"], 1)
                    for t in range(QT_B):
                        dve.scalar_tensor_tensor(out=mask[:, t, :], in0=later[:, t, :], scalar=NEG, in1=pen,
                                                 op0=ALU.mult, op1=ALU.add)
            with nc.Block() as block:
                @block.gpsimd
                def _(pool):
                    for sm in q.values():
                        pool.sem_clear(sm)
            whole = slice(0, S)
            att.run(lambda qt, h: [(whole, QP[:, h, bass.ds(b * S + qt * P, P)], KP[:, h, bass.ds(b * S, S)])],
                    lambda qt: mask[:, qt, :], lambda qt, h, k: VB[:, k, h, :], WOUT, brow[:, :],
                    lambda dve, qt, delta: add_scaled(dve, c, 2, c.X[:, bass.ds(b * QT_B + qt, 1), :]
                                                      .rearrange("p a d -> p (a d)"), delta), sel=sel[:, :])
            att.clear()



WINDOW = 16


def layer3_attention(c, ctx_T, w, consts, scratch):
    nc = c.nc
    chunk = lambda b: slice(b * S, (b + 1) * S)
    tile = lambda t: slice(t * P, (t + 1) * P)
    with ExitStack() as ctx:
        sb = lambda n, shape, dt=F32: c.sb(ctx, "a3_" + n, shape, dt)
        QP, KP = sb("QP", [PACKED, H, T], BF16), sb("KP", [PACKED, H, T], BF16)
        V = sb("V", [P, NT, D])
        WOUT, bo, sel = sb("WOUT", [P, 4, D]), sb("bo", [1, D]), sb("sel", [P, P])
        zero_key = sb("zero_key", [PACKED, P], BF16)
        row = lambda v: v.rearrange("(a n) -> a n", a=1)
        with ExitStack() as early:
            tb = lambda n, shape, dt=F32: c.sb(early, "a3_" + n, shape, dt)
            W = {n: tb("W" + n, [P, DK, D]) for n in "qkv"}
            bq, bk, bv = tb("bq", [P, DK]), tb("bk", [P, DK]), tb("bv", [1, D])
            q_bias = tb("q_bias", [P, DK])
            with ExitStack() as kctx:
                ctxT = c.sb(kctx, "a3_ctxT", [P, DK, T])
                load_all(c, "a3", [(W[n][:, :, :], w[f"W{n}_T"]) for n in "kvq"] + [
                    (bq[:, :], w["bq_cols"]), (bk[:, :], w["bk_cols"]), (bv[:, :], row(w["bv"])),
                    (bo[:, :], row(w["bo"])), (WOUT[:, :, :], w["Wo_slots"]), (sel[:, :], consts["sum_rows"]),
                    (ctxT[:, :, :], ctx_T)])
                with nc.Block() as block:
                    @block.vector
                    def _(dve):
                        dve.tensor_scalar(q_bias[:, :], bq[:, :], -0.25, None, ALU.mult)

                    @block.gpsimd
                    def _(pool):
                        pool.memset(zero_key[:, :], 0.0)
                split_and_pack(c, "a3_ks", [[([(W["k"][:, i, tile(k)], ctxT[:, i, chunk(n)]) for i in range(DK)],
                                              bk[:, k:k + 1], None) for k in range(DK)] for n in range(B)],
                               KP, K_PARTS, scratch, S)
                project_columns(c, "a3_v", [
                    (columns(P, D), [(ctxT[:, i, tile(t)], W["v"][:, i, :]) for i in range(DK)]
                     + [(c.ones[0:1, :], bv[:, :])], V[:, t, :]) for t in range(NT)])
            layernorm(c, early, "a3_ln")
            split_and_pack(c, "a3_qs", [[([(W["q"][:, i, tile(k)], c.XNT[:, i, chunk(n)]) for i in range(DK)],
                                          q_bias[:, k:k + 1], None) for k in range(DK)] for n in range(B)],
                           QP, Q_PARTS, scratch, S, scale=-0.25)
        att = Attention(c, ctx, "a3_att", 2 * P, False, True)
        VB = sb("VB", [P, 1 + QT_B, H, SLOT])
        mask = sb("mask", [P, 2, 2 * P])
        built = c.sem("a3_built")
        with nc.Block() as block:
            @block.gpsimd
            def _(pool):
                pool.memset(VB[:, :, :, :], 0.0).then_inc(built, 1)
                pool.memset(mask[:, :, :], 0.0).then_inc(built, 1)
                pool.wait_ge(built, 2)
                pool.memset(VB[:, :, :, DH:DH + 1], 1.0).then_inc(built, 1)
                kinds = [(0, P, -1, 1), (0, WINDOW - 1 - P, 1, -1), (1, P, -1, 1), (1, WINDOW - 1 - P, 1, -1),
                         (0, P - WINDOW + 1, -1, 2)]
                for i, (m, base, step, per_query) in enumerate(kinds):
                    pool.affine_select(out=mask[:, m, :], in_=mask[:, m, :], compare_op=ALU.is_ge, fill=-F32_MIN / 2,
                                       base=base, pattern=[[step, 2 * P]], channel_multiplier=per_query)\
                        .then_inc(built, 1)
                    pool.wait_ge(built, 4 + i)
        with nc.Fori(0, B) as b:
            with nc.Block() as block:
                @block.gpsimd
                def _(pool):
                    pool.tensor_copy(VB[:, 1:1 + QT_B, :, 0:DH],
                                     V[:, bass.ds(b * QT_B, QT_B), :].rearrange("p t (h d) -> p t h d", h=H))

            def scores(qt, h):
                q = QP[:, h, bass.ds(b * S + qt * P, P)]
                if qt == 0:
                    return [(slice(0, P), q, zero_key[:, :]), (slice(P, 2 * P), q, KP[:, h, bass.ds(b * S, P)])]
                return [(slice(0, 2 * P), q, KP[:, h, bass.ds(b * S + (qt - 1) * P, 2 * P)])]
            att.run(scores, lambda qt: mask[:, min(qt, 1), :], lambda qt, h, k: VB[:, qt + k, h, :], WOUT, bo[:, :],
                    lambda dve, qt, delta: add_scaled(dve, c, 3, c.X[:, bass.ds(b * QT_B + qt, 1), :]
                                                      .rearrange("p a d -> p (a d)"), delta), sel=sel[:, :])
            att.clear()



FF3 = 1024


def layer3_ffn(c, w):
    nc = c.nc
    nf = FF3 // P
    with ExitStack() as ctx:
        sb = lambda n, shape, dt=F32: c.sb(ctx, "f3_" + n, shape, dt)
        W1, W2 = sb("W1", [P, DK * FF3]), sb("W2", [P, nf * D])
        b1, b2 = sb("b1", [P, nf]), sb("b2", [1, D])
        hid = sb("hid", [P, 2, nf, S])
        load_all(c, "f3", [(W1[:, :], w["W1_T"].rearrange("p k n -> p (k n)")),
                           (W2[:, :], w["W2_T"].rearrange("p k n -> p (k n)")),
                           (b1[:, :], w["b1_cols"]), (b2[:, :], w["b2"].rearrange("(a n) -> a n", a=1))])
        with ExitStack() as early:
            rounded = c.sb(early, "f3_rounded", [P, 2, DK * FF3])
            tot, scale = c.sb(early, "f3_tot", [P, 2]), c.sb(early, "f3_scale", [P, 2])
            v, summed = Tally(c.sem("f3_w_dve")), c.sem("f3_summed")
            with nc.Block() as block:
                @block.vector
                def _(dve):
                    n = [0]

                    def then(ins):
                        dve.wait_ge(v.sem, v.mark(ins))
                    for i, Wt in enumerate((W1, W2)):
                        then(dve.tensor_reduce(tot[:, i:i + 1], Wt[:, :], X_AXIS, ALU.add, apply_absolute_value=True))
                    dve.wait_ge(summed, 1)
                    then(dve.tensor_scalar(scale[:, :], c.PS[:, 0, 0:2], 1.0 / (D * FF3), 1e-8, ALU.mult, ALU.max))
                    then(dve.reciprocal(scale[:, :], scale[:, :]))
                    for i, Wt in enumerate((W1, W2)):
                        R = rounded[:, i, :]
                        then(dve.tensor_scalar(R, Wt[:, :], scale[:, i:i + 1], MAGIC, ALU.mult, ALU.add))
                        then(dve.tensor_scalar(R, R, -MAGIC, 1.0, ALU.add, ALU.min))
                        then(dve.scalar_tensor_tensor(out=R, in0=R, scalar=-1.0, in1=Wt[:, :], op0=ALU.max,
                                                      op1=ALU.subtract))
                        then(dve.tensor_tensor(Wt[:, :], Wt[:, :], R, ALU.add))

                @block.tensor
                def _(pe):
                    pe.wait_ge(v.sem, 2)
                    pe.matmul(c.PS[:, 0, 0:2], c.ones[:, :], tot[:, :], start=True, stop=True).then_inc(summed, 1)
        layernorm(c, ctx, "f3_ln")
        s = {k: c.sem("f3_" + k) for k in ("made", "gelu", "out", "added")}
        W1v = W1[:, :].rearrange("p (k n) -> p k n", k=DK)
        W2v = W2[:, :].rearrange("p (k n) -> p k n", k=nf)
        with nc.Block() as block:
            @block.tensor
            def _(pe):
                def up(n):
                    for f in range(nf):
                        i = n * nf + f
                        if i >= 4:
                            pe.wait_ge(s["gelu"], i - 3)
                        for k in range(DK):
                            mm = pe.matmul(c.PS[:, i % 4, :], W1v[:, k, f * P:(f + 1) * P],
                                           c.XNT[:, k, n * S:(n + 1) * S], start=(k == 0), stop=(k == DK - 1))
                        mm.then_inc(s["made"], 1)

                def down(n):
                    pe.wait_ge(s["gelu"], nf * (n + 1))
                    for t in range(QT_B):
                        i = n * QT_B + t
                        if i >= 4:
                            pe.wait_ge(s["added"], i - 3)
                        for f in range(nf):
                            pe.matmul(c.PS[:, 4 + i % 4, 0:D], hid[:, n % 2, f, t * P:(t + 1) * P], W2v[:, f, :],
                                      start=(f == 0), stop=False)
                        pe.matmul(c.PS[:, 4 + i % 4, 0:D], c.ones[0:1, :], b2[:, :], start=False, stop=True)\
                            .then_inc(s["out"], 1)
                up(0)
                for n in range(B):
                    if n + 1 < B:
                        up(n + 1)
                    down(n)

            @block.scalar
            def _(act):
                for n in range(B):
                    for f in range(nf):
                        i = n * nf + f
                        act.wait_ge(s["made"], i + 1)
                        if n >= 2 and f == 0:
                            act.wait_ge(s["out"], QT_B * (n - 1))
                        act.activation(hid[:, n % 2, f, :], c.PS[:, i % 4, :], ACT.Gelu, bias=b1[:, f:f + 1])\
                           .then_inc(s["gelu"], 1)

            @block.vector
            def _(dve):
                for i in range(NT):
                    dve.wait_ge(s["out"], i + 1)
                    add_scaled(dve, c, 7, c.X[:, i, :], c.PS[:, 4 + i % 4, 0:D]).then_inc(s["added"], 1)



E = 8
SLOT_TILES = NT + E - 1
MAGIC = 1.5 * 2.0 ** 23


def first_best(c, dve, then, values, best, number, junk3, numbers):
    then(dve.tensor_tensor(junk3, values, best.unsqueeze(2).to_broadcast([P, NT, E]), ALU.is_equal))
    then(dve.scalar_tensor_tensor(out=junk3, in0=numbers, scalar=-float(E), in1=junk3, op0=ALU.add, op1=ALU.mult))
    then(dve.tensor_reduce(number, junk3, X_AXIS, ALU.min))
    then(dve.tensor_scalar(number, number, float(E), None, ALU.add))


def dispatch(c, name, place, tile_expert, expert, rows, consts, xs, clear_xs):
    nc = c.nc
    with ExitStack() as ctx:
        sb = lambda n, shape, dt=F32: c.sb(ctx, name + "_" + n, shape, dt)
        numbers, tiles_no = sb("numbers", [P, NT, E]), sb("tiles_no", [P, SLOT_TILES, E])
        later = sb("later", [P, P])
        hot, before = sb("hot", [P, NT, E]), sb("before", [P, NT, E])
        carry = sb("carry", [P, NT + 1, E])
        need, end, start = sb("need", [P, E]), sb("end", [P, E]), sb("start", [P, E])
        place_f, tile_f, cmp = sb("place_f", [P, NT]), sb("tile_f", [P, SLOT_TILES]), sb("cmp", [P, SLOT_TILES, E])
        zeros = sb("zeros", [P, D])
        load_all(c, name + "_c", [(numbers[:, :, :], consts["numbers"]), (tiles_no[:, :, :], consts["tile_numbers"]),
                                  (later[:, :], consts["later"])])
        v, hot_ready, counted = Tally(c.sem(name + "_dve")), c.sem(name + "_hot"), c.sem(name + "_counted")
        placed, zeroed, cleared = c.sem(name + "_placed"), c.sem(name + "_zeroed"), c.soft_sems[name + "_cleared"]
        sent = c.soft_sems[name + "_sent"]
        flat = lambda ap: ap.rearrange("p t e -> p (t e)")
        with nc.Block() as block:
            @block.vector
            def _(dve):
                def then(ins):
                    dve.wait_ge(v.sem, v.mark(ins))
                then(dve.memset(carry[:, 0, :], 0.0))
                dve.tensor_tensor(hot[:, :, :], numbers[:, :, :],
                                  expert.unsqueeze(2).to_broadcast([P, NT, E]), ALU.is_equal).then_inc(hot_ready, 1)
                dve.wait_ge(counted, 1)
                totals = c.PS[:, 1, 0:NT * E].rearrange("p (t e) -> p t e", t=NT)
                for t in range(NT):
                    then(dve.tensor_tensor(carry[:, t + 1, :], totals[:, t, :], carry[:, t, :], ALU.add))
                then(dve.tensor_scalar(need[:, :], carry[:, NT, :], 1.0 / P, 0.5 - 0.5 / P, ALU.mult, ALU.add))
                then(dve.tensor_scalar(need[:, :], need[:, :], MAGIC, None, ALU.add))
                then(dve.tensor_scalar(need[:, :], need[:, :], -MAGIC, None, ALU.add))
                then(dve.tensor_tensor_scan(end[:, :], c.ones[:, 0:E], need[:, :], 0.0, ALU.mult, ALU.add))
                then(dve.tensor_tensor(start[:, :], end[:, :], need[:, :], ALU.subtract))
                then(dve.tensor_scalar(start[:, :], start[:, :], float(P), None, ALU.mult))
                then(dve.tensor_tensor(before[:, :, :], c.PS[:, 0, 0:NT * E].rearrange("p (t e) -> p t e", t=NT),
                                       carry[:, 0:NT, :], ALU.add))
                then(dve.tensor_tensor(before[:, :, :], before[:, :, :],
                                       start[:, :].unsqueeze(1).to_broadcast([P, NT, E]), ALU.add))
                then(dve.tensor_tensor(before[:, :, :], before[:, :, :], hot[:, :, :], ALU.mult))
                then(dve.tensor_reduce(place_f[:, :], before[:, :, :], X_AXIS, ALU.add))
                dve.tensor_copy(place[:, :], place_f[:, :]).then_inc(placed, 1)
                then(dve.tensor_tensor(cmp[:, :, :], tiles_no[:, :, :],
                                       end[:, :].unsqueeze(1).to_broadcast([P, SLOT_TILES, E]), ALU.is_ge))
                then(dve.tensor_reduce(tile_f[:, :], cmp[:, :, :], X_AXIS, ALU.add))
                then(dve.tensor_scalar(tile_f[:, :], tile_f[:, :], E - 1.0, None, ALU.min))
                dve.tensor_copy(tile_expert[:, :], tile_f[:, :])

            @block.tensor
            def _(pe):
                pe.wait_ge(hot_ready, 1)
                pe.matmul(c.PS[:, 0, 0:NT * E], later[:, :], flat(hot[:, :, :]), start=True, stop=True)
                pe.matmul(c.PS[:, 1, 0:NT * E], c.ones[:, :], flat(hot[:, :, :]), start=True, stop=True)\
                    .then_inc(counted, 1)

            @block.gpsimd
            def _(pool):
                if clear_xs:
                    pool.memset(zeros[:, :], 0.0).then_inc(zeroed, 1)
                    pool.wait_ge(zeroed, 1)
                    for i in range(SLOT_TILES):
                        pool.dma_start(xs[i * P:(i + 1) * P, :], zeros[:, :]).then_inc(cleared, 16)
                    pool.wait_ge(cleared, 16 * SLOT_TILES)
                pool.wait_ge(placed, 1)
                for t in range(NT):
                    pool.indirect_dma_start(xs, bass.IndirectOffsetOnAxis(ap=place[:, t:t + 1].bitcast(U32), axis=0),
                                            rows[:, t, :], None).then_inc(sent, 16)
                pool.wait_ge(sent, 16 * NT)


class Turn:

    def __init__(self, n, half, par):
        self.n, self.half, self.par = n, half, par


def expert_tiles(c, name, scope, tile_expert, xs, ys, weights_in, weights_out, hidden, gated, biases=None):
    nc = c.nc
    nh = hidden // P
    with ExitStack() as ctx:
        sb = lambda n, shape, dt=F32: c.sb(ctx, name + "_" + n, shape, dt)
        xr, xt = sb("xr", [P, 2, D]), sb("xt", [P, 2, DK, P])
        act_h, hid, hidT, y = sb("act_h", [P, 2, 512]), sb("hid", [P, 2, hidden]), sb("hidT", [P, 2, nh, P]), sb("y", [P, 2, D])
        brow1, brow2 = (sb("brow1", [1, 2, hidden]), sb("brow2", [1, 2, D])) if biases else (None, None)
        s = {k: c.sem(name + "_" + k) for k in ("x_turned", "x_copied", "hidden", "act", "hid", "h_turned",
                                                "h_copied_a", "h_copied_d", "out", "y")}
        loaded = [c.sem(f"{name}_loaded{i}") for i in range(2)]
        stored = [c.sem(f"{name}_stored{i}") for i in range(2)]
        b1_in = [c.sem(f"{name}_b1_in{i}") for i in range(2)]
        b2_in = [c.sem(f"{name}_b2_in{i}") for i in range(2)]

        with nc.Block() as block:
            @block.tensor
            def _(pe):
                for k in ("x_turned", "hidden", "out"):
                    pe.sem_inc(s[k], 2)

            @block.scalar
            def _(act):
                for k in ("act", "x_copied", "h_copied_a"):
                    act.sem_inc(s[k], 2)

            @block.vector
            def _(dve):
                for k in ("hid", "y", "h_copied_d"):
                    dve.sem_inc(s[k], 2)

            @block.sync
            def _(sp):
                for q in stored:
                    sp.sem_inc(q, 16)

        FIRST, LAST = 1, SLOT_TILES - 2

        def over_tiles(eng, step, before, after):
            before()
            with eng.Fori(0, (LAST - FIRST) // 2) as it:
                for j in range(2):
                    step(Turn(it * 2 + (FIRST + j), it + (FIRST + j) // 2, (FIRST + j) % 2))
            after()

        assert (LAST - FIRST) % 2 == 0
        fixed = lambda n: Turn(n, n // 2, n % 2)
        N = SLOT_TILES

        with nc.Block() as block:
            @block.sync
            def _(sp):
                def load(t):
                    sp.wait_ge(s["x_turned"], t.n + 1)
                    sp.dma_start(xr[:, t.par, :], xs[bass.ds(t.n * P, P), :]).then_inc(loaded[t.par], 16)

                def load_bias(t, which):
                    if not biases:
                        return
                    row, used, into = ((brow1, "hidden", b1_in), (brow2, "out", b2_in))[which]
                    e = sp.value_load(tile_expert[0:1, bass.ds(t.n, 1)], min_val=0, max_val=E - 1)
                    sp.wait_ge(s[used], t.n + 1)
                    sp.dma_start(row[:, t.par, :], biases[which][bass.ds(e, 1), :]).then_inc(into[t.par], 16)

                def save(t):
                    sp.wait_ge(s["y"], t.n + 3)
                    sp.dma_start(ys[bass.ds(t.n * P, P), :], y[:, t.par, :]).then_inc(stored[t.par], 16)

                def step(t):
                    nxt = Turn(t.n + 1, t.half + t.par, 1 - t.par)
                    load(nxt)
                    load_bias(nxt, 0)
                    save(Turn(t.n - 1, t.half - 1 + t.par, 1 - t.par))
                    load_bias(t, 1)
                over_tiles(sp, step, lambda: (load(fixed(0)), load_bias(fixed(0), 0), load(fixed(1)),
                                              load_bias(fixed(1), 0), load_bias(fixed(0), 1)),
                           lambda: (step(fixed(N - 2)), save(fixed(N - 2)), load_bias(fixed(N - 1), 1),
                                    save(fixed(N - 1))))
                for par in range(2):
                    sp.wait_ge(stored[par], 16 * (1 + (N + 1 - par) // 2))

            @block.tensor
            def _(pe):
                def turn_x(t):
                    pe.wait_ge(loaded[t.par], t.half * 16 + 16)
                    pe.wait_ge(s["x_copied"], t.n + 2)
                    for k in range(DK):
                        mm = pe.transpose(c.PS[:, 0, k * P:(k + 1) * P], xr[:, t.par, k * P:(k + 1) * P],
                                          c.ident[:, :])
                    mm.then_inc(s["x_turned"], 1)

                def first(t):
                    pe.wait_ge(s["x_copied"], t.n + 3)
                    pe.wait_ge(s["act"], t.n + 1)
                    pe.wait_ge(s["hid"], t.n + 1)
                    e = pe.value_load(tile_expert[0:1, bass.ds(t.n, 1)], min_val=0, max_val=E - 1)
                    for i, Wi in enumerate(weights_in):
                        bank = c.PS[:, 2 + 2 * t.par + i, :]
                        for k in range(DK):
                            mm = pe.matmul(bank, xt[:, t.par, k, :],
                                           Wi[:, k, bass.ds(e, 1), :].rearrange("p a n -> p (a n)"),
                                           start=(k == 0), stop=(k == DK - 1 and not biases))
                        if biases:
                            if i == 0:
                                pe.wait_ge(b1_in[t.par], t.half * 16 + 16)
                            mm = pe.matmul(bank, c.ones[0:1, :], brow1[:, t.par, 512 * i:512 * (i + 1)], start=False,
                                           stop=True)
                    mm.then_inc(s["hidden"], 1)

                def second(t):
                    pe.wait_ge(s["hid"], t.n + 3)
                    if biases:
                        pe.wait_ge(s["act"], t.n + 3)
                    pe.wait_ge(s["h_copied_d"], t.n + 2)
                    if nh > 4:
                        pe.wait_ge(s["h_copied_a"], t.n + 2)
                    for f in range(nh):
                        mm = pe.transpose(c.PS[:, 1 if f < 4 else 6, (f % 4) * P:(f % 4 + 1) * P],
                                          hid[:, t.par, f * P:(f + 1) * P], c.ident[:, :])
                    mm.then_inc(s["h_turned"], 1)
                    e = pe.value_load(tile_expert[0:1, bass.ds(t.n, 1)], min_val=0, max_val=E - 1)
                    pe.wait_ge(s["h_copied_d"], t.n + 3)
                    if nh > 4:
                        pe.wait_ge(s["h_copied_a"], t.n + 3)
                    pe.wait_ge(s["y"], t.n + 2)
                    for f in range(nh):
                        mm = pe.matmul(c.PS[:, 7, 0:D], hidT[:, t.par, f, :],
                                       weights_out[:, f, bass.ds(e, 1), :].rearrange("p a n -> p (a n)"),
                                       start=(f == 0), stop=(f == nh - 1 and not biases))
                    if biases:
                        pe.wait_ge(b2_in[t.par], t.half * 16 + 16)
                        mm = pe.matmul(c.PS[:, 7, 0:D], c.ones[0:1, :], brow2[:, t.par, :], start=False, stop=True)
                    mm.then_inc(s["out"], 1)

                def step(t):
                    first(t)
                    turn_x(Turn(t.n + 1, t.half + t.par, 1 - t.par))
                    second(Turn(t.n - 1, t.half - 1 + t.par, 1 - t.par))
                over_tiles(pe, step, lambda: (turn_x(fixed(0)), first(fixed(0)), turn_x(fixed(1))),
                           lambda: (step(fixed(N - 2)), first(fixed(N - 1)), second(fixed(N - 2)),
                                    second(fixed(N - 1))))

            @block.scalar
            def _(act):
                def copy_x(t):
                    act.wait_ge(s["x_turned"], t.n + 3)
                    if True:
                        act.wait_ge(s["act"], t.n + 1)
                    act.copy(xt[:, t.par, :, :], c.PS[:, 0, 0:D].rearrange("p (k q) -> p k q", k=DK))\
                       .then_inc(s["x_copied"], 1)

                def activate(t):
                    act.wait_ge(s["hidden"], t.n + 3)
                    act.wait_ge(s["out"], t.n + 1)
                    if gated:
                        act.activation(act_h[:, t.par, :], c.PS[:, 2 + 2 * t.par, :], ACT.Silu)\
                           .then_inc(s["act"], 1)
                    else:
                        act.activation(hid[:, t.par, 0:512], c.PS[:, 2 + 2 * t.par, :], ACT.Relu)\
                           .then_inc(s["act"], 1)

                def copy_h(t):
                    if nh > 4:
                        act.wait_ge(s["h_turned"], t.n + 1)
                        act.copy(hidT[:, t.par, 4:8, :], c.PS[:, 6, :].rearrange("p (f q) -> p f q", f=4))\
                           .then_inc(s["h_copied_a"], 1)

                def step(t):
                    activate(t)
                    copy_x(Turn(t.n + 1, t.half + t.par, 1 - t.par))
                    copy_h(Turn(t.n - 1, t.half - 1 + t.par, 1 - t.par))
                over_tiles(act, step, lambda: (copy_x(fixed(0)), activate(fixed(0)), copy_x(fixed(1))),
                           lambda: (step(fixed(N - 2)), activate(fixed(N - 1)), copy_h(fixed(N - 2)),
                                    copy_h(fixed(N - 1))))

            @block.vector
            def _(dve):
                def combine(t):
                    dve.wait_ge(s["hidden"], t.n + 3)
                    if gated:
                        dve.wait_ge(s["act"], t.n + 3)
                    dve.wait_ge(s["out"], t.n + 1)
                    up = c.PS[:, 3 + 2 * t.par, :]
                    if gated:
                        dve.tensor_tensor(hid[:, t.par, :], up, act_h[:, t.par, :], ALU.mult).then_inc(s["hid"], 1)
                    else:
                        dve.tensor_scalar(hid[:, t.par, 512:1024], up, 0.0, None, ALU.max).then_inc(s["hid"], 1)

                def finish(t):
                    dve.wait_ge(s["h_turned"], t.n + 1)
                    dve.tensor_copy(hidT[:, t.par, 0:4, :], c.PS[:, 1, :].rearrange("p (f q) -> p f q", f=4))\
                       .then_inc(s["h_copied_d"], 1)
                    dve.wait_ge(s["out"], t.n + 3)
                    dve.wait_ge(stored[t.par], t.half * 16 + 16)
                    dve.tensor_copy(y[:, t.par, :], c.PS[:, 7, 0:D]).then_inc(s["y"], 1)

                def step(t):
                    combine(t)
                    finish(Turn(t.n - 1, t.half - 1 + t.par, 1 - t.par))
                over_tiles(dve, step, lambda: combine(fixed(0)),
                           lambda: (step(fixed(N - 2)), combine(fixed(N - 1)), finish(fixed(N - 2)),
                                    finish(fixed(N - 1))))


def collect(c, name, place, ys, gate):
    with ExitStack() as ctx:
        got = c.sb(ctx, name + "_got", [P, NT, D])
        arrived = [c.soft_sems[f"{name}_got{t}"] for t in range(4)]
        with c.nc.Block() as block:
            @block.gpsimd
            def _(pool):
                for t in range(NT):
                    pool.indirect_dma_start(got[:, t, :], None, ys,
                                            bass.IndirectOffsetOnAxis(ap=place[:, t:t + 1].bitcast(U32), axis=0))\
                        .then_inc(arrived[t // 4], 16)

            @block.vector
            def _(dve):
                for i in range(4):
                    dve.wait_ge(arrived[i], 64)
                    for t in range(4 * i, 4 * i + 4):
                        add_scaled(dve, c, gate, c.X[:, t, :], got[:, t, :])



FF0 = 512


def layer0_ffn(c, w, consts, xs, ys):
    nc = c.nc
    nf = FF0 // P
    with ExitStack() as ctx:
        sb = lambda n, shape, dt=F32: c.sb(ctx, "f0_" + n, shape, dt)
        place, tile_expert = sb("place", [P, NT], I32), sb("tile_expert", [P, SLOT_TILES], I32)
        Wg, Wu, Wd = sb("Wg", [P, DK, E, FF0]), sb("Wu", [P, DK, E, FF0]), sb("Wd", [P, nf, E, D])
        with ExitStack() as early:
            tb = lambda n, shape, dt=F32: c.sb(early, "f0_" + n, shape, dt)
            c.XNT = tb("XNT", [P, DK, T])
            c.XN = tb("XN", [P, NT, D])
            Sg, Su, Sd = tb("Sg", [P, DK, FF0]), tb("Su", [P, DK, FF0]), tb("Sd", [P, nf, D])
            router, lnw, lnb = tb("router", [P, DK, E]), tb("lnw", [P, D]), tb("lnb", [P, D])
            logits, best, expert, score = tb("logits", [P, NT, E]), tb("best", [P, NT]), tb("expert", [P, NT]), tb("score", [P, NT])
            eq, numbers = tb("eq", [P, NT, E]), tb("numbers", [P, NT, E])
            load_all(c, "f0", [(Sg[:, :, :], w["sh_gate"].rearrange("(k p) n -> p k n", p=P)),
                               (Su[:, :, :], w["sh_up"].rearrange("(k p) n -> p k n", p=P)),
                               (Sd[:, :, :], w["sh_down"].rearrange("(k p) n -> p k n", p=P)),
                               (router[:, :, :], w["router_w"].rearrange("(k p) n -> p k n", p=P)),
                               (lnw[:, :], w["ln_w"].partition_broadcast(P)), (lnb[:, :], w["ln_b"].partition_broadcast(P)),
                               (numbers[:, :, :], consts["numbers"])] + [
                (dst[:, k, :, :], src[:, k * P:(k + 1) * P, :].rearrange("e p n -> p e n"))
                for dst, src, n in ((Wg, w["gate_w"], DK), (Wu, w["up_w"], DK), (Wd, w["down_w"], nf))
                for k in range(n)])
            normalise(c, "f0_n1", c.X, c.XN)
            with nc.Block() as block:
                @block.vector
                def _(dve):
                    for t in range(NT):
                        add_scaled(dve, c, 4, c.X[:, t, :], c.XN[:, t, :])
            normalise(c, "f0_n2", c.XN, c.XN, (lnw, lnb))
            transpose_tokens(c, "f0_t", c.XN, c.XNT)
            token_logits(c, "f0_route", router, E, logits[:, :, :])
            v, scored = Tally(c.sem("f0_r_dve")), c.sem("f0_scored")
            with nc.Block() as block:
                @block.vector
                def _(dve):
                    def then(ins):
                        dve.wait_ge(v.sem, v.mark(ins))
                    then(dve.tensor_reduce(best[:, :], logits[:, :, :], X_AXIS, ALU.max))
                    first_best(c, dve, then, logits[:, :, :], best[:, :], expert[:, :], eq[:, :, :], numbers[:, :, :])

                @block.scalar
                def _(act):
                    act.wait_ge(v.sem, 1)
                    act.activation(score[:, :], best[:, :], ACT.Sigmoid)
            s = {k: c.sem("f0_" + k) for k in ("gate", "silu", "hid", "out", "added")}
            with ExitStack() as sh:
                silu, hid = c.sb(sh, "f0_silu", [P, 2, S]), c.sb(sh, "f0_hid", [P, nf, S])
                with nc.Block() as block:
                    @block.tensor
                    def _(pe):
                        for n in range(B):
                            for f in range(nf):
                                i = n * nf + f
                                if i >= 2:
                                    pe.wait_ge(s["hid"], i - 1)
                                for m, Wm in ((0, Sg), (1, Su)):
                                    for k in range(DK):
                                        mm = pe.matmul(c.PS[:, 2 * (i % 2) + m, :], Wm[:, k, f * P:(f + 1) * P],
                                                       c.XNT[:, k, n * S:(n + 1) * S], start=(k == 0),
                                                       stop=(k == DK - 1))
                                mm.then_inc(s["gate"], 1)
                            pe.wait_ge(s["hid"], nf * (n + 1))
                            for t in range(QT_B):
                                i = n * QT_B + t
                                if i >= 4:
                                    pe.wait_ge(s["added"], i - 3)
                                for f in range(nf):
                                    mm = pe.matmul(c.PS[:, 4 + i % 4, 0:D], hid[:, f, t * P:(t + 1) * P], Sd[:, f, :],
                                                   start=(f == 0), stop=(f == nf - 1))
                                mm.then_inc(s["out"], 1)

                    @block.scalar
                    def _(act):
                        for i in range(B * nf):
                            act.wait_ge(s["gate"], i + 1)
                            if i >= 2:
                                act.wait_ge(s["hid"], i - 1)
                            act.activation(silu[:, i % 2, :], c.PS[:, 2 * (i % 2), :], ACT.Silu).then_inc(s["silu"], 1)

                    @block.vector
                    def _(dve):
                        for n in range(B):
                            for f in range(nf):
                                i = n * nf + f
                                dve.wait_ge(s["silu"], i + 1)
                                if n >= 1 and f == 0:
                                    dve.wait_ge(s["out"], QT_B * n)
                                dve.tensor_tensor(hid[:, f, :], c.PS[:, 2 * (i % 2) + 1, :], silu[:, i % 2, :],
                                                  ALU.mult).then_inc(s["hid"], 1)
                            for t in range(QT_B):
                                i = n * QT_B + t
                                dve.wait_ge(s["out"], i + 1)
                                add_scaled(dve, c, 4, c.X[:, i, :], c.PS[:, 4 + i % 4, 0:D]).then_inc(s["added"], 1)
            with nc.Block() as block:
                @block.vector
                def _(dve):
                    for t in range(NT):
                        dve.tensor_scalar(c.XN[:, t, :], c.XN[:, t, :], score[:, t:t + 1], None, ALU.mult)
            dispatch(c, "f0_d", place, tile_expert, expert[:, :], c.XN, consts, xs, True)
        expert_tiles(c, "f0_e", ctx, tile_expert, xs, ys, (Wg, Wu), Wd, FF0, True)
        collect(c, "f0_c", place, ys, 4)



FF2 = 1024
CAPACITY = -(-T * 5 // (E * 4))


def layer2_ffn(c, w, consts, xs, ys):
    nc = c.nc
    with ExitStack() as ctx:
        sb = lambda n, shape, dt=F32: c.sb(ctx, "f2_" + n, shape, dt)
        W1a, W1b = sb("W1a", [P, DK, E, 512]), sb("W1b", [P, DK, E, 512])
        place, tile_expert = sb("place", [P, NT], I32), sb("tile_expert", [P, SLOT_TILES], I32)
        with ExitStack() as early:
            tb = lambda n, shape, dt=F32: c.sb(early, "f2_" + n, shape, dt)
            layernorm(c, early, "f2_ln", keep_rows=True)
            router, earlier, numbers = tb("router", [P, DK, E]), tb("earlier", [P, P]), tb("numbers", [P, NT, E])
            logits, best, expert = tb("logits", [P, NT, E]), tb("best", [P, NT]), tb("expert", [P, NT])
            tot, eq, rank, keep = tb("tot", [P, NT]), tb("eq", [P, NT, E]), tb("rank", [P, NT]), tb("keep", [P, NT])
            p_rows, e_rows = tb("p_rows", [P, T]), tb("e_rows", [P, T])
            part = tb("part", [P, NT, 4])
            load_all(c, "f2", [(router[:, :, :], w["router_T"]), (earlier[:, :], consts["earlier"]),
                               (numbers[:, :, :], consts["numbers"])] + [
                (dst[:, k, :, :], w["W1"][:, k * P:(k + 1) * P, 512 * i:512 * (i + 1)].rearrange("e p n -> p e n"))
                for i, dst in enumerate((W1a, W1b)) for k in range(DK)])
            token_logits(c, "f2_route", router, E, logits[:, :, :])
            v, exped = Tally(c.sem("f2_r_dve")), c.sem("f2_exped")
            wide = lambda ap: ap.unsqueeze(2).to_broadcast([P, NT, E])
            with nc.Block() as block:
                @block.vector
                def _(dve):
                    def then(ins):
                        dve.wait_ge(v.sem, v.mark(ins))
                    lg = logits[:, :, :]
                    then(dve.tensor_reduce(best[:, :], lg, X_AXIS, ALU.max))
                    then(dve.tensor_tensor(lg, lg, wide(best[:, :]), ALU.subtract))
                    dve.wait_ge(exped, 1)
                    then(dve.tensor_reduce(tot[:, :], lg, X_AXIS, ALU.add))
                    then(dve.reciprocal(tot[:, :], tot[:, :]))
                    then(dve.tensor_tensor(lg, lg, wide(tot[:, :]), ALU.mult))
                    then(dve.tensor_reduce(best[:, :], lg, X_AXIS, ALU.max))
                    first_best(c, dve, then, lg, best[:, :], expert[:, :], eq[:, :, :], numbers[:, :, :])

                @block.scalar
                def _(act):
                    act.wait_ge(v.sem, 2)
                    act.activation(logits[:, :, :], logits[:, :, :], ACT.Exp).then_inc(exped, 1)
            with ExitStack() as tmp:
                rows_of_columns(c, "f2_p", tmp, best, p_rows)
            with ExitStack() as tmp:
                rows_of_columns(c, "f2_e", tmp, expert, e_rows)
            with ExitStack() as tmp:
                same, junk = c.sb(tmp, "f2_same", [P, 2, T], BF16), c.sb(tmp, "f2_junk", [P, 2, T], BF16)
                diag, junk2 = c.sb(tmp, "f2_diag", [P, 2, P]), c.sb(tmp, "f2_junk2", [P, 2, P])
                k = Tally(c.sem("f2_k_dve"))
                with nc.Block() as block:
                    @block.vector
                    def _(dve):
                        then = lambda ins: k.mark(ins)
                        then(dve.memset(part[:, :, :], 0.0))
                        dve.wait_ge(k.sem, 1)
                        for t in range(NT):
                            r2 = t % 2
                            key = best[:, t:t + 1]
                            if t >= 2:
                                dve.wait_ge(k.sem, k.n - 5 if t != 2 and t != NT - 1 else k.n)
                            then(dve.tensor_scalar(same[:, r2, :], e_rows[:, :], expert[:, t:t + 1], None, ALU.is_equal))
                            dve.wait_ge(k.sem, k.n)
                            then(dve.tensor_tensor(diag[:, r2, :], earlier[:, :], same[:, r2, t * P:(t + 1) * P], ALU.mult))
                            dve.wait_ge(k.sem, k.n)
                            for i, (lo, hi, op) in enumerate(((0, t * P, ALU.is_ge), (t * P, T, ALU.is_gt))):
                                if lo < hi:
                                    then(dve.scalar_tensor_tensor(
                                        out=junk[:, r2, lo:hi], in0=p_rows[:, lo:hi], scalar=key,
                                        in1=same[:, r2, lo:hi], op0=op, op1=ALU.mult, accum_out=part[:, t, i:i + 1]))
                            then(dve.scalar_tensor_tensor(
                                out=junk2[:, r2, :], in0=p_rows[:, t * P:(t + 1) * P], scalar=key,
                                in1=diag[:, r2, :], op0=ALU.is_equal, op1=ALU.mult, accum_out=part[:, t, 2:3]))
                        dve.wait_ge(k.sem, k.n)
                        then(dve.tensor_reduce(rank[:, :], part[:, :, :], X_AXIS, ALU.add))
                        dve.wait_ge(k.sem, k.n)
                        then(dve.tensor_scalar(keep[:, :], rank[:, :], float(CAPACITY), None, ALU.is_lt))
                        dve.wait_ge(k.sem, k.n)
                        then(dve.tensor_tensor(expert[:, :], expert[:, :], keep[:, :], ALU.mult))
            dispatch(c, "f2_d", place, tile_expert, expert[:, :], c.XN, consts, xs, False)
        W2 = sb("W2", [P, FF2 // P, E, D])
        load_all(c, "f2_w2", [(W2[:, k, :, :], w["W2"][:, k * P:(k + 1) * P, :].rearrange("e p n -> p e n"))
                              for k in range(FF2 // P)])
        expert_tiles(c, "f2_e", ctx, tile_expert, xs, ys, (W1a, W1b), W2, FF2, False, (w["b1"], w["b2"]))
        collect(c, "f2_c", place, ys, 6)


def store(c, out):
    stored = c.sem("stored")
    with c.nc.Block() as block:
        @block.sync
        def _(sp):
            sp.dma_start(out.rearrange("b (t p) d -> p (b t) d", p=P), c.X[:, :, :]).then_inc(stored, 16)
            sp.wait_ge(stored, 16)


def build(nc, a, out):
    with ExitStack() as ctx:
        c = Core(nc, ctx)
        scratch = nc.dram_tensor("parts_scratch", (3, D, T), BF16).ap()
        xs = nc.dram_tensor("expert_in", (SLOT_TILES * P, D), F32).ap()
        ys = nc.dram_tensor("expert_out", (SLOT_TILES * P, D), F32).ap()
        prologue(c, a["x"], a["ctx_1024"], a["g_xattn"], a["g_ffn"])
        part = lambda prefix: {k[len(prefix):]: v for k, v in a.items() if k.startswith(prefix)}
        stages = [
            lambda: layer0_attention(c, a["ctx_T"], a["seg_T"], part("L0_xattn_"), a["rope_tables"]),
            lambda: layer0_ffn(c, part("L0_ffn_"), part("const_"), xs, ys),
            lambda: layer1_attention(c, a["ctx_T"], a["ctx_rows"], part("L1_xattn_")),
            lambda: layer1_ffn(c, part("L1_ffn_"), part("const_"), scratch),
            lambda: layer2_attention(c, a["ctx_T"], a["ctx_rows"], a["mask_BxS2_ik0"], part("L2_xattn_"),
                                     part("const_"), scratch),
            lambda: layer2_ffn(c, part("L2_ffn_"), part("const_"), xs, ys),
            lambda: layer3_attention(c, a["ctx_T"], part("L3_xattn_"), part("const_"), scratch),
            lambda: layer3_ffn(c, part("L3_ffn_")),
        ]
        for st in stages:
            st()
            c.end_stage()
        store(c, out)




def rope_tables():
    half = HD // 2
    inv = (1.0 / 10000.0 ** (np.arange(half, dtype=np.float32) / np.float32(half))).astype(np.float32)
    ang = (np.arange(S, dtype=np.float32)[None, :] * inv[:, None]).astype(np.float32)
    cos, sin = np.cos(ang), np.sin(ang)
    C = np.concatenate([np.ones((LAT, S), np.float32), cos, cos])
    N = np.concatenate([np.zeros((LAT, S), np.float32), -sin, sin])
    scale = np.float32(-1.0) / np.sqrt(HD + HD).astype(np.float32)
    return np.stack([C * scale, N * scale, C, N], axis=1).astype(np.float32)


def head_slots(v):
    out = np.zeros((4, SLOT, 4, v.shape[1]), np.float32)
    out[:, :DH] = v.reshape(4, 4, DH, -1).transpose(1, 2, 0, 3)
    return out.reshape(P, 4, -1)


def kernel(**inputs):
    import concourse.bacc as _bacc
    from concourse.bass_utils import run_bass_kernel_spmd as _run

    nc = _bacc.Bacc("TRN2", target_bir_lowering=False, num_devices=1)
    arrays, args = {}, {}
    given = dict(inputs)
    given["rope_tables"] = rope_tables()
    rows_first = lambda v: v.reshape(DK, P, -1).transpose(1, 0, 2)
    width_first = lambda v: np.transpose(np.reshape(v, (-1, DK, P)), (2, 1, 0))
    heads_T = lambda v: np.transpose(np.reshape(v, (v.shape[0], H, -1)), (2, 1, 0))
    given["ctx_T"] = width_first(np.asarray(inputs["ctx_1024"]))
    given["seg_T"] = np.asarray(inputs["itok_BxS_0_511"]).reshape(NT, P).T
    for name in ("w_q_up", "w_k_up", "w_v_up"):
        given[f"L0_xattn_{name}_T"] = heads_T(np.asarray(inputs[f"L0_xattn_{name}"]))
    given["ctx_rows"] = np.asarray(inputs["ctx_1024"]).reshape(NT, P, D).transpose(1, 0, 2)
    given["L1_xattn_W_l_T"] = np.asarray(inputs["L1_xattn_W_l"]).T.reshape(4, DK, P, D).transpose(2, 0, 1, 3)
    given["L1_xattn_vecs"] = np.stack([np.asarray(inputs["L1_xattn_" + n]).reshape(DK, P).T
                                       for n in ("w_cq", "w_c", "w_q")], axis=1)
    given["L1_ffn_Wg_cols"] = rows_first(np.asarray(inputs["L1_ffn_Wg"]))
    given["L1_ffn_Wo_slots"] = head_slots(np.asarray(inputs["L1_ffn_Wo"]))
    A2 = {k: np.asarray(inputs["L2_xattn_" + k]) for k in ("Wq", "Wk", "Wv", "bq", "bk", "bv")}
    for n in "qk":
        given[f"L2_xattn_W{n}T"] = A2["W" + n].reshape(D, HID).T
        given[f"L2_xattn_W{n}_rows"] = rows_first(A2["W" + n].reshape(D, HID))
        given[f"L2_xattn_b{n}_rows"] = rows_first(np.repeat(A2["b" + n], DH, axis=0))
    slots = np.zeros((HID, H, P), np.float32)
    for h in range(H):
        slots[:, h, SLOT * (h % 4):SLOT * (h % 4) + DH] = A2["Wv"][h].T
    given["L2_xattn_Wv_slots"] = slots
    given["L2_xattn_bvT"] = A2["bv"].T
    for n in "qkv":
        given[f"L3_xattn_W{n}_T"] = rows_first(np.asarray(inputs[f"L3_xattn_W{n}"]).T)
    for n in "qk":
        given[f"L3_xattn_b{n}_cols"] = np.asarray(inputs[f"L3_xattn_b{n}"]).reshape(DK, P).T
    given["L3_xattn_Wo_slots"] = head_slots(np.asarray(inputs["L3_xattn_Wo"]).T)
    given["L3_ffn_W1_T"] = rows_first(np.asarray(inputs["L3_ffn_W1"]).T)
    given["L3_ffn_W2_T"] = np.asarray(inputs["L3_ffn_W2"]).T.reshape(FF3 // P, P, D).transpose(1, 0, 2)
    given["L3_ffn_b1_cols"] = np.asarray(inputs["L3_ffn_b1"]).reshape(FF3 // P, P).T
    p = np.arange(P)
    given["const_blocks"] = (p[:, None] // DH == p[None, :] // DH).astype(np.float32)
    given["const_heads"] = rows_first((np.arange(D)[:, None] // DH == np.arange(H)[None, :]).astype(np.float32))
    given["const_sum_rows"] = (p[:, None] == p[None, :] // SLOT * SLOT + DH).astype(np.float32)
    given["const_later"] = (p[None, :] > p[:, None]).astype(np.float32)
    given["const_numbers"] = np.broadcast_to(np.arange(E, dtype=np.float32), (P, NT, E))
    given["const_tile_numbers"] = np.broadcast_to(np.arange(SLOT_TILES, dtype=np.float32)[:, None],
                                                  (P, SLOT_TILES, E))
    given["L2_ffn_router_T"] = rows_first(np.asarray(inputs["L2_ffn_router_w"]).T)
    given["const_earlier"] = (p[None, :] < p[:, None]).astype(np.float32)
    for name, value in given.items():
        v = np.ascontiguousarray(value)
        if v.ndim == 0:
            v = v.reshape(1)
        arrays[f"in_{name}_dram"] = v
        args[name] = nc.dram_tensor(f"in_{name}_dram", v.shape, mybir.dt.from_np(v.dtype), kind="ExternalInput").ap()
    out = nc.dram_tensor("out_0_dram", (B, S, D), F32, kind="ExternalOutput").ap()
    build(nc, args, out)
    r = _run(nc, [arrays], core_ids=[0])
    return r.results[0]["out_0_dram"]
```

```python
from contextlib import ExitStack

import numpy as np
import concourse.bass as bass
from concourse import mybir

F32 = mybir.dt.float32
BF16 = mybir.dt.bfloat16
I32 = mybir.dt.int32
U32 = mybir.dt.uint32
ALU = mybir.AluOpType
ACT = mybir.ActivationFunctionType
X_AXIS = mybir.AxisListType.X

P = 128
B, S, D = 4, 512, 256
T = B * S
NT = T // P
QT_B = S // P
DK = D // P
H = 16
EPS = 1e-5
F32_MIN = float(np.finfo(np.float32).min)


class Tally:

    def __init__(self, sem):
        self.sem = sem
        self.n = 0

    def mark(self, ins):
        ins.then_inc(self.sem, 1)
        self.n += 1
        return self.n


class Core:

    def __init__(self, nc, ctx):
        self.nc = nc
        self.ctx = ctx
        self.stage_sems = []
        self.soft_sems = {k: ctx.enter_context(nc.semaphore(k)) for n in ("f0", "f2") for k in (
            n + "_d_sent", *(f"{n}_c_got{t}" for t in range(4)))}
        self.soft_sems.update({k: ctx.enter_context(nc.semaphore(k)) for k in (f"a0_near{b}" for b in range(B))})
        self.X = self.sb(ctx, "resid", [P, NT, D])
        self.XN = self.XNT = None
        self.ident = self.sb(ctx, "ident", [P, P])
        self.ones = self.sb(ctx, "ones", [P, P])
        self.tg = self.sb(ctx, "tanh_gates", [P, 8])
        self.zeros = self.sb(ctx, "zeros", [P, D])
        self.xs_cleared = ctx.enter_context(nc.semaphore("xs_cleared"))
        self.PS = ctx.enter_context(nc.psum_tensor("PS", [P, 8, 512], F32))

    def sb(self, ctx, name, shape, dt=F32):
        return ctx.enter_context(self.nc.sbuf_tensor(name, shape, dt))

    def sem(self, name):
        held = self.nc.semaphore(name)
        s = held.__enter__()
        self.stage_sems.append((held, s))
        return s

    def end_stage(self):
        with self.nc.Block() as block:
            @block.gpsimd
            def _(pool):
                for _, s in self.stage_sems:
                    pool.sem_clear(s)
        for held, _ in reversed(self.stage_sems):
            held.__exit__(None, None, None)
        self.stage_sems = []


def prologue(c, x, g_xattn, g_ffn):
    loaded, gates_in, built = c.sem("x_loaded"), c.sem("gates_loaded"), c.sem("ident_built")
    with c.nc.Block() as block:
        @block.sync
        def _(sp):
            sp.dma_start(c.tg[:, 0:4], g_xattn.partition_broadcast(P)).then_inc(gates_in, 16)
            sp.dma_start(c.tg[:, 4:8], g_ffn.partition_broadcast(P)).then_inc(gates_in, 16)
            sp.dma_start(c.X[:, :, :], x.rearrange("b (t p) d -> p (b t) d", p=P)).then_inc(loaded, 16)
            sp.wait_ge(loaded, 16)

        @block.gpsimd
        def _(pool):
            pool.memset(c.ident[:, :], 0.0).then_inc(built, 1)
            pool.memset(c.ones[:, :], 1.0).then_inc(built, 1)
            pool.memset(c.zeros[:, :], 0.0)
            pool.wait_ge(built, 2)
            pool.affine_select(out=c.ident[:, :], in_=c.ident[:, :], compare_op=ALU.not_equal, fill=1.0,
                               base=0, pattern=[[-1, P]], channel_multiplier=1).then_inc(built, 1)

        @block.scalar
        def _(act):
            act.wait_ge(gates_in, 32)
            act.activation(c.tg[:, :], c.tg[:, :], ACT.Tanh)


def layernorm(c, scope, name, keep_rows=False, pool_work=None, sync_work=None, placed=False):
    if not placed:
        c.XNT = c.sb(scope, name + "_XNT", [P, DK, T])
    with ExitStack() as own:
        if not (placed and keep_rows):
            c.XN = c.sb(scope if keep_rows else own, name + "_XN", [P, NT, D])
        normalise(c, name, c.X, c.XN, pool_work=pool_work, sync_work=sync_work, turned_into=c.XNT)


def normalise(c, name, src, dst, affine=None, pool_work=None, sync_work=None, turned_into=None):
    nc = c.nc
    with ExitStack() as ctx:
        stats = c.sb(ctx, name + "_stats", [P, NT, 6])
        mv = c.sb(ctx, name + "_mv", [P, NT, 2])
        std = c.sb(ctx, name + "_std", [P, NT])
        rstd = c.sb(ctx, name + "_rstd", [P, NT])
        step = Tally(c.sem(name + "_dve"))
        root = c.sem(name + "_root")
        turned = c.sem(name + "_turned") if turned_into is not None else None
        with nc.Block() as block:
            var_ready, tile_ready = [0], [0]

            @block.vector
            def _(dve):
                for t in range(NT):
                    step.mark(dve.bn_stats(stats[:, t, :], src[:, t, :]))
                for t in range(NT):
                    dve.wait_ge(step.sem, t + 1)
                    step.mark(dve.bn_aggr(mv[:, t, :], stats[:, t, :]))
                dve.wait_ge(step.sem, step.n)
                var_ready[0] = step.mark(dve.tensor_scalar(std[:, :], mv[:, :, 1], EPS, None, ALU.add))
                dve.wait_ge(root, 1)
                dve.wait_ge(step.sem, var_ready[0])
                r = step.mark(dve.reciprocal(rstd[:, :], std[:, :]))
                dve.wait_ge(step.sem, r)
                if affine:
                    w, b = affine
                    for t in range(NT):
                        step.mark(dve.scalar_tensor_tensor(out=dst[:, t, :], in0=src[:, t, :], scalar=mv[:, t, 0:1],
                                                           in1=w[:, :], op0=ALU.subtract, op1=ALU.mult))
                    tile_ready[0] = step.n
                    for t in range(NT):
                        dve.wait_ge(step.sem, r + t + 1)
                        step.mark(dve.scalar_tensor_tensor(out=dst[:, t, :], in0=dst[:, t, :],
                                                           scalar=rstd[:, t:t + 1], in1=b[:, :], op0=ALU.mult,
                                                           op1=ALU.add))
                else:
                    tile_ready[0] = step.n
                    for t in range(NT):
                        step.mark(dve.tensor_scalar(dst[:, t, :], src[:, t, :], mv[:, t, 0:1], rstd[:, t:t + 1],
                                                    ALU.subtract, ALU.mult))

            if sync_work:
                @block.sync
                def _(sp):
                    sync_work(sp)

            if pool_work:
                @block.gpsimd
                def _(pool):
                    pool_work(pool)

            @block.scalar
            def _(act):
                act.wait_ge(step.sem, var_ready[0])
                act.activation(std[:, :], std[:, :], ACT.Sqrt).then_inc(root, 1)
                if turned_into is not None:
                    for i in range(NT // 2):
                        act.wait_ge(turned, i + 1)
                        act.copy(turned_into[:, :, 2 * i * P:2 * (i + 1) * P],
                                 c.PS[:, i, :].rearrange("p (k q) -> p k q", k=DK))

            if turned_into is not None:
                @block.tensor
                def _(pe):
                    for i in range(NT // 2):
                        pe.wait_ge(step.sem, tile_ready[0] + 2 * i + 2)
                        bank = c.PS[:, i, :].rearrange("p (k q) -> p k q", k=DK)
                        for t in range(2):
                            for k in range(DK):
                                last = pe.transpose(bank[:, k, t * P:(t + 1) * P],
                                                    dst[:, 2 * i + t, k * P:(k + 1) * P], c.ident[:, :])
                        last.then_inc(turned, 1)


def add_scaled(eng, c, gate, tile_ap, delta):
    return eng.scalar_tensor_tensor(out=tile_ap, in0=delta, scalar=c.tg[:, gate:gate + 1], in1=tile_ap,
                                    op0=ALU.mult, op1=ALU.add)


class Attention:

    def __init__(self, c, ctx, name, nk, masked, q_tiles=QT_B, ring=4, lag=0):
        self.RING, self.lag = ring, lag
        self.c, self.name, self.nk, self.masked, self.q_tiles = c, name, nk, masked, q_tiles
        self.kt = nk // P
        self.probs = c.sb(ctx, name + "_probs", [P, self.RING, nk])
        self.probsT = c.sb(ctx, name + "_probsT", [P, 8, self.kt, P])
        self.neg_max = c.sb(ctx, name + "_negmax", [P, 8])
        self.heads = c.sb(ctx, name + "_heads", [P, 2, 4, P])
        self.total = c.sb(ctx, name + "_total", [P, 2, H])
        self.over = c.sb(ctx, name + "_over", [P, H, SLOT])
        names = ["scores", "neg_max", "probs", "turned", "copied_a", "copied_d", "heads", "heads_out",
                 "rsum", "spread", "sums", "normed", "projected", "added"]
        self.s = {k: c.sem(name + "_" + k) for k in names}

    def clear(self):
        with self.c.nc.Block() as block:
            @block.gpsimd
            def _(pool):
                for s in self.s.values():
                    pool.sem_clear(s)

    def run(self, scores, mask, values, w_out, bias_row, emit):
        c, s, kt = self.c, self.s, self.kt
        PS = c.PS
        n_heads = self.q_tiles * H
        units = n_heads // 4

        def PT(n):
            return PS[:, 4 + n % 2, 0:self.nk].rearrange("p (k q) -> p k q", k=kt)

        tail = 16 + self.lag
        with c.nc.Block() as block:
            @block.tensor
            def _(pe):
                def score(n):
                    if n >= 4:
                        pe.wait_ge(s["neg_max"], n - 3)
                        if not self.masked:
                            pe.wait_ge(s["probs"], n - 3)
                    parts = scores(n // H, n % H)
                    for cols, lhsT, rhs in parts:
                        last = pe.matmul(PS[:, n % 4, cols], lhsT, rhs, start=True, stop=True)
                    last.then_inc(s["scores"], 1)

                def turn(n):
                    pe.wait_ge(s["probs"], n + 1)
                    if n >= 2:
                        pe.wait_ge(s["copied_a"] if n % 2 == 0 else s["copied_d"], n // 2)
                    for k in range(kt):
                        last = pe.transpose(PT(n)[:, k, :], self.probs[:, n % self.RING, k * P:(k + 1) * P],
                                            c.ident[:, :])
                    last.then_inc(s["turned"], 1)

                def attend(u):
                    pe.wait_ge(s["copied_a"], 2 * u + 2)
                    pe.wait_ge(s["copied_d"], 2 * u + 2)
                    if u >= 1:
                        pe.wait_ge(s["heads_out"], u)
                    base = 4 * (u % 2)
                    for k in range(kt):
                        for j in range(4):
                            last = pe.matmul(PS[32 * j:32 * j + 32, 6, 0:P], values(u // 4, 4 * (u % 4) + j, k),
                                             self.probsT[:, base + j, k, :], start=(k == 0), stop=(k == kt - 1))
                    last.then_inc(s["heads"], 1)

                def sums(qt):
                    pe.wait_ge(s["spread"], qt + 1)
                    if qt >= 1:
                        pe.wait_ge(s["added"], qt)
                    for g in range(4):
                        last = pe.transpose(PS[:, 7, g * P:(g + 1) * P],
                                            self.over[:, 4 * g:4 * g + 4, :].rearrange("p h d -> p (h d)"),
                                            c.ident[:, :])
                    last.then_inc(s["sums"], 1)

                def project(qt):
                    pe.wait_ge(s["normed"], qt + 1)
                    groups = 4
                    for g in range(groups):
                        last = pe.matmul(PS[:, 7, 0:D], self.heads[:, qt % 2, g, :], w_out[:, g, :], start=(g == 0),
                                         stop=(g == groups - 1 and bias_row is None))
                    if bias_row is not None:
                        last = pe.matmul(PS[:, 7, 0:D], c.ones[0:1, :], bias_row, start=False, stop=True)
                    last.then_inc(s["projected"], 1)

                for n in range(4):
                    score(n)
                for i in range(n_heads + tail):
                    n = i - self.lag
                    if self.lag and i + 4 < n_heads:
                        score(i + 4)
                    if 0 <= n < n_heads:
                        turn(n)
                    if not self.lag and i + 4 < n_heads:
                        score(i + 4)
                    if n % 4 == 3 and 0 <= n // 4 - 1 < units:
                        attend(n // 4 - 1)
                    if n % 16 == 8 and 0 <= n // 16 - 1 < self.q_tiles:
                        sums(n // 16 - 1)
                    if n % 16 == 13 and 0 <= n // 16 - 1 < self.q_tiles:
                        project(n // 16 - 1)

            @block.vector
            def _(dve):
                def row_max(n):
                    dve.wait_ge(s["scores"], n + 1)
                    if n >= 8:
                        dve.wait_ge(s["probs"], n - 7)
                    if self.masked:
                        if n >= self.RING:
                            dve.wait_ge(s["turned"], n - self.RING + 1)
                        dve.tensor_tensor_reduce(self.probs[:, n % self.RING, :], PS[:, n % 4, 0:self.nk],
                                                 mask(n // H), 1.0, -F32_MIN, ALU.add, ALU.min,
                                                 self.neg_max[:, n % 8:n % 8 + 1]).then_inc(s["neg_max"], 1)
                    else:
                        dve.tensor_reduce(self.neg_max[:, n % 8:n % 8 + 1], PS[:, n % 4, 0:self.nk], X_AXIS,
                                          ALU.min).then_inc(s["neg_max"], 1)

                def copy_turned(n):
                    dve.wait_ge(s["turned"], n + 1)
                    if n >= 8:
                        dve.wait_ge(s["heads"], n // 4 - 1)
                    dve.tensor_copy(self.probsT[:, n % 8, :, :], PT(n)).then_inc(s["copied_d"], 1)

                for i in range(n_heads + tail):
                    n = i - self.lag
                    if i < n_heads:
                        row_max(i)
                    if 0 <= n - 3 < n_heads and (n - 3) % 2 == 1:
                        copy_turned(n - 3)
                    if n % 16 == 1 and 0 <= n // 16 - 1 < self.q_tiles:
                        qt = n // 16 - 1
                        dve.wait_ge(s["probs"], H * (qt + 1))
                        dve.reciprocal(self.total[:, qt % 2, :], self.total[:, qt % 2, :]).then_inc(s["rsum"], 1)
                    if n % 16 == 10 and 0 <= n // 16 - 1 < self.q_tiles:
                        qt = n // 16 - 1
                        dve.wait_ge(s["sums"], qt + 1)
                        dve.wait_ge(s["heads_out"], 4 * qt + 4)
                        h2 = self.heads[:, qt % 2, :, :].rearrange("p g q -> p (g q)")
                        dve.tensor_tensor(h2, h2, PS[:, 7, :], ALU.mult).then_inc(s["normed"], 1)
                    if n % 16 == 15 and 0 <= n // 16 - 1 < self.q_tiles:
                        qt = n // 16 - 1
                        dve.wait_ge(s["projected"], qt + 1)
                        emit(dve, qt, PS[:, 7, 0:D]).then_inc(s["added"], 1)

            @block.scalar
            def _(act):
                def exponent(n):
                    act.wait_ge(s["neg_max"], n + 1)
                    if n >= 2 * H and n % H == 0:
                        act.wait_ge(s["spread"], n // H - 1)
                    if not self.masked and n >= self.RING:
                        act.wait_ge(s["turned"], n - self.RING + 1)
                    src = self.probs[:, n % self.RING, :] if self.masked else PS[:, n % 4, 0:self.nk]
                    act.activation(self.probs[:, n % self.RING, :], src, ACT.Exp, scale=-1.0,
                                   bias=self.neg_max[:, n % 8:n % 8 + 1],
                                   accum_out=self.total[:, n // H % 2, n % H:n % H + 1]).then_inc(s["probs"], 1)

                def copy_turned(n):
                    act.wait_ge(s["turned"], n + 1)
                    if n >= 8:
                        act.wait_ge(s["heads"], n // 4 - 1)
                    act.copy(self.probsT[:, n % 8, :, :], PT(n)).then_inc(s["copied_a"], 1)

                for i in range(n_heads + tail):
                    n = i - self.lag
                    if i < n_heads:
                        exponent(i)
                    if 0 <= n - 2 < n_heads and (n - 2) % 2 == 0:
                        copy_turned(n - 2)
                    if n % 4 == 1 and 0 <= n // 4 - 2 < units:
                        u = n // 4 - 2
                        act.wait_ge(s["heads"], u + 1)
                        if u >= 8 and u % 4 == 0:
                            act.wait_ge(s["projected"], u // 4 - 1)
                        act.copy(self.heads[:, u // 4 % 2, u % 4, :], PS[:, 6, 0:P]).then_inc(s["heads_out"], 1)

            @block.gpsimd
            def _(pool):
                for qt in range(self.q_tiles):
                    pool.wait_ge(s["rsum"], qt + 1)
                    if qt >= 1:
                        pool.wait_ge(s["sums"], qt)
                    pool.tensor_copy(self.over[:, :, :],
                                     self.total[:, qt % 2, :].unsqueeze(2).to_broadcast([P, H, SLOT]))\
                        .then_inc(s["spread"], 1)


def project_columns(c, name, jobs, sync_work=None):
    made, out_a, out_d = c.sem(name + "_made"), c.sem(name + "_out_a"), c.sem(name + "_out_d")
    with c.nc.Block() as block:
        if sync_work:
            @block.sync
            def _(sp):
                sync_work(sp)

        @block.tensor
        def _(pe):
            for i, (view, steps, _) in enumerate(jobs):
                if i >= 8:
                    pe.wait_ge(out_a if i % 2 == 0 else out_d, i // 2 - 3)
                for n, (lhsT, rhs) in enumerate(steps):
                    last = pe.matmul(view(c.PS[:, i % 8, :]), lhsT, rhs, start=(n == 0), stop=(n == len(steps) - 1))
                last.then_inc(made, 1)

        @block.scalar
        def _(act):
            for i in range(0, len(jobs), 2):
                view, _, dst = jobs[i]
                act.wait_ge(made, i + 1)
                act.copy(dst, view(c.PS[:, i % 8, :])).then_inc(out_a, 1)

        @block.vector
        def _(dve):
            for i in range(1, len(jobs), 2):
                view, _, dst = jobs[i]
                dve.wait_ge(made, i + 1)
                dve.tensor_copy(dst, view(c.PS[:, i % 8, :])).then_inc(out_d, 1)


def columns(parts, n, first=0):
    return lambda bank: bank[first:first + parts, 0:n]


def start_loads(c, name, pairs):
    sems, shares = (c.sem(name + "_in_sp"), c.sem(name + "_in_act")), (pairs[0::2], pairs[1::2])
    with c.nc.Block() as block:
        for get, sem, mine in zip((block.sync, block.scalar), sems, shares):
            @get
            def _(eng, sem=sem, mine=mine):
                for dst, src in mine:
                    eng.dma_start(dst, src).then_inc(sem, 16)
    return [(sem, 16 * len(mine)) for sem, mine in zip(sems, shares) if mine]


def finish_loads(c, *loads):
    with c.nc.Block() as block:
        @block.sync
        def _(sp):
            for load in loads:
                for sem, count in load:
                    sp.wait_ge(sem, count)


def load_all(c, name, pairs):
    in_sp, in_act = c.sem(name + "_in_sp"), c.sem(name + "_in_act")
    with c.nc.Block() as block:
        for get, sem, mine in ((block.sync, in_sp, pairs[0::2]), (block.scalar, in_act, pairs[1::2])):
            @get
            def _(eng, sem=sem, mine=mine):
                for dst, src in mine:
                    eng.dma_start(dst, src).then_inc(sem, 16)
                if mine:
                    eng.wait_ge(sem, 16 * len(mine))



LAT, QLAT, HD = 64, 96, 64
NEAR = 3
MEAN_ROW = S + NEAR - 1
TABLE_ROWS = MEAN_ROW + 1


def layer0_attention(c, ctx_T, seg, w, rope, table, xs):
    nc = c.nc
    half = HD // 2
    with ExitStack() as ctx:
        sb = lambda n, shape, dt=F32: c.sb(ctx, "a0_" + n, shape, dt)
        QW = sb("QW", [QLAT, H, P])
        WVO = sb("WVO", [P, H // 2, D])
        near = sb("near", [P, NT, NEAR, P])
        qcT = sb("qcT", [QLAT, T])
        rot = sb("rotations", [P, QT_B, 2, HD])
        penalty = sb("penalty", [P, NT, NEAR])
        place = sb("place", [P, NT], I32)
        gathered = [c.soft_sems[f"a0_near{b}"] for b in range(B)]
        chunk = lambda b: slice(b * S, (b + 1) * S)
        rows = table.rearrange("(b r) (j n) -> b r j n", b=B, j=NEAR)
        with ExitStack() as early:
            tb = lambda n, shape, dt=F32: c.sb(early, "a0_" + n, shape, dt)
            keys = tb("keys", [P, NT, P])
            kcT = tb("kcT", [LAT, T])
            mean, zeros = tb("mean", [B, P]), tb("zeros", [B, 2, P])
            KW = tb("KW", [LAT, P])
            even = tb("even", [P, B, B])
            segs = tb("segs", [P, NT], I32)
            f, inside, low = tb("seg_f", [P, NT]), tb("inside", [P, NEAR + 1, NT]), tb("above", [P, NEAR + 1, NT])
            wkc, wqd = tb("wkc", [P, DK, LAT]), tb("wqd", [P, DK, QLAT])
            wqr, wkr = tb("wqr", [QLAT, H, HD]), tb("wkr", [LAT, HD])
            wo = tb("wo", [HD, H, D])
            wquT, wkuT, wvuT = tb("wquT", [HD, H, QLAT]), tb("wkuT", [HD, H, LAT]), tb("wvuT", [HD, H, LAT])
            swapped = tb("swapped", [P, QT_B, HD])
            with ExitStack() as first:
                ctxT = c.sb(first, "a0_ctxT", [P, DK, T])
                load_all(c, "a0", [
                    (ctxT[:, 0, :], ctx_T[:, 0, :]), (ctxT[:, 1, :], ctx_T[:, 1, :]),
                    (wkc[:, :, :], w["w_kv_comp"].rearrange("(k p) n -> p k n", p=P)),
                    (wqd[:, :, :], w["w_q_down"].rearrange("(k p) n -> p k n", p=P)),
                    (wqr[:, :, :], w["w_q_rope"].rearrange("c (h e) -> c h e", h=H)),
                    (wkr[:, :], w["w_k_rope"]),
                    (wquT[:, :, :], w["w_q_up_T"]), (wkuT[:, :, :], w["w_k_up_T"]), (wvuT[:, :, :], w["w_v_up_T"]),
                    (wo[:, :, :], w["w_out"].rearrange("(h e) n -> e h n", h=H)),
                    (rot[:, :, :, :], rope), (segs[:, :], seg),
                ])
                absorbed, v, filled = c.sem("a0_absorbed"), Tally(c.sem("a0_dve")), c.sem("a0_filled")
                with nc.Block() as block:
                    @block.tensor
                    def _(pe):
                        for h in range(H):
                            mm = pe.matmul(c.PS[0:QLAT, h // 8, (h % 8) * LAT:(h % 8 + 1) * LAT], wquT[:, h, :],
                                           wkuT[:, h, :], start=True, stop=True)
                        mm.then_inc(absorbed, 1)
                        for h in range(H):
                            r = 64 * (h % 2)
                            mm = pe.matmul(c.PS[r:r + 64, 2 + h // 4, D * (h // 2 % 2):D * (h // 2 % 2 + 1)],
                                           wvuT[:, h, :], wo[:, h, :], start=True, stop=True)
                        mm.then_inc(absorbed, 1)

                    @block.gpsimd
                    def _(pool):
                        pool.tensor_copy(KW[:, 0:LAT], c.ident[0:LAT, 0:LAT])
                        pool.tensor_copy(KW[:, LAT:P], wkr[:, :])
                        pool.memset(even[:, :, :], 0.0).then_inc(filled, 1)
                        pool.wait_ge(filled, 1)
                        for b in range(B):
                            pool.memset(even[:, b, b:b + 1], 1.0 / S)
                        pool.memset(zeros[:, :, :], 0.0)
                        pool.tensor_copy(QW[:, :, LAT:P], wqr[:, :, :])

                    @block.vector
                    def _(dve):
                        def then(ins):
                            dve.wait_ge(v.sem, v.mark(ins))
                        then(dve.tensor_copy(f[:, :], segs[:, :]))
                        for j in range(NEAR + 1):
                            first_seen, last_seen = (float(j), float(S - 1 + j)) if j < NEAR else (0.0, float(S + 1))
                            then(dve.tensor_scalar(low[:, j, :], f[:, :], first_seen, None, ALU.is_ge))
                            then(dve.scalar_tensor_tensor(out=inside[:, j, :], in0=f[:, :], scalar=last_seen,
                                                          in1=low[:, j, :], op0=ALU.is_le, op1=ALU.mult))
                            if j < NEAR:
                                then(dve.tensor_scalar(penalty[:, :, j], inside[:, j, :], -1.0, -F32_MIN, ALU.add,
                                                       ALU.mult))
                        then(dve.scalar_tensor_tensor(out=f[:, :], in0=f[:, :], scalar=-float(MEAN_ROW),
                                                      in1=inside[:, NEAR, :], op0=ALU.add, op1=ALU.mult))
                        for b in range(B):
                            dve.tensor_scalar(low[:, 0, b * QT_B:(b + 1) * QT_B], f[:, b * QT_B:(b + 1) * QT_B],
                                              float(MEAN_ROW + b * TABLE_ROWS), None, ALU.add).then_inc(v.sem, 1)
                            v.n += 1
                        dve.wait_ge(v.sem, v.n)
                        dve.tensor_copy(place[:, :], low[:, 0, :])
                        dve.wait_ge(absorbed, 1)
                        for i in range(2):
                            dve.tensor_copy(QW[:, 8 * i:8 * i + 8, 0:LAT],
                                            c.PS[0:QLAT, i, :].rearrange("p (h n) -> p h n", h=8))

                    @block.scalar
                    def _(act):
                        act.wait_ge(absorbed, 2)
                        for i in range(4):
                            act.copy(WVO[:, 2 * i:2 * i + 2, :], c.PS[:, 2 + i, :].rearrange("p (h n) -> p h n", h=2))
                project_columns(c, "a0_comp", [
                    (columns(LAT, S), [(wkc[:, k, :], ctxT[:, k, chunk(b)]) for k in range(DK)], kcT[:, chunk(b)])
                    for b in range(B)])
            made, copied, turned = c.sem("a0_k_made"), c.sem("a0_k_copied"), Tally(c.sem("a0_k_turned"))
            meaned, mean_out = c.sem("a0_k_meaned"), c.sem("a0_k_mean_out")
            written, done = c.sem("a0_table_written"), [0] * B
            with nc.Block() as block:
                @block.tensor
                def _(pe):
                    for b in range(B):
                        for t in range(QT_B):
                            mm = pe.matmul(c.PS[:, b, t * P:(t + 1) * P],
                                           kcT[:, b * S + t * P:b * S + (t + 1) * P], KW[:, :], start=True, stop=True)
                        mm.then_inc(made, 1)
                    pe.wait_ge(copied, B)
                    pe.wait_ge(turned.sem, 4 * B)
                    for t in range(NT):
                        mm = pe.matmul(c.PS[0:B, 4, 0:P], even[:, t // QT_B, :], keys[:, t, :], start=(t == 0),
                                       stop=(t == NT - 1))
                    mm.then_inc(meaned, 1)

                @block.vector
                def _(dve):
                    for b in range(B):
                        raw = c.PS[:, b, :].rearrange("p (t n) -> p t n", t=QT_B)
                        dst = keys[:, b * QT_B:(b + 1) * QT_B, LAT:P]
                        dve.wait_ge(made, b + 1)
                        if b >= 1:
                            dve.wait_ge(turned.sem, turned.n)
                        turned.mark(dve.tensor_tensor(dst, raw[:, :, LAT:P], rot[:, :, 0, :], ALU.mult))
                        turned.mark(dve.tensor_tensor(swapped[:, :, 0:half], raw[:, :, LAT + half:P],
                                                      rot[:, :, 1, 0:half], ALU.mult))
                        turned.mark(dve.tensor_tensor(swapped[:, :, half:HD], raw[:, :, LAT:LAT + half],
                                                      rot[:, :, 1, half:HD], ALU.mult))
                        dve.wait_ge(turned.sem, turned.n)
                        done[b] = turned.mark(dve.tensor_tensor(dst, dst, swapped[:, :, :], ALU.add))

                @block.scalar
                def _(act):
                    for b in range(B):
                        act.wait_ge(turned.sem, 4 * b + 3)
                        act.copy(keys[:, b * QT_B:(b + 1) * QT_B, 0:LAT],
                                 c.PS[:, b, :].rearrange("p (t n) -> p t n", t=QT_B)[:, :, 0:LAT])\
                            .then_inc(copied, 1)
                    act.wait_ge(meaned, 1)
                    act.copy(mean[:, :], c.PS[0:B, 4, 0:P]).then_inc(mean_out, 1)

                @block.sync
                def _(sp):
                    for dst, n in ((rows[:, 0, 1:3, :], 2), (rows[:, 1, 2:3, :], 1), (rows[:, S, 0:1, :], 1),
                                   (rows[:, S + 1, 0:2, :], 2)):
                        sp.dma_start(dst, zeros[:, 0:n, :]).then_inc(written, 16)
                    for b in range(B):
                        sp.wait_ge(copied, b + 1)
                        sp.wait_ge(turned.sem, 4 * b + 4)
                        for j in range(NEAR):
                            sp.dma_start(rows[b, j:j + S, j, :].rearrange("(t p) n -> p t n", p=P),
                                         keys[:, b * QT_B:(b + 1) * QT_B, :]).then_inc(written, 16)
                    sp.wait_ge(mean_out, 1)
                    for j in range(NEAR):
                        sp.dma_start(rows[:, MEAN_ROW, j, :], mean[:, :]).then_inc(written, 16)

            def gather(pool):
                pool.wait_ge(written, 16 * (4 + (B + 1) * NEAR))
                for t in range(NT):
                    pool.indirect_dma_start(near[:, t, :, :].rearrange("p j n -> p (j n)"), None, table,
                                            bass.IndirectOffsetOnAxis(ap=place[:, t:t + 1].bitcast(U32), axis=0))\
                        .then_inc(gathered[t // QT_B], 16)
            layernorm(c, early, "a0_ln", pool_work=gather)
            project_columns(c, "a0_down", [
                (columns(QLAT, S), [(wqd[:, k, :], c.XNT[:, k, chunk(b)]) for k in range(DK)], qcT[:, chunk(b)])
                for b in range(B)])
        with ExitStack() as own:
            other = [c.sb(own, f"a0_back{i}", [P, QT_B, NEAR, HD]) for i in range(2)]
            backs = [Tally(c.sem(f"a0_back{i}")) for i in range(2)]
            with nc.Block() as block:
                for get, i in ((block.vector, 0), (block.gpsimd, 1)):
                    @get
                    def _(eng, tmp=other[i], back=backs[i], mine=(2 * i, 2 * i + 1)):
                        table_of = lambda k, lo, hi: rot[:, :, k, lo:hi].unsqueeze(2)\
                            .to_broadcast([P, QT_B, NEAR, hi - lo])
                        for b in mine:
                            key = near[:, b * QT_B:(b + 1) * QT_B, :, LAT:P]
                            eng.wait_ge(gathered[b], 16 * QT_B)
                            if back.n:
                                eng.wait_ge(back.sem, back.n)
                            back.mark(eng.tensor_tensor(tmp[:, :, :, 0:half], key[:, :, :, half:HD],
                                                        table_of(1, 0, half), ALU.mult))
                            back.mark(eng.tensor_tensor(tmp[:, :, :, half:HD], key[:, :, :, 0:half],
                                                        table_of(1, half, HD), ALU.mult))
                            eng.wait_ge(back.sem, back.n)
                            back.mark(eng.tensor_tensor(key, key, table_of(0, 0, HD), ALU.mult))
                            eng.wait_ge(back.sem, back.n)
                            back.mark(eng.tensor_tensor(key, key, tmp[:, :, :, :], ALU.subtract))
        clear_expert_rows(c, xs)
        TURN = NT // 2
        qc_turn = sb("qc_turn", [QLAT, TURN * P])
        pen_turn = sb("penalty_turn", [P, TURN, NEAR])
        near_turn = sb("near_turn", [P, TURN, NEAR, P])
        scores, probs = sb("scores", [P, 2, H, NEAR]), sb("probs", [P, 2, H, NEAR])
        top, total = sb("top", [P, 2, H]), sb("total", [P, 2, H])
        unused = sb("products", [P, 2, 4 * NEAR, P])
        terms = sb("terms", [P, 2, H, NEAR, LAT])
        att = sb("att", [P, 2, H, LAT])
        attT = sb("attT", [P, 2, H // 2, P])
        s = {k: c.sem("a0_" + k) for k in ("turn_in", "q_made", "scored", "small", "shifted", "exped", "normed",
                                           "termed", "half_added", "attended", "turned_att", "copied_att", "projected", "added")}
        groups = H // 4
        with nc.Fori(0, NT // TURN) as turn:
            with nc.Block() as block:
                @block.tensor
                def _(pe):
                    def out_of(t):
                        pe.wait_ge(s["attended"], t + 1)
                        if t >= 1:
                            pe.wait_ge(s["copied_att"], t)
                        for m in range(H // 2):
                            last = pe.transpose(c.PS[:, 4 + m // 4, (m % 4) * P:(m % 4 + 1) * P],
                                                att[:, t % 2, 2 * m:2 * m + 2, :].rearrange("p h d -> p (h d)"),
                                                c.ident[:, :])
                        last.then_inc(s["turned_att"], 1)
                        pe.wait_ge(s["copied_att"], t + 1)
                        if t >= 2:
                            pe.wait_ge(s["added"], t - 1)
                        for m in range(H // 2):
                            last = pe.matmul(c.PS[:, 6 + t % 2, 0:D], attT[:, t % 2, m, :], WVO[:, m, :],
                                             start=(m == 0), stop=(m == H // 2 - 1))
                        last.then_inc(s["projected"], 1)

                    pe.wait_ge(s["turn_in"], 1)
                    for t in range(TURN + 3):
                        if t < TURN:
                            for g in range(groups):
                                if t >= 1:
                                    pe.wait_ge(s["scored"], groups * (t - 1) + g + 1)
                                pe.matmul(c.PS[:, g, :], qc_turn[:, t * P:(t + 1) * P], QW[:, 4 * g:4 * g + 4, :],
                                          start=True, stop=True).then_inc(s["q_made"], 1)
                        if t >= 3:
                            out_of(t - 3)

                @block.scalar
                def _(act):
                    act.copy(qc_turn[:, :], qcT[:, bass.ds(turn * TURN * P, TURN * P)]).then_inc(s["turn_in"], 1)
                    act.copy(near_turn[:, :, :, :], near[:, bass.ds(turn * TURN, TURN), :, :]).then_inc(s["turn_in"], 1)
                    act.copy(pen_turn[:, :, :], penalty[:, bass.ds(turn * TURN, TURN), :]).then_inc(s["turn_in"], 1)
                    def weigh(t):
                        act.wait_ge(s["normed"], t + 1)
                        if t >= 2:
                            act.wait_ge(s["attended"], t - 1)
                        for h in range(H):
                            for j in range(NEAR):
                                last = act.activation(terms[:, t % 2, h, j, :], near_turn[:, t, j, 0:LAT], ACT.Copy,
                                                      scale=probs[:, t % 2, h, j:j + 1])
                        last.then_inc(s["termed"], 1)

                    for t in range(TURN + 3):
                        if t >= 3:
                            act.wait_ge(s["turned_att"], t - 2)
                            act.copy(attT[:, (t - 3) % 2, :, :].rearrange("p m q -> p (m q)"),
                                     c.PS[:, 4:6, :].rearrange("p k q -> p (k q)")).then_inc(s["copied_att"], 1)
                        if 1 <= t <= TURN:
                            weigh(t - 1)
                        if t < TURN:
                            act.wait_ge(s["shifted"], t + 1)
                            if t >= 2:
                                act.wait_ge(s["termed"], t - 1)
                            act.activation(probs[:, t % 2, :, :], scores[:, t % 2, :, :], ACT.Exp,
                                           scale=float(1.0 / np.sqrt(np.float32(HD + HD)))).then_inc(s["exped"], 1)

                @block.vector
                def _(dve):
                    small = Tally(s["small"])

                    def then(ins):
                        dve.wait_ge(small.sem, small.mark(ins))

                    def score(t, g):
                        n = groups * t + g
                        dve.wait_ge(s["q_made"], n + 1)
                        if n >= 2:
                            dve.wait_ge(s["scored"], n - 1)
                        for h in range(4):
                            for j in range(NEAR):
                                last = dve.tensor_tensor_reduce(
                                    unused[:, n % 2, NEAR * h + j, :], c.PS[:, g, h * P:(h + 1) * P],
                                    near_turn[:, t, j, :], 1.0, 0.0, ALU.mult, ALU.add,
                                    scores[:, t % 2, 4 * g + h, j:j + 1])
                        last.then_inc(s["scored"], 1)

                    def shift(t):
                        sc = scores[:, t % 2, :, :]
                        dve.wait_ge(s["scored"], groups * (t + 1))
                        then(dve.tensor_tensor(sc, sc, pen_turn[:, t, :].unsqueeze(1).to_broadcast([P, H, NEAR]), ALU.add))
                        then(dve.tensor_reduce(top[:, t % 2, :], sc, X_AXIS, ALU.max))
                        dve.tensor_tensor(sc, sc, top[:, t % 2, :].unsqueeze(2).to_broadcast([P, H, NEAR]),
                                          ALU.subtract).then_inc(s["shifted"], 1)

                    def normalise(t):
                        pr, tot = probs[:, t % 2, :, :], total[:, t % 2, :]
                        dve.wait_ge(s["exped"], t + 1)
                        then(dve.tensor_reduce(tot, pr, X_AXIS, ALU.add))
                        then(dve.reciprocal(tot, tot))
                        dve.tensor_tensor(pr, pr, tot.unsqueeze(2).to_broadcast([P, H, NEAR]), ALU.mult)\
                            .then_inc(s["normed"], 1)

                    dve.wait_ge(s["turn_in"], 3)
                    for t in range(TURN + 3):
                        if t < TURN:
                            for g in range(groups):
                                score(t, g)
                                if g == 0 and t >= 1:
                                    normalise(t - 1)
                            shift(t)
                        elif t == TURN:
                            normalise(t - 1)
                        if t >= 3:
                            dve.wait_ge(s["projected"], t - 2)
                            add_scaled(dve, c, 0, c.X[:, bass.ds(turn * TURN + t - 3, 1), :].rearrange("p a d -> p (a d)"),
                                       c.PS[:, 6 + (t - 3) % 2, 0:D]).then_inc(s["added"], 1)

                @block.gpsimd
                def _(pool):
                    for t in range(TURN):
                        pool.wait_ge(s["termed"], t + 1)
                        pool.tensor_tensor(terms[:, t % 2, :, 0, :], terms[:, t % 2, :, 0, :], terms[:, t % 2, :, 1, :],
                                           ALU.add).then_inc(s["half_added"], 1)
                        pool.wait_ge(s["half_added"], t + 1)
                        if t >= 2:
                            pool.wait_ge(s["turned_att"], t - 1)
                        pool.tensor_tensor(att[:, t % 2, :, :], terms[:, t % 2, :, 0, :], terms[:, t % 2, :, 2, :], ALU.add)\
                            .then_inc(s["attended"], 1)

            with nc.Block() as block:
                @block.gpsimd
                def _(pool):
                    for sm in s.values():
                        pool.sem_clear(sm)



Q_PARTS = (0, 0, 1, 1, 0, 2)
K_PARTS = (0, 1, 0, 1, 2, 0)
DH = D // H
BATCHES = 2
CAUSAL_BATCHES = 1
PACKED = 6 * DH
SLOT = 32


def split_and_pack(c, name, jobs, pack, parts_of, scratch, chunk_w, rows=P, scale=1.0, lead=None, ring=3,
                   pool_work=None):
    nc = c.nc
    nk = len(jobs[0])
    flat = [(n, k) for n in range(len(jobs)) for k in range(nk)]
    with ExitStack() as ctx:
        whole = c.sb(ctx, name + "_whole", [rows, 2, chunk_w])
        rest = c.sb(ctx, name + "_rest", [rows, 2, chunk_w])
        parts = c.sb(ctx, name + "_parts", [rows, ring, 3, chunk_w], BF16)
        s = {k: c.sem(name + "_" + k) for k in ("made", "whole", "high", "rest", "middle", "low", "packed")}
        saved = [c.sem(f"{name}_saved{i}") for i in range(ring)]
        with nc.Block() as block:
            if pool_work:
                @block.gpsimd
                def _(pool):
                    pool_work(pool)

            @block.tensor
            def _(pe):
                for i, (n, k) in enumerate(flat):
                    steps = jobs[n][k][0]
                    if steps is None:
                        continue
                    if i >= 8:
                        pe.wait_ge(s["whole"], i - 7)
                    for m, (lhsT, rhs) in enumerate(steps):
                        last = pe.matmul(c.PS[0:rows, i % 8, 0:chunk_w], lhsT, rhs, start=(m == 0),
                                         stop=(m == len(steps) - 1))
                    last.then_inc(s["made"], 1)

            @block.scalar
            def _(act):
                for i, (n, k) in enumerate(flat):
                    steps, bias, src = jobs[n][k]
                    if steps is not None:
                        act.wait_ge(s["made"], i + 1)
                        src = c.PS[0:rows, i % 8, 0:chunk_w]
                    if i >= 2:
                        act.wait_ge(s["rest"], i - 1)
                    if bias is None:
                        act.activation(whole[:, i % 2, :], src, ACT.Copy, scale=scale).then_inc(s["whole"], 1)
                    else:
                        act.activation(whole[:, i % 2, :], src, ACT.Identity, bias=bias, scale=scale)\
                           .then_inc(s["whole"], 1)
                    act.wait_ge(s["whole"], i + 1)
                    if i >= ring:
                        act.wait_ge(saved[i % ring], 16 * (i // ring))
                    act.copy(parts[:, i % ring, 0, :], whole[:, i % 2, :]).then_inc(s["high"], 1)

            @block.vector
            def _(dve):
                for i in range(len(flat)):
                    p = parts[:, i % ring, :, :]
                    dve.wait_ge(s["high"], i + 1)
                    if i >= 2:
                        dve.wait_ge(s["low"], i - 1)
                    dve.tensor_tensor(rest[:, i % 2, :], whole[:, i % 2, :], p[:, 0, :], ALU.subtract)\
                        .then_inc(s["rest"], 1)
                    dve.wait_ge(s["rest"], i + 1)
                    dve.tensor_copy(p[:, 1, :], rest[:, i % 2, :]).then_inc(s["middle"], 1)
                    dve.wait_ge(s["middle"], i + 1)
                    dve.tensor_tensor(p[:, 2, :], rest[:, i % 2, :], p[:, 1, :], ALU.subtract).then_inc(s["low"], 1)

            @block.sync
            def _(sp):
                for i, (n, k) in enumerate(flat):
                    cols = slice(n * chunk_w, (n + 1) * chunk_w)
                    sp.wait_ge(s["low"], i + 1)
                    sp.dma_start(scratch[:, k * P:k * P + rows, cols].rearrange("a r t -> r a t"),
                                 parts[:, i % ring, :, :]).then_inc(saved[i % ring], 16)
                for m in range(max(0, len(flat) - ring), len(flat)):
                    sp.wait_ge(saved[m % ring], 16 * (m // ring + 1))

        def load(sp):
            for i, (n, k) in enumerate(flat):
                cols = slice(n * chunk_w, (n + 1) * chunk_w)
                if k == nk - 1:
                    if lead is None:
                        for a, part in enumerate(parts_of):
                            sp.dma_start(pack[DH * a:DH * (a + 1), :, cols],
                                         scratch[part, 0:D, cols].rearrange("(h d) t -> d h t", d=DH))\
                              .then_inc(s["packed"], 16)
                    else:
                        sp.dma_start(pack[lead:lead + 3, :, cols], scratch[:, 0:H, cols]).then_inc(s["packed"], 16)
        return load, [(s["packed"], 16 * len(jobs) * (1 if parts_of is None else len(parts_of)))]




def layer1_attention(c, ctx_T, ctx_rows, w):
    nc = c.nc
    kt = S // P
    with ExitStack() as ctx:
        sb = lambda n, shape, dt=F32: c.sb(ctx, "a1_" + n, shape, dt)
        c.XNT, c.XN = sb("XNT", [P, DK, T]), sb("XN", [P, NT, D])
        R, rows = sb("R", [P, DK, T]), sb("rows", [P, NT, D])
        W, W14 = sb("W", [P, 4, DK, D]), sb("W14", [P, B, DK, D])
        vecs = sb("vecs", [P, 3, DK])
        biases, bl, row_term = sb("biases", [1, 3]), sb("bl", [1, D]), sb("row_term", [1, T])
        bias = sb("bias", [1, 1])
        attT, prod = sb("attT", [P, DK, T]), sb("prod", [P, DK, T])
        probs, probsT = sb("probs", [P, 2, S]), sb("probsT", [P, 2, kt, S])
        nmax, sums, rsum = sb("nmax", [P, NT]), sb("sums", [P, NT]), sb("rsum", [P, NT])
        with ExitStack() as early:
            ctxT = c.sb(early, "a1_ctxT", [P, DK, T])
            one = lambda v: v.rearrange("(a n) -> a n", a=1)
            weights = start_loads(c, "a1", [(ctxT[:, :, :], ctx_T), (rows[:, :, :], ctx_rows), (W[:, :, :, :], w["W_l_T"]),
                               (vecs[:, :, :], w["vecs"]), (bl[:, :], one(w["b_l"])),
                               (biases[:, 0:1], one(w["b_cq"])), (biases[:, 1:2], one(w["b_c"])),
                               (biases[:, 2:3], one(w["b_q"]))])
            layernorm(c, early, "a1_ln", keep_rows=True, placed=True)
            finish_loads(c, weights)
            termed, bsum = c.sem("a1_termed"), c.sem("a1_bsum")
            with nc.Block() as block:
                @block.tensor
                def _(pe):
                    for b in range(B):
                        for k in range(DK):
                            mm = pe.matmul(c.PS[0:1, b, :], vecs[:, 2, k:k + 1], ctxT[:, k, b * S:(b + 1) * S],
                                           start=(k == 0), stop=(k == DK - 1))
                        mm.then_inc(termed, 1)

                @block.vector
                def _(dve):
                    dve.reduce_sum(bias[:, :], biases[:, :], X_AXIS).then_inc(bsum, 1)
                    for k in range(DK):
                        dve.tensor_scalar(R[:, k, :], ctxT[:, k, :], vecs[:, 0, k:k + 1], vecs[:, 1, k:k + 1],
                                          ALU.mult, ALU.add)
                    dve.wait_ge(bsum, 1)
                    for b in range(B):
                        dve.wait_ge(termed, b + 1)
                        dve.tensor_scalar(row_term[:, b * S:(b + 1) * S], c.PS[0:1, b, :], bias[:, 0:1], None,
                                          ALU.add)
        s = {k: c.sem("a1_" + k) for k in ("scores", "max", "probs", "rsum", "scaled", "turned", "copied", "att",
                                           "att_out")}
        with nc.Block() as block:
            @block.tensor
            def _(pe):
                def score(t):
                    if t >= 2:
                        pe.wait_ge(s["probs"], t - 1)
                    b = t // kt
                    for k in range(DK):
                        pe.matmul(c.PS[:, t % 2, :], c.XNT[:, k, t * P:(t + 1) * P], R[:, k, b * S:(b + 1) * S],
                                  start=(k == 0), stop=False)
                    pe.matmul(c.PS[:, t % 2, :], c.ones[0:1, :], row_term[:, b * S:(b + 1) * S], start=False,
                              stop=True).then_inc(s["scores"], 1)

                def turn(t):
                    pe.wait_ge(s["scaled"], t + 1)
                    if t >= 2:
                        pe.wait_ge(s["copied"], t - 1)
                    for k in range(kt):
                        mm = pe.transpose(c.PS[:, 2 + t % 2, k * P:(k + 1) * P], probs[:, t % 2, k * P:(k + 1) * P],
                                          c.ident[:, :])
                    mm.then_inc(s["turned"], 1)

                def attend(b):
                    pe.wait_ge(s["copied"], kt * (b + 1))
                    if b >= 2:
                        pe.wait_ge(s["att_out"], b - 1)
                    for half in range(DK):
                        for k in range(kt):
                            mm = pe.matmul(c.PS[:, 4 + 2 * (b % 2) + half, :],
                                           rows[:, b * kt + k, half * P:(half + 1) * P], probsT[:, b % 2, k, :],
                                           start=(k == 0), stop=(k == kt - 1))
                    mm.then_inc(s["att"], 1)
                score(0)
                score(1)
                for t in range(NT):
                    turn(t)
                    if t + 2 < NT:
                        score(t + 2)
                    if t % kt == 1 and t >= kt:
                        attend(t // kt - 1)
                attend(B - 1)

            @block.vector
            def _(dve):
                for t in range(NT + 2):
                    if t < NT:
                        dve.wait_ge(s["scores"], t + 1)
                        dve.tensor_reduce(nmax[:, t:t + 1], c.PS[:, t % 2, :], X_AXIS, ALU.max, negate=True)\
                            .then_inc(s["max"], 1)
                    if t >= 1 and t - 1 < NT:
                        n = t - 1
                        dve.wait_ge(s["probs"], n + 1)
                        dve.reciprocal(rsum[:, n:n + 1], sums[:, n:n + 1]).then_inc(s["rsum"], 1)
                        dve.wait_ge(s["rsum"], n + 1)
                        dve.tensor_scalar(probs[:, n % 2, :], probs[:, n % 2, :], rsum[:, n:n + 1], None, ALU.mult)\
                            .then_inc(s["scaled"], 1)

            @block.gpsimd
            def _(pool):
                for b in range(B):
                    pool.wait_ge(s["att_out"], b + 1)
                    for k in range(DK):
                        cols = slice(b * S, (b + 1) * S)
                        pool.tensor_tensor(prod[:, k, cols], attT[:, k, cols], c.XNT[:, k, cols], ALU.mult)

            @block.scalar
            def _(act):
                def out(b):
                    act.wait_ge(s["att"], b + 1)
                    act.copy(attT[:, :, b * S:(b + 1) * S], c.PS[:, 4 + 2 * (b % 2):6 + 2 * (b % 2), :])\
                       .then_inc(s["att_out"], 1)
                for t in range(NT + 2):
                    if t < NT:
                        act.wait_ge(s["max"], t + 1)
                        if t >= 2:
                            act.wait_ge(s["turned"], t - 1)
                        act.activation(probs[:, t % 2, :], c.PS[:, t % 2, :], ACT.Exp, bias=nmax[:, t:t + 1],
                                       accum_out=sums[:, t:t + 1]).then_inc(s["probs"], 1)
                    if 1 <= t and t - 1 < NT:
                        n = t - 1
                        b, l = n // kt, n % kt
                        act.wait_ge(s["turned"], n + 1)
                        if b >= 2:
                            act.wait_ge(s["att"], b - 1)
                        act.copy(probsT[:, b % 2, :, l * P:(l + 1) * P],
                                 c.PS[:, 2 + n % 2, :].rearrange("p (k q) -> p k q", k=kt)).then_inc(s["copied"], 1)
                    if t >= kt + 3 and (t - 3) % kt == 0:
                        out((t - 3) // kt - 1)
                out(B - 1)
        bmin = sb("bmin", [P, B])
        e, tot, mean = sb("e", [P, NT]), sb("tot", [P, B]), sb("mean", [P, B, DK])
        v, allr, exped, meant = Tally(c.sem("a1_m_dve")), c.sem("a1_allr"), c.sem("a1_exped"), c.sem("a1_meant")
        neg, least, spread = sb("neg", [P, B]), sb("least", [B, 1]), sb("spread", [B, B])
        with nc.Block() as block:
            @block.vector
            def _(dve):
                def then(ins):
                    dve.wait_ge(v.sem, v.mark(ins))
                then(dve.tensor_reduce(bmin[:, :], nmax[:, :].rearrange("p (b t) -> p b t", b=B), X_AXIS, ALU.min))
                dve.wait_ge(allr, 1)
                then(dve.tensor_reduce(least[:, :], c.PS[0:B, 2, 0:P], X_AXIS, ALU.min))
                then(dve.tensor_scalar(spread[:, :], c.ident[0:B, 0:B], least[:, 0:1], None, ALU.mult))
                dve.wait_ge(allr, 2)
                then(dve.tensor_copy(neg[:, :], c.PS[:, 2, P:P + B]))
                dve.wait_ge(meant, 1)
                then(dve.tensor_reduce(tot[:, :], c.PS[:, 0, 0:NT].rearrange("p (b t) -> p b t", b=B), X_AXIS,
                                       ALU.add))
                then(dve.reciprocal(tot[:, :], tot[:, :]))
                for b in range(B):
                    then(dve.tensor_scalar(mean[:, b, :], c.PS[:, 1, 2 * b:2 * b + 2], tot[:, b:b + 1], None,
                                           ALU.mult))
                    for k in range(DK):
                        then(dve.scalar_tensor_tensor(out=W14[:, b, k, :], in0=W[:, 3, k, :],
                                                      scalar=mean[:, b, k:k + 1], in1=W[:, 0, k, :],
                                                      op0=ALU.mult, op1=ALU.add))

            @block.scalar
            def _(act):
                act.wait_ge(v.sem, 4)
                for b in range(B):
                    act.activation(e[:, b * kt:(b + 1) * kt], nmax[:, b * kt:(b + 1) * kt], ACT.Exp, scale=-1.0,
                                   bias=neg[:, b:b + 1]).then_inc(exped, 1)

            @block.tensor
            def _(pe):
                pe.wait_ge(v.sem, 1)
                pe.transpose(c.PS[0:B, 2, 0:P], bmin[:, :], c.ident[:, :]).then_inc(allr, 1)
                pe.wait_ge(v.sem, 3)
                pe.matmul(c.PS[:, 2, P:P + B], c.ones[0:B, :], spread[:, :], start=True, stop=True).then_inc(allr, 1)
                pe.wait_ge(exped, B)
                pe.matmul(c.PS[:, 0, 0:NT], c.ones[:, :], e[:, :], start=True, stop=True)
                for b in range(B):
                    for half in range(DK):
                        for k in range(kt):
                            t = b * kt + k
                            mm = pe.matmul(c.PS[:, 1, 2 * b + half:2 * b + half + 1],
                                           c.XN[:, t, half * P:(half + 1) * P], e[:, t:t + 1], start=(k == 0),
                                           stop=(k == kt - 1))
                mm.then_inc(meant, 1)
        out, added = c.sem("a1_out"), c.sem("a1_added")
        with nc.Block() as block:
            @block.tensor
            def _(pe):
                for t in range(NT):
                    if t >= 8:
                        pe.wait_ge(added, t - 7)
                    z, cols = c.PS[:, t % 8, 0:D], slice(t * P, (t + 1) * P)
                    for k in range(DK):
                        pe.matmul(z, c.XNT[:, k, cols], W14[:, t // kt, k, :], start=(k == 0), stop=False)
                        pe.matmul(z, attT[:, k, cols], W[:, 1, k, :], start=False, stop=False)
                        pe.matmul(z, prod[:, k, cols], W[:, 2, k, :], start=False, stop=False)
                    pe.matmul(z, c.ones[0:1, :], bl[:, :], start=False, stop=True).then_inc(out, 1)

            @block.vector
            def _(dve):
                for t in range(NT):
                    dve.wait_ge(out, t + 1)
                    add_scaled(dve, c, 1, c.X[:, t, :], c.PS[:, t % 8, 0:D]).then_inc(added, 1)



KEEP = S // 2
NK_T = B * KEEP // P


def rows_of_columns(c, name, scope, cols, out):
    wide = c.sb(scope, name + "_wide", [P, NT, P])
    spread, turned, copied = c.sem(name + "_spread"), c.sem(name + "_turned"), c.sem(name + "_copied")
    with c.nc.Block() as block:
        @block.vector
        def _(dve):
            for t in range(NT):
                dve.tensor_scalar(wide[:, t, :], c.ones[:, :], cols[:, t:t + 1], None, ALU.mult).then_inc(spread, 1)

        @block.tensor
        def _(pe):
            for t in range(NT):
                pe.wait_ge(spread, t + 1)
                mm = pe.transpose(c.PS[:, t // 4, (t % 4) * P:(t % 4 + 1) * P], wide[:, t, :], c.ident[:, :])
                if t % 4 == 3:
                    mm.then_inc(turned, 1)

        @block.scalar
        def _(act):
            for i in range(NT // 4):
                act.wait_ge(turned, i + 1)
                act.copy(out[:, 4 * i * P:4 * (i + 1) * P], c.PS[:, i, :]).then_inc(copied, 1)


def token_logits(c, name, weights, n, out):
    made = c.sem(name + "_made")
    with c.nc.Block() as block:
        @block.tensor
        def _(pe):
            for t in range(NT):
                for k in range(DK):
                    mm = pe.matmul(c.PS[:, 0, t * n:(t + 1) * n], c.XNT[:, k, t * P:(t + 1) * P], weights[:, k, :],
                                   start=(k == 0), stop=(k == DK - 1))
            mm.then_inc(made, 1)

        @block.vector
        def _(dve):
            dve.wait_ge(made, 1)
            dve.tensor_copy(out, c.PS[:, 0, 0:NT * n].rearrange("p (t n) -> p t n", t=NT))


def rank_within(c, name, scope, key_cols, key_rows, rank, spans, earlier):
    span = max(b - a for a, b in spans) * P
    part = c.sb(scope, name + "_part", [P, NT, 4])
    junk = c.sb(scope, name + "_junk", [P, 4, span], BF16)
    zeroed, step = c.sem(name + "_zeroed"), Tally(c.sem(name + "_step"))
    with c.nc.Block() as block:
        @block.vector
        def _(dve):
            def spare(w):
                if step.n >= 4:
                    dve.wait_ge(step.sem, step.n - 3)
                return junk[:, step.n % 4, 0:w]
            dve.memset(part[:, :, :], 0.0).then_inc(zeroed, 1)
            dve.wait_ge(zeroed, 1)
            for t in range(NT):
                a, b = spans[t]
                key = key_cols[:, t:t + 1]
                for i, (lo, hi, op) in enumerate(((a, t, ALU.is_ge), (t, b, ALU.is_gt))):
                    if lo < hi:
                        step.mark(dve.tensor_scalar(spare((hi - lo) * P), key_rows[:, lo * P:hi * P], key, None, op,
                                                    ALU.add, accum_out=part[:, t, i:i + 1]))
                step.mark(dve.scalar_tensor_tensor(out=spare(P), in0=key_rows[:, t * P:(t + 1) * P], scalar=key,
                                                   in1=earlier[:, :], op0=ALU.is_equal, op1=ALU.mult,
                                                   accum_out=part[:, t, 2:3]))
            dve.wait_ge(step.sem, step.n)
            dve.tensor_reduce(rank, part[:, :, :], X_AXIS, ALU.add)


def layer1_ffn(c, w, consts, scratch):
    nc = c.nc
    TK = B * KEEP
    tile = lambda t: slice(t * P, (t + 1) * P)
    with ExitStack() as ctx:
        sb = lambda n, shape, dt=F32: c.sb(ctx, "f1_" + n, shape, dt)
        WOUT, gate = sb("WOUT", [P, 4, D]), sb("gate", [P, NT])
        pickT = sb("pickT", [P, 2, T])
        QP, KP = sb("QP", [PACKED, H, TK], BF16), sb("KP", [PACKED, H, TK], BF16)
        V, Y = sb("V", [P, NK_T, D]), sb("Y", [P, NK_T, D])
        W = {n: sb("W" + n, [P, DK, D]) for n in "qkv"}
        kept = sb("kept", [P, DK, TK])
        with ExitStack() as early:
            tb = lambda n, shape, dt=F32: c.sb(early, "f1_" + n, shape, dt)
            Wg, earlier = tb("Wg", [P, DK, 1]), tb("earlier", [P, P])
            slots_i, slots = tb("slots_i", [P, KEEP], I32), tb("slots", [P, KEEP])
            rank, gate_rows, pick = tb("rank", [P, NT]), tb("gate_rows", [P, T]), tb("pick", [P, NT, KEEP])
            weights = start_loads(c, "f1", [(Wg[:, :, :], w["Wg_cols"]),
                               (WOUT[:, :, :], w["Wo_slots"]),
                               (earlier[:, :], consts["earlier"])]
                     + [(W[n][:, :, :], w["W" + n].rearrange("(k p) n -> p k n", p=P)) for n in "qkv"])
            layernorm(c, early, "f1_ln", keep_rows=True)
            finish_loads(c, weights)
            token_logits(c, "f1_gate", Wg, 1, gate[:, :].rearrange("p (t n) -> p t n", n=1))
            with nc.Block() as block:
                @block.scalar
                def _(act):
                    act.activation(gate[:, :], gate[:, :], ACT.Sigmoid)

                @block.gpsimd
                def _(pool):
                    pool.iota(slots_i[:, :], pattern=[[1, KEEP]], base=0, channel_multiplier=0)
            with ExitStack() as tmp:
                rows_of_columns(c, "f1_rows", tmp, gate, gate_rows)
                rank_within(c, "f1_rank", tmp, gate, gate_rows, rank[:, :],
                            [(t // QT_B * QT_B, t // QT_B * QT_B + QT_B) for t in range(NT)], earlier)
            ready, picked, turned, out_a, kept_made, kept_out = (c.sem("f1_" + k) for k in (
                "slots_ready", "picked", "pick_turned", "pick_out", "kept_made", "kept_out"))
            with nc.Block() as block:
                @block.vector
                def _(dve):
                    dve.tensor_copy(slots[:, :], slots_i[:, :]).then_inc(ready, 1)
                    dve.wait_ge(ready, 1)
                    for t in range(NT):
                        dve.tensor_scalar(pick[:, t, :], slots[:, :], rank[:, t:t + 1], None, ALU.is_equal)\
                            .then_inc(picked, 1)
                    for b in range(B):
                        dve.wait_ge(kept_made, b + 1)
                        dve.tensor_copy(kept[:, :, b * KEEP:(b + 1) * KEEP],
                                        c.PS[:, b, :].rearrange("p (k n) -> p k n", k=DK)).then_inc(kept_out, 1)

                @block.tensor
                def _(pe):
                    for b in range(B):
                        pe.wait_ge(picked, QT_B * (b + 1))
                        for half in range(DK):
                            for l in range(QT_B):
                                t = b * QT_B + l
                                mm = pe.matmul(c.PS[:, b, half * KEEP:(half + 1) * KEEP],
                                               c.XN[:, t, half * P:(half + 1) * P], pick[:, t, :], start=(l == 0),
                                               stop=(l == QT_B - 1))
                        mm.then_inc(kept_made, 1)
                    for i in range(NT // 2):
                        if i >= 4:
                            pe.wait_ge(out_a, i - 3)
                        for l in range(2):
                            for hf in range(2):
                                mm = pe.transpose(c.PS[:, 4 + i % 4, hf * D + l * P:hf * D + (l + 1) * P],
                                                  pick[:, 2 * i + l, hf * P:(hf + 1) * P], c.ident[:, :])
                        mm.then_inc(turned, 1)

                @block.scalar
                def _(act):
                    for i in range(NT // 2):
                        act.wait_ge(turned, i + 1)
                        act.copy(pickT[:, :, 2 * i * P:2 * (i + 1) * P],
                                 c.PS[:, 4 + i % 4, :].rearrange("p (s n) -> p s n", s=2)).then_inc(out_a, 1)
        half_chunk = lambda n: slice(n * S, (n + 1) * S)
        packs = []
        for n, pack, parts, scale in (("q", QP, Q_PARTS, -0.25), ("k", KP, K_PARTS, 1.0)):
            packs.append(split_and_pack(c, f"f1_{n}s", [[([(W[n][:, i, tile(k)], kept[:, i, half_chunk(m)]) for i in range(DK)],
                                             None, None) for k in range(DK)] for m in range(TK // S)],
                           pack, parts, scratch[n], S, scale=scale))
        project_columns(c, "f1_v", [
            (columns(P, D), [(kept[:, i, tile(t)], W["v"][:, i, :]) for i in range(DK)], V[:, t, :])
            for t in range(NK_T)], sync_work=lambda sp: [load(sp) for load, _ in packs])
        att = Attention(c, ctx, "f1_att", KEEP, False, q_tiles=BATCHES * KEEP // P)
        VB = sb("VB", [P, BATCHES * KEEP // P, H, SLOT])
        with nc.Block() as block:
            @block.gpsimd
            def _(pool):
                pool.memset(VB[:, :, :, :], 0.0)
        per = KEEP // P
        finish_loads(c, *(packed for _, packed in packs))
        with nc.Fori(0, B // BATCHES) as turn:
            with nc.Block() as block:
                @block.gpsimd
                def _(pool):
                    pool.tensor_copy(VB[:, :, :, 0:DH], V[:, bass.ds(turn * BATCHES * per, BATCHES * per), :]
                                     .rearrange("p t (h d) -> p t h d", h=H))
            first = turn * BATCHES * KEEP
            att.run(lambda qt, h: [(slice(0, KEEP), QP[:, h, bass.ds(first + qt * P, P)],
                                    KP[:, h, bass.ds(first + qt // per * KEEP, KEEP)])],
                    None, lambda qt, h, k: VB[:, qt // per * per + k, h, :], WOUT, None,
                    lambda dve, qt, delta: dve.tensor_copy(Y[:, bass.ds(turn * BATCHES * per + qt, 1), :]
                                                           .rearrange("p a d -> p (a d)"), delta))
            att.clear()
        placed, added, gated = c.sem("f1_placed"), c.sem("f1_added"), c.sem("f1_gated")
        with nc.Block() as block:
            @block.vector
            def _(dve):
                dve.tensor_scalar(gate[:, :], gate[:, :], c.tg[:, 5:6], None, ALU.mult).then_inc(gated, 1)
                dve.wait_ge(gated, 1)
                for t in range(NT):
                    dve.wait_ge(placed, t + 1)
                    dve.scalar_tensor_tensor(out=c.X[:, t, :], in0=c.PS[:, t % 8, 0:D], scalar=gate[:, t:t + 1],
                                             in1=c.X[:, t, :], op0=ALU.mult, op1=ALU.add).then_inc(added, 1)

            @block.tensor
            def _(pe):
                for t in range(NT):
                    if t >= 8:
                        pe.wait_ge(added, t - 7)
                    for hf in range(2):
                        mm = pe.matmul(c.PS[:, t % 8, 0:D], pickT[:, hf, tile(t)], Y[:, t // QT_B * per + hf, :],
                                       start=(hf == 0), stop=(hf == 1))
                    mm.then_inc(placed, 1)



HID = 64
NEG = 1e18


def layer2_attention(c, ctx_T, ctx_rows, key_mask, w, consts, scratch):
    nc = c.nc
    chunk = lambda b: slice(b * S, (b + 1) * S)
    with ExitStack() as ctx:
        sb = lambda n, shape, dt=F32: c.sb(ctx, "a2_" + n, shape, dt)
        rows = PACKED + 3
        WOUT, brow = sb("WOUT", [P, 4, D]), sb("brow", [1, D])
        G, CW = sb("G", [P, DK, P]), sb("CW", [P, DK, H])
        g, cc = sb("g", [P, 2, DK]), sb("cc", [H, 1])
        QP, KP = sb("QP", [rows, H, T], BF16), sb("KP", [rows, H, T], BF16)
        keys = ExitStack()
        ctxT = c.sb(keys, "a2_ctxT", [P, DK, T])
        with ExitStack() as early:
            tb = lambda n, shape, dt=F32: c.sb(early, "a2_" + n, shape, dt)
            WqT, WkT = tb("WqT", [HID, D]), tb("WkT", [HID, D])
            Wq, Wk = tb("Wq", [P, DK, HID]), tb("Wk", [P, DK, HID])
            bqr, bkr = tb("bqr", [P, DK, HID]), tb("bkr", [P, DK, HID])
            bq, bk = tb("bq", [H, HID]), tb("bk", [H, HID])
            Z, Wo, bvT, bo = tb("Z", [HID, H, P]), tb("Wo", [HID, H, D]), tb("bvT", [HID, H]), tb("bo", [1, D])
            blocks, heads = tb("blocks", [P, P]), tb("heads", [P, DK, H])
            junk = tb("junk", [P, HID])
            weights = start_loads(c, "a2", [
                (WqT[:, :], w["WqT"]), (WkT[:, :], w["WkT"]), (Wq[:, :, :], w["Wq_rows"]), (Wk[:, :, :], w["Wk_rows"]),
                (bqr[:, :, :], w["bq_rows"]), (bkr[:, :, :], w["bk_rows"]), (bq[:, :], w["bq"]), (bk[:, :], w["bk"]),
                (Z[:, :, :], w["Wv_slots"]), (Wo[:, :, :], w["Wo"].rearrange("(h e) n -> e h n", h=H)),
                (bvT[:, :], w["bvT"]), (bo[:, :], w["bo"].rearrange("(a n) -> a n", a=1)),
                (blocks[:, :], consts["blocks"]), (heads[:, :, :], consts["heads"]),
            ])
            ctx_in = start_loads(c, "a2_ctx", [(ctxT[:, k, :], ctx_T[:, k, :]) for k in range(DK)])
            finish_loads(c, weights)
            made, v = c.sem("a2_w_made"), Tally(c.sem("a2_w_dve"))
            with nc.Block() as block:
                @block.tensor
                def _(pe):
                    for k in range(DK):
                        mm = pe.matmul(c.PS[:, 0, k * P:(k + 1) * P], WqT[:, k * P:(k + 1) * P],
                                       WkT[:, k * P:(k + 1) * P], start=True, stop=True)
                    mm.then_inc(made, 1)
                    for q in range(4):
                        for j in range(4):
                            mm = pe.matmul(c.PS[:, 1 + q // 2, (q % 2) * D:(q % 2 + 1) * D], Z[:, 4 * q + j, :],
                                           Wo[:, 4 * q + j, :], start=(j == 0), stop=(j == 3))
                    mm.then_inc(made, 1)
                    for h in range(H):
                        mm = pe.matmul(c.PS[0:1, 3, 0:D], bvT[:, h:h + 1], Wo[:, h, :], start=(h == 0),
                                       stop=(h == H - 1))
                    mm.then_inc(made, 1)

                @block.vector
                def _(dve):
                    def dots(out, a, b_):
                        n = v.mark(dve.tensor_tensor_reduce(junk[0:a.shape[0], :], a, b_, 1.0, 0.0, ALU.mult, ALU.add,
                                                            out))
                        dve.wait_ge(v.sem, n)
                    for k in range(DK):
                        dots(g[:, 0, k:k + 1], Wk[:, k, :], bqr[:, k, :])
                        dots(g[:, 1, k:k + 1], Wq[:, k, :], bkr[:, k, :])
                    dots(cc[:, :], bq[:, :], bk[:, :])
                    v.mark(dve.tensor_scalar(g[:, 0, :], g[:, 0, :], -1.0, None, ALU.mult))
                    v.mark(dve.tensor_scalar(cc[:, :], cc[:, :], -1.0, None, ALU.mult))
                    for k in range(DK):
                        v.mark(dve.tensor_scalar(CW[:, k, :], heads[:, k, :], g[:, 1, k:k + 1], None, ALU.mult))
                    dve.wait_ge(made, 3)
                    for k in range(DK):
                        v.mark(dve.tensor_tensor(G[:, k, :], c.PS[:, 0, k * P:(k + 1) * P], blocks[:, :], ALU.mult))
                    for i in range(2):
                        v.mark(dve.tensor_copy(WOUT[:, 2 * i:2 * i + 2, :],
                                               c.PS[:, 1 + i, :].rearrange("p (g n) -> p g n", g=2)))
                    v.mark(dve.tensor_tensor(brow[:, :], c.PS[0:1, 3, 0:D], bo[:, :], ALU.add))

        finish_loads(c, ctx_in)
        with keys:
            load_k, k_packed = split_and_pack(
                c, "a2_ks", [[(None, None, ctxT[:, k, chunk(n)]) for k in range(DK)] for n in range(B)], KP, K_PARTS,
                scratch["k"], S, pool_work=lambda pool: pool.memset(KP[PACKED:PACKED + 3, :, :], 1.0))
        with ExitStack() as early:
            layernorm(c, early, "a2_ln", sync_work=load_k)
            load_q, q_packed = split_and_pack(
                c, "a2_qs", [[([(G[:, k, :], c.XNT[:, k, chunk(n)])], g[:, 0, k:k + 1], None) for k in range(DK)]
                             for n in range(B)], QP, Q_PARTS, scratch["q"], S, scale=-1.0)
            load_c, c_packed = split_and_pack(
                c, "a2_cs", [[([(CW[:, k, :], c.XNT[:, k, chunk(n)]) for k in range(DK)], cc[:, :], None)]
                             for n in range(B)], QP, None, scratch["c"], S, rows=H, scale=-1.0, lead=PACKED)
        att = Attention(c, ctx, "a2_att", S, True, q_tiles=CAUSAL_BATCHES * QT_B, ring=6, lag=2)
        crow = att.probs[:, 0:2 * CAUSAL_BATCHES, :].rearrange("p a (t d) -> p (a t) d", t=2)
        pen = att.probs[:, 2 * CAUSAL_BATCHES:3 * CAUSAL_BATCHES, :]
        VB = sb("VB", [P, CAUSAL_BATCHES * QT_B, H, SLOT])
        later, mask = sb("later", [P, QT_B, S], BF16), sb("mask", [P, CAUSAL_BATCHES, QT_B, S])
        set_, q = c.sem("a2_set"), {k: c.sem("a2_b_" + k) for k in ("rows", "mask", "pen")}
        with nc.Block() as block:
            @block.sync
            def _(sp):
                load_q(sp)
                load_c(sp)

            @block.gpsimd
            def _(pool):
                pool.memset(VB[:, :, :, DH:SLOT], 0.0).then_inc(set_, 1)
                pool.memset(later[:, :, :], 0.0).then_inc(set_, 1)
                pool.wait_ge(set_, 2)
                for t in range(QT_B):
                    pool.affine_select(out=later[:, t, :], in_=later[:, t, :], compare_op=ALU.is_ge, fill=1.0,
                                       base=t * P, pattern=[[-1, S]], channel_multiplier=1)
        finish_loads(c, k_packed, q_packed, c_packed)
        with nc.Fori(0, B // CAUSAL_BATCHES) as turn:
            with nc.Block() as block:
                @block.sync
                def _(sp):
                    for i in range(CAUSAL_BATCHES):
                        sp.dma_start(pen[:, i, :].bitcast(I32), key_mask[bass.ds(turn * CAUSAL_BATCHES + i, 1), :]
                                     .rearrange("a s -> (a s)").partition_broadcast(P)).then_inc(q["mask"], 16)
                    sp.dma_start(crow, ctx_rows[:, bass.ds(turn * CAUSAL_BATCHES * QT_B, CAUSAL_BATCHES * QT_B), :])\
                      .then_inc(q["rows"], 16)

                @block.gpsimd
                def _(pool):
                    pool.wait_ge(q["rows"], 16)
                    pool.tensor_copy(VB[:, :, :, 0:DH], crow.rearrange("p t (h d) -> p t h d", h=H))

                @block.vector
                def _(dve):
                    dve.wait_ge(q["mask"], 16 * CAUSAL_BATCHES)
                    dve.tensor_scalar(pen, pen.bitcast(I32), -1.0, -NEG, ALU.add, ALU.mult).then_inc(q["pen"], 1)
                    dve.wait_ge(q["pen"], 1)
                    for i in range(CAUSAL_BATCHES):
                        for t in range(QT_B):
                            dve.scalar_tensor_tensor(out=mask[:, i, t, :], in0=later[:, t, :], scalar=NEG,
                                                     in1=pen[:, i, :], op0=ALU.mult, op1=ALU.add)
            with nc.Block() as block:
                @block.gpsimd
                def _(pool):
                    for sm in q.values():
                        pool.sem_clear(sm)
            whole = slice(0, S)
            first = turn * CAUSAL_BATCHES * S
            att.run(lambda qt, h: [(whole, QP[:, h, bass.ds(first + qt * P, P)],
                                    KP[:, h, bass.ds(first + qt // QT_B * S, S)])],
                    lambda qt: mask[:, qt // QT_B, qt % QT_B, :], lambda qt, h, k: VB[:, qt // QT_B * QT_B + k, h, :],
                    WOUT, brow[:, :],
                    lambda dve, qt, delta: add_scaled(dve, c, 2, c.X[:, bass.ds(turn * CAUSAL_BATCHES * QT_B + qt, 1), :]
                                                      .rearrange("p a d -> p (a d)"), delta))
            att.clear()



WINDOW = 16


def layer3_attention(c, ctx_T, w, scratch):
    nc = c.nc
    chunk = lambda b: slice(b * S, (b + 1) * S)
    tile = lambda t: slice(t * P, (t + 1) * P)
    with ExitStack() as ctx:
        sb = lambda n, shape, dt=F32: c.sb(ctx, "a3_" + n, shape, dt)
        QP, KP = sb("QP", [PACKED, H, T], BF16), sb("KP", [PACKED, H, T], BF16)
        V = sb("V", [P, NT, D])
        WOUT, bo = sb("WOUT", [P, 4, D]), sb("bo", [1, D])
        zero_key = sb("zero_key", [PACKED, P], BF16)
        row = lambda v: v.rearrange("(a n) -> a n", a=1)
        with ExitStack() as early:
            tb = lambda n, shape, dt=F32: c.sb(early, "a3_" + n, shape, dt)
            W = {n: tb("W" + n, [P, DK, D]) for n in "qkv"}
            bq, bk, bv = tb("bq", [P, DK]), tb("bk", [P, DK]), tb("bv", [1, D])
            q_bias = tb("q_bias", [P, DK])
            with ExitStack() as kctx:
                ctxT = c.sb(kctx, "a3_ctxT", [P, DK, T])
                load_all(c, "a3", [(W[n][:, :, :], w[f"W{n}_T"]) for n in "kvq"] + [
                    (bq[:, :], w["bq_cols"]), (bk[:, :], w["bk_cols"]), (bv[:, :], row(w["bv"])),
                    (bo[:, :], row(w["bo"])), (WOUT[:, :, :], w["Wo_slots"]),
                    (ctxT[:, :, :], ctx_T)])
                with nc.Block() as block:
                    @block.vector
                    def _(dve):
                        dve.tensor_scalar(q_bias[:, :], bq[:, :], -0.25, None, ALU.mult)

                    @block.gpsimd
                    def _(pool):
                        pool.memset(zero_key[:, :], 0.0)
                load_k, k_packed = split_and_pack(
                    c, "a3_ks", [[([(W["k"][:, i, tile(k)], ctxT[:, i, chunk(n)]) for i in range(DK)],
                                   bk[:, k:k + 1], None) for k in range(DK)] for n in range(B)], KP, K_PARTS,
                    scratch["k"], S)
                project_columns(c, "a3_v", [
                    (columns(P, D), [(ctxT[:, i, tile(t)], W["v"][:, i, :]) for i in range(DK)]
                     + [(c.ones[0:1, :], bv[:, :])], V[:, t, :]) for t in range(NT)], sync_work=load_k)
            layernorm(c, early, "a3_ln")
            load_q, q_packed = split_and_pack(
                c, "a3_qs", [[([(W["q"][:, i, tile(k)], c.XNT[:, i, chunk(n)]) for i in range(DK)],
                               q_bias[:, k:k + 1], None) for k in range(DK)] for n in range(B)], QP, Q_PARTS,
                scratch["q"], S, scale=-0.25)
        att = Attention(c, ctx, "a3_att", 2 * P, True, q_tiles=BATCHES * QT_B, ring=4, lag=1)
        VB = sb("VB", [P, BATCHES, 1 + QT_B, H, SLOT])
        mask = sb("mask", [P, 2, 2 * P])
        built = c.sem("a3_built")
        with nc.Block() as block:
            @block.sync
            def _(sp):
                load_q(sp)

            @block.gpsimd
            def _(pool):
                pool.memset(VB[:, :, :, :, :], 0.0).then_inc(built, 1)
                pool.memset(mask[:, :, :], 0.0).then_inc(built, 1)
                pool.wait_ge(built, 2)
                kinds = [(0, P, -1, 1), (0, WINDOW - 1 - P, 1, -1), (1, P, -1, 1), (1, WINDOW - 1 - P, 1, -1),
                         (0, P - WINDOW + 1, -1, 2)]
                for i, (m, base, step, per_query) in enumerate(kinds):
                    pool.affine_select(out=mask[:, m, :], in_=mask[:, m, :], compare_op=ALU.is_ge, fill=-F32_MIN / 2,
                                       base=base, pattern=[[step, 2 * P]], channel_multiplier=per_query)\
                        .then_inc(built, 1)
                    pool.wait_ge(built, 3 + i)
        finish_loads(c, k_packed, q_packed)
        with nc.Fori(0, B // BATCHES) as turn:
            with nc.Block() as block:
                @block.gpsimd
                def _(pool):
                    for i in range(BATCHES):
                        pool.tensor_copy(VB[:, i, 1:1 + QT_B, :, 0:DH],
                                         V[:, bass.ds((turn * BATCHES + i) * QT_B, QT_B), :]
                                         .rearrange("p t (h d) -> p t h d", h=H))

            def scores(qt, h):
                first = turn * BATCHES * S + qt * P
                q = QP[:, h, bass.ds(first, P)]
                if qt % QT_B == 0:
                    return [(slice(0, P), q, zero_key[:, :]), (slice(P, 2 * P), q, KP[:, h, bass.ds(first, P)])]
                return [(slice(0, 2 * P), q, KP[:, h, bass.ds(first - P, 2 * P)])]
            att.run(scores, lambda qt: mask[:, min(qt % QT_B, 1), :],
                    lambda qt, h, k: VB[:, qt // QT_B, qt % QT_B + k, h, :], WOUT, bo[:, :],
                    lambda dve, qt, delta: add_scaled(dve, c, 3, c.X[:, bass.ds(turn * BATCHES * QT_B + qt, 1), :]
                                                      .rearrange("p a d -> p (a d)"), delta))
            att.clear()



FF3 = 1024


def layer3_ffn(c, w):
    nc = c.nc
    nf = FF3 // P
    with ExitStack() as ctx:
        sb = lambda n, shape, dt=F32: c.sb(ctx, "f3_" + n, shape, dt)
        W1, W2 = sb("W1", [P, DK * FF3]), sb("W2", [P, nf * D])
        b1, b2 = sb("b1", [P, nf]), sb("b2", [1, D])
        hid = sb("hid", [P, 2, nf, S])
        c.XNT = sb("XNT", [P, DK, T])
        weights = start_loads(c, "f3", [(W1[:, :], w["W1_T"].rearrange("p k n -> p (k n)")),
                           (W2[:, :], w["W2_T"].rearrange("p k n -> p (k n)")),
                           (b1[:, :], w["b1_cols"]), (b2[:, :], w["b2"].rearrange("(a n) -> a n", a=1))])
        layernorm(c, ctx, "f3_ln", placed=True)
        finish_loads(c, weights)
        with ExitStack() as early:
            rounded = c.sb(early, "f3_rounded", [P, 2, DK * FF3])
            tot, scale = c.sb(early, "f3_tot", [P, 2]), c.sb(early, "f3_scale", [P, 2])
            v, summed = Tally(c.sem("f3_w_dve")), c.sem("f3_summed")
            with nc.Block() as block:
                @block.vector
                def _(dve):
                    def then(ins):
                        dve.wait_ge(v.sem, v.mark(ins))
                    for i, Wt in enumerate((W1, W2)):
                        then(dve.tensor_reduce(tot[:, i:i + 1], Wt[:, :], X_AXIS, ALU.add, apply_absolute_value=True))
                    dve.wait_ge(summed, 1)
                    then(dve.tensor_scalar(scale[:, :], c.PS[:, 0, 0:2], 1.0 / (D * FF3), 1e-8, ALU.mult, ALU.max))
                    then(dve.reciprocal(scale[:, :], scale[:, :]))
                    for i, Wt in enumerate((W1, W2)):
                        R = rounded[:, i, :]
                        then(dve.tensor_scalar(R, Wt[:, :], scale[:, i:i + 1], MAGIC, ALU.mult, ALU.add))
                        then(dve.tensor_scalar(R, R, -MAGIC, 1.0, ALU.add, ALU.min))
                        then(dve.scalar_tensor_tensor(out=R, in0=R, scalar=-1.0, in1=Wt[:, :], op0=ALU.max,
                                                      op1=ALU.subtract))
                        then(dve.tensor_tensor(Wt[:, :], Wt[:, :], R, ALU.add))

                @block.tensor
                def _(pe):
                    pe.wait_ge(v.sem, 2)
                    pe.matmul(c.PS[:, 0, 0:2], c.ones[:, :], tot[:, :], start=True, stop=True).then_inc(summed, 1)
        s = {k: c.sem("f3_" + k) for k in ("made", "gelu", "out", "added")}
        W1v = W1[:, :].rearrange("p (k n) -> p k n", k=DK)
        W2v = W2[:, :].rearrange("p (k n) -> p k n", k=nf)
        with nc.Block() as block:
            @block.tensor
            def _(pe):
                def up(n):
                    for f in range(nf):
                        i = n * nf + f
                        if i >= 4:
                            pe.wait_ge(s["gelu"], i - 3)
                        for k in range(DK):
                            mm = pe.matmul(c.PS[:, i % 4, :], W1v[:, k, f * P:(f + 1) * P],
                                           c.XNT[:, k, n * S:(n + 1) * S], start=(k == 0), stop=(k == DK - 1))
                        mm.then_inc(s["made"], 1)

                def down(n):
                    pe.wait_ge(s["gelu"], nf * (n + 1))
                    for t in range(QT_B):
                        i = n * QT_B + t
                        if i >= 4:
                            pe.wait_ge(s["added"], i - 3)
                        for f in range(nf):
                            pe.matmul(c.PS[:, 4 + i % 4, 0:D], hid[:, n % 2, f, t * P:(t + 1) * P], W2v[:, f, :],
                                      start=(f == 0), stop=False)
                        pe.matmul(c.PS[:, 4 + i % 4, 0:D], c.ones[0:1, :], b2[:, :], start=False, stop=True)\
                            .then_inc(s["out"], 1)
                up(0)
                for n in range(B):
                    if n + 1 < B:
                        up(n + 1)
                    down(n)

            @block.scalar
            def _(act):
                for n in range(B):
                    for f in range(nf):
                        i = n * nf + f
                        act.wait_ge(s["made"], i + 1)
                        if n >= 2 and f == 0:
                            act.wait_ge(s["out"], QT_B * (n - 1))
                        act.activation(hid[:, n % 2, f, :], c.PS[:, i % 4, :], ACT.Gelu, bias=b1[:, f:f + 1])\
                           .then_inc(s["gelu"], 1)

            @block.vector
            def _(dve):
                for i in range(NT):
                    dve.wait_ge(s["out"], i + 1)
                    add_scaled(dve, c, 7, c.X[:, i, :], c.PS[:, 4 + i % 4, 0:D]).then_inc(s["added"], 1)



E = 8
SLOT_TILES = NT + E - 1
MAGIC = 1.5 * 2.0 ** 23


def first_best(c, dve, then, values, best, number, junk3, numbers):
    then(dve.tensor_tensor(junk3, values, best.unsqueeze(2).to_broadcast([P, NT, E]), ALU.is_equal))
    then(dve.scalar_tensor_tensor(out=junk3, in0=numbers, scalar=-float(E), in1=junk3, op0=ALU.add, op1=ALU.mult))
    then(dve.tensor_reduce(number, junk3, X_AXIS, ALU.min))
    then(dve.tensor_scalar(number, number, float(E), None, ALU.add))


def clear_expert_rows(c, xs):
    with c.nc.Block() as block:
        @block.sync
        def _(sp):
            sp.dma_start(xs.rearrange("(i p) d -> p i d", p=P),
                         c.zeros[:, :].unsqueeze(1).to_broadcast([P, SLOT_TILES, D])).then_inc(c.xs_cleared, 16)


def dispatch(c, name, place, tile_expert, expert, rows, consts, xs, meanwhile=None, send_later=False):
    nc = c.nc
    with ExitStack() as ctx:
        sb = lambda n, shape, dt=F32: c.sb(ctx, name + "_" + n, shape, dt)
        numbers, tiles_no = sb("numbers", [P, NT, E]), sb("tiles_no", [P, SLOT_TILES, E])
        later = sb("later", [P, P])
        hot, before = sb("hot", [P, NT, E]), sb("before", [P, NT, E])
        carry = sb("carry", [P, NT + 1, E])
        need, end, start = sb("need", [P, E]), sb("end", [P, E]), sb("start", [P, E])
        place_f, tile_f, cmp = sb("place_f", [P, NT]), sb("tile_f", [P, SLOT_TILES]), sb("cmp", [P, SLOT_TILES, E])
        load_all(c, name + "_c", [(numbers[:, :, :], consts["numbers"]), (tiles_no[:, :, :], consts["tile_numbers"]),
                                  (later[:, :], consts["later"])])
        if meanwhile:
            meanwhile()
        v, hot_ready, counted = Tally(c.sem(name + "_dve")), c.sem(name + "_hot"), c.sem(name + "_counted")
        placed, sent = c.sem(name + "_placed"), c.soft_sems[name + "_sent"]
        flat = lambda ap: ap.rearrange("p t e -> p (t e)")

        def send(pool):
            pool.wait_ge(c.xs_cleared, 16)
            for t in range(NT):
                pool.indirect_dma_start(xs, bass.IndirectOffsetOnAxis(ap=place[:, t:t + 1].bitcast(U32), axis=0),
                                        rows[:, t, :], None).then_inc(sent, 16)
            pool.wait_ge(sent, 16 * NT)

        with nc.Block() as block:
            @block.vector
            def _(dve):
                def then(ins):
                    dve.wait_ge(v.sem, v.mark(ins))
                then(dve.memset(carry[:, 0, :], 0.0))
                dve.tensor_tensor(hot[:, :, :], numbers[:, :, :],
                                  expert.unsqueeze(2).to_broadcast([P, NT, E]), ALU.is_equal).then_inc(hot_ready, 1)
                dve.wait_ge(counted, 1)
                totals = c.PS[:, 1, 0:NT * E].rearrange("p (t e) -> p t e", t=NT)
                for t in range(NT):
                    then(dve.tensor_tensor(carry[:, t + 1, :], totals[:, t, :], carry[:, t, :], ALU.add))
                then(dve.tensor_scalar(need[:, :], carry[:, NT, :], 1.0 / P, 0.5 - 0.5 / P, ALU.mult, ALU.add))
                then(dve.tensor_scalar(need[:, :], need[:, :], MAGIC, None, ALU.add))
                then(dve.tensor_scalar(need[:, :], need[:, :], -MAGIC, None, ALU.add))
                then(dve.tensor_tensor_scan(end[:, :], c.ones[:, 0:E], need[:, :], 0.0, ALU.mult, ALU.add))
                then(dve.tensor_tensor(start[:, :], end[:, :], need[:, :], ALU.subtract))
                then(dve.tensor_scalar(start[:, :], start[:, :], float(P), None, ALU.mult))
                then(dve.tensor_tensor(before[:, :, :], c.PS[:, 0, 0:NT * E].rearrange("p (t e) -> p t e", t=NT),
                                       carry[:, 0:NT, :], ALU.add))
                then(dve.tensor_tensor(before[:, :, :], before[:, :, :],
                                       start[:, :].unsqueeze(1).to_broadcast([P, NT, E]), ALU.add))
                then(dve.tensor_tensor(before[:, :, :], before[:, :, :], hot[:, :, :], ALU.mult))
                then(dve.tensor_reduce(place_f[:, :], before[:, :, :], X_AXIS, ALU.add))
                dve.tensor_copy(place[:, :], place_f[:, :]).then_inc(placed, 1)
                then(dve.tensor_tensor(cmp[:, :, :], tiles_no[:, :, :],
                                       end[:, :].unsqueeze(1).to_broadcast([P, SLOT_TILES, E]), ALU.is_ge))
                then(dve.tensor_reduce(tile_f[:, :], cmp[:, :, :], X_AXIS, ALU.add))
                then(dve.tensor_scalar(tile_f[:, :], tile_f[:, :], E - 1.0, None, ALU.min))
                dve.tensor_copy(tile_expert[:, :], tile_f[:, :])
                if send_later:
                    dve.wait_ge(placed, 1)

            @block.tensor
            def _(pe):
                pe.wait_ge(hot_ready, 1)
                pe.matmul(c.PS[:, 0, 0:NT * E], later[:, :], flat(hot[:, :, :]), start=True, stop=True)
                pe.matmul(c.PS[:, 1, 0:NT * E], c.ones[:, :], flat(hot[:, :, :]), start=True, stop=True)\
                    .then_inc(counted, 1)

            @block.gpsimd
            def _(pool):
                if not send_later:
                    pool.wait_ge(placed, 1)
                    send(pool)
    return send


class Turn:

    def __init__(self, n, half, par):
        self.n, self.half, self.par = n, half, par


def expert_tiles(c, name, scope, tile_expert, xs, ys, weights_in, weights_out, hidden, gated, biases=None):
    nc = c.nc
    nh = hidden // P
    with ExitStack() as ctx:
        sb = lambda n, shape, dt=F32: c.sb(ctx, name + "_" + n, shape, dt)
        xr, xt = sb("xr", [P, 2, D]), sb("xt", [P, 2, DK, P])
        act_h, hid, hidT, y = sb("act_h", [P, 2, 512]), sb("hid", [P, 2, hidden]), sb("hidT", [P, 2, nh, P]), sb("y", [P, 2, D])
        brow1, brow2 = (sb("brow1", [1, 2, hidden]), sb("brow2", [1, 2, D])) if biases else (None, None)
        s = {k: c.sem(name + "_" + k) for k in ("x_turned", "x_copied", "hidden", "act", "hid", "h_turned",
                                                "h_copied_a", "h_copied_d", "out", "y")}
        loaded = [c.sem(f"{name}_loaded{i}") for i in range(2)]
        stored = [c.sem(f"{name}_stored{i}") for i in range(2)]
        b1_in = [c.sem(f"{name}_b1_in{i}") for i in range(2)]
        b2_in = [c.sem(f"{name}_b2_in{i}") for i in range(2)]

        with nc.Block() as block:
            @block.tensor
            def _(pe):
                for k in ("x_turned", "hidden", "out"):
                    pe.sem_inc(s[k], 2)

            @block.scalar
            def _(act):
                for k in ("act", "x_copied", "h_copied_a"):
                    act.sem_inc(s[k], 2)

            @block.vector
            def _(dve):
                for k in ("hid", "y", "h_copied_d"):
                    dve.sem_inc(s[k], 2)

            @block.sync
            def _(sp):
                for q in stored:
                    sp.sem_inc(q, 16)

        FIRST, LAST = 1, SLOT_TILES - 2

        def over_tiles(eng, step, before, after):
            before()
            with eng.Fori(0, (LAST - FIRST) // 2) as it:
                for j in range(2):
                    step(Turn(it * 2 + (FIRST + j), it + (FIRST + j) // 2, (FIRST + j) % 2))
            after()

        assert (LAST - FIRST) % 2 == 0
        fixed = lambda n: Turn(n, n // 2, n % 2)
        N = SLOT_TILES

        with nc.Block() as block:
            @block.sync
            def _(sp):
                def load(t):
                    sp.wait_ge(s["x_turned"], t.n + 1)
                    sp.dma_start(xr[:, t.par, :], xs[bass.ds(t.n * P, P), :]).then_inc(loaded[t.par], 16)

                def load_bias(t, which):
                    if not biases:
                        return
                    row, used, into = ((brow1, "hidden", b1_in), (brow2, "out", b2_in))[which]
                    e = sp.value_load(tile_expert[0:1, bass.ds(t.n, 1)], min_val=0, max_val=E - 1)
                    sp.wait_ge(s[used], t.n + 1)
                    sp.dma_start(row[:, t.par, :], biases[which][bass.ds(e, 1), :]).then_inc(into[t.par], 16)

                def save(t):
                    sp.wait_ge(s["y"], t.n + 3)
                    sp.dma_start(ys[bass.ds(t.n * P, P), :], y[:, t.par, :]).then_inc(stored[t.par], 16)

                def step(t):
                    nxt = Turn(t.n + 1, t.half + t.par, 1 - t.par)
                    load(nxt)
                    load_bias(nxt, 0)
                    save(Turn(t.n - 1, t.half - 1 + t.par, 1 - t.par))
                    load_bias(t, 1)
                over_tiles(sp, step, lambda: (load(fixed(0)), load_bias(fixed(0), 0), load(fixed(1)),
                                              load_bias(fixed(1), 0), load_bias(fixed(0), 1)),
                           lambda: (step(fixed(N - 2)), save(fixed(N - 2)), load_bias(fixed(N - 1), 1),
                                    save(fixed(N - 1))))
                for par in range(2):
                    sp.wait_ge(stored[par], 16 * (1 + (N + 1 - par) // 2))

            @block.tensor
            def _(pe):
                def turn_x(t):
                    pe.wait_ge(loaded[t.par], t.half * 16 + 16)
                    pe.wait_ge(s["x_copied"], t.n + 2)
                    for k in range(DK):
                        mm = pe.transpose(c.PS[:, 0, k * P:(k + 1) * P], xr[:, t.par, k * P:(k + 1) * P],
                                          c.ident[:, :])
                    mm.then_inc(s["x_turned"], 1)

                def first(t):
                    pe.wait_ge(s["x_copied"], t.n + 3)
                    pe.wait_ge(s["act"], t.n + 1)
                    pe.wait_ge(s["hid"], t.n + 1)
                    e = pe.value_load(tile_expert[0:1, bass.ds(t.n, 1)], min_val=0, max_val=E - 1)
                    for i, Wi in enumerate(weights_in):
                        bank = c.PS[:, 2 + 2 * t.par + i, :]
                        for k in range(DK):
                            mm = pe.matmul(bank, xt[:, t.par, k, :],
                                           Wi[:, k, bass.ds(e, 1), :].rearrange("p a n -> p (a n)"),
                                           start=(k == 0), stop=(k == DK - 1 and not biases))
                        if biases:
                            if i == 0:
                                pe.wait_ge(b1_in[t.par], t.half * 16 + 16)
                            mm = pe.matmul(bank, c.ones[0:1, :], brow1[:, t.par, 512 * i:512 * (i + 1)], start=False,
                                           stop=True)
                    mm.then_inc(s["hidden"], 1)

                def second(t):
                    pe.wait_ge(s["hid"], t.n + 3)
                    if biases:
                        pe.wait_ge(s["act"], t.n + 3)
                    pe.wait_ge(s["h_copied_d"], t.n + 2)
                    if nh > 4:
                        pe.wait_ge(s["h_copied_a"], t.n + 2)
                    for f in range(nh):
                        mm = pe.transpose(c.PS[:, 1 if f < 4 else 6, (f % 4) * P:(f % 4 + 1) * P],
                                          hid[:, t.par, f * P:(f + 1) * P], c.ident[:, :])
                    mm.then_inc(s["h_turned"], 1)
                    e = pe.value_load(tile_expert[0:1, bass.ds(t.n, 1)], min_val=0, max_val=E - 1)
                    pe.wait_ge(s["h_copied_d"], t.n + 3)
                    if nh > 4:
                        pe.wait_ge(s["h_copied_a"], t.n + 3)
                    pe.wait_ge(s["y"], t.n + 2)
                    for f in range(nh):
                        mm = pe.matmul(c.PS[:, 7, 0:D], hidT[:, t.par, f, :],
                                       weights_out[:, f, bass.ds(e, 1), :].rearrange("p a n -> p (a n)"),
                                       start=(f == 0), stop=(f == nh - 1 and not biases))
                    if biases:
                        pe.wait_ge(b2_in[t.par], t.half * 16 + 16)
                        mm = pe.matmul(c.PS[:, 7, 0:D], c.ones[0:1, :], brow2[:, t.par, :], start=False, stop=True)
                    mm.then_inc(s["out"], 1)

                def step(t):
                    first(t)
                    turn_x(Turn(t.n + 1, t.half + t.par, 1 - t.par))
                    second(Turn(t.n - 1, t.half - 1 + t.par, 1 - t.par))
                over_tiles(pe, step, lambda: (turn_x(fixed(0)), first(fixed(0)), turn_x(fixed(1))),
                           lambda: (step(fixed(N - 2)), first(fixed(N - 1)), second(fixed(N - 2)),
                                    second(fixed(N - 1))))

            @block.scalar
            def _(act):
                def copy_x(t):
                    act.wait_ge(s["x_turned"], t.n + 3)
                    act.wait_ge(s["act"], t.n + 1)
                    act.copy(xt[:, t.par, :, :], c.PS[:, 0, 0:D].rearrange("p (k q) -> p k q", k=DK))\
                       .then_inc(s["x_copied"], 1)

                def activate(t):
                    act.wait_ge(s["hidden"], t.n + 3)
                    act.wait_ge(s["out"], t.n + 1)
                    if gated:
                        act.activation(act_h[:, t.par, :], c.PS[:, 2 + 2 * t.par, :], ACT.Silu)\
                           .then_inc(s["act"], 1)
                    else:
                        act.activation(hid[:, t.par, 0:512], c.PS[:, 2 + 2 * t.par, :], ACT.Relu)\
                           .then_inc(s["act"], 1)

                def copy_h(t):
                    if nh > 4:
                        act.wait_ge(s["h_turned"], t.n + 1)
                        act.copy(hidT[:, t.par, 4:8, :], c.PS[:, 6, :].rearrange("p (f q) -> p f q", f=4))\
                           .then_inc(s["h_copied_a"], 1)

                def step(t):
                    activate(t)
                    copy_x(Turn(t.n + 1, t.half + t.par, 1 - t.par))
                    copy_h(Turn(t.n - 1, t.half - 1 + t.par, 1 - t.par))
                over_tiles(act, step, lambda: (copy_x(fixed(0)), activate(fixed(0)), copy_x(fixed(1))),
                           lambda: (step(fixed(N - 2)), activate(fixed(N - 1)), copy_h(fixed(N - 2)),
                                    copy_h(fixed(N - 1))))

            @block.vector
            def _(dve):
                def combine(t):
                    dve.wait_ge(s["hidden"], t.n + 3)
                    if gated:
                        dve.wait_ge(s["act"], t.n + 3)
                    dve.wait_ge(s["out"], t.n + 1)
                    up = c.PS[:, 3 + 2 * t.par, :]
                    if gated:
                        dve.tensor_tensor(hid[:, t.par, :], up, act_h[:, t.par, :], ALU.mult).then_inc(s["hid"], 1)
                    else:
                        dve.tensor_scalar(hid[:, t.par, 512:1024], up, 0.0, None, ALU.max).then_inc(s["hid"], 1)

                def finish(t):
                    dve.wait_ge(s["h_turned"], t.n + 1)
                    dve.tensor_copy(hidT[:, t.par, 0:4, :], c.PS[:, 1, :].rearrange("p (f q) -> p f q", f=4))\
                       .then_inc(s["h_copied_d"], 1)
                    dve.wait_ge(s["out"], t.n + 3)
                    dve.wait_ge(stored[t.par], t.half * 16 + 16)
                    dve.tensor_copy(y[:, t.par, :], c.PS[:, 7, 0:D]).then_inc(s["y"], 1)

                def step(t):
                    combine(t)
                    finish(Turn(t.n - 1, t.half - 1 + t.par, 1 - t.par))
                over_tiles(dve, step, lambda: combine(fixed(0)),
                           lambda: (step(fixed(N - 2)), combine(fixed(N - 1)), finish(fixed(N - 2)),
                                    finish(fixed(N - 1))))


def collect(c, name, place, ys, gate):
    with ExitStack() as ctx:
        got = c.sb(ctx, name + "_got", [P, NT, D])
        arrived = [c.soft_sems[f"{name}_got{t}"] for t in range(4)]
        with c.nc.Block() as block:
            @block.gpsimd
            def _(pool):
                for t in range(NT):
                    pool.indirect_dma_start(got[:, t, :], None, ys,
                                            bass.IndirectOffsetOnAxis(ap=place[:, t:t + 1].bitcast(U32), axis=0))\
                        .then_inc(arrived[t // 4], 16)

            @block.vector
            def _(dve):
                for i in range(4):
                    dve.wait_ge(arrived[i], 64)
                    for t in range(4 * i, 4 * i + 4):
                        add_scaled(dve, c, gate, c.X[:, t, :], got[:, t, :])



FF0 = 512


def layer0_ffn(c, w, consts, xs, ys):
    nc = c.nc
    nf = FF0 // P
    with ExitStack() as ctx:
        sb = lambda n, shape, dt=F32: c.sb(ctx, "f0_" + n, shape, dt)
        place, tile_expert = sb("place", [P, NT], I32), sb("tile_expert", [P, SLOT_TILES], I32)
        Wg, Wu, Wd = sb("Wg", [P, DK, E, FF0]), sb("Wu", [P, DK, E, FF0]), sb("Wd", [P, nf, E, D])
        with ExitStack() as early:
            tb = lambda n, shape, dt=F32: c.sb(early, "f0_" + n, shape, dt)
            c.XNT = tb("XNT", [P, DK, T])
            c.XN = tb("XN", [P, NT, D])
            Sg, Su, Sd = tb("Sg", [P, DK, FF0]), tb("Su", [P, DK, FF0]), tb("Sd", [P, nf, D])
            router, lnw, lnb = tb("router", [P, DK, E]), tb("lnw", [P, D]), tb("lnb", [P, D])
            logits, best, expert, score = tb("logits", [P, NT, E]), tb("best", [P, NT]), tb("expert", [P, NT]), tb("score", [P, NT])
            eq, numbers = tb("eq", [P, NT, E]), tb("numbers", [P, NT, E])
            small = start_loads(c, "f0", [
                (Sg[:, :, :], w["sh_gate"].rearrange("(k p) n -> p k n", p=P)),
                (Su[:, :, :], w["sh_up"].rearrange("(k p) n -> p k n", p=P)),
                (Sd[:, :, :], w["sh_down"].rearrange("(k p) n -> p k n", p=P)),
                (router[:, :, :], w["router_w"].rearrange("(k p) n -> p k n", p=P)),
                (lnw[:, :], w["ln_w"].partition_broadcast(P)), (lnb[:, :], w["ln_b"].partition_broadcast(P)),
                (numbers[:, :, :], consts["numbers"])])
            experts = start_loads(c, "f0_w", [
                (dst[:, k, :, :], src[:, k * P:(k + 1) * P, :].rearrange("e p n -> p e n"))
                for dst, src, n in ((Wg, w["gate_w"], DK), (Wu, w["up_w"], DK), (Wd, w["down_w"], nf))
                for k in range(n)])
            normalise(c, "f0_n1", c.X, c.XN)
            finish_loads(c, small)
            with nc.Block() as block:
                @block.vector
                def _(dve):
                    for t in range(NT):
                        add_scaled(dve, c, 4, c.X[:, t, :], c.XN[:, t, :])
            normalise(c, "f0_n2", c.XN, c.XN, (lnw, lnb), turned_into=c.XNT)
            token_logits(c, "f0_route", router, E, logits[:, :, :])
            v = Tally(c.sem("f0_r_dve"))
            with nc.Block() as block:
                @block.vector
                def _(dve):
                    def then(ins):
                        dve.wait_ge(v.sem, v.mark(ins))
                    then(dve.tensor_reduce(best[:, :], logits[:, :, :], X_AXIS, ALU.max))
                    first_best(c, dve, then, logits[:, :, :], best[:, :], expert[:, :], eq[:, :, :], numbers[:, :, :])

                @block.scalar
                def _(act):
                    act.wait_ge(v.sem, 1)
                    act.activation(score[:, :], best[:, :], ACT.Sigmoid)
            with nc.Block() as block:
                @block.vector
                def _(dve):
                    for t in range(NT):
                        dve.tensor_scalar(c.XN[:, t, :], c.XN[:, t, :], score[:, t:t + 1], None, ALU.mult)
            send = dispatch(c, "f0_d", place, tile_expert, expert[:, :], c.XN, consts, xs, send_later=True)
            s = {k: c.sem("f0_" + k) for k in ("gate", "silu", "hid", "out", "added")}
            with ExitStack() as sh:
                silu, hid = c.sb(sh, "f0_silu", [P, 2, S]), c.sb(sh, "f0_hid", [P, nf, S])
                with nc.Block() as block:
                    @block.gpsimd
                    def _(pool):
                        send(pool)

                    @block.tensor
                    def _(pe):
                        for n in range(B):
                            for f in range(nf):
                                i = n * nf + f
                                if i >= 2:
                                    pe.wait_ge(s["hid"], i - 1)
                                for m, Wm in ((0, Sg), (1, Su)):
                                    for k in range(DK):
                                        mm = pe.matmul(c.PS[:, 2 * (i % 2) + m, :], Wm[:, k, f * P:(f + 1) * P],
                                                       c.XNT[:, k, n * S:(n + 1) * S], start=(k == 0),
                                                       stop=(k == DK - 1))
                                mm.then_inc(s["gate"], 1)
                            pe.wait_ge(s["hid"], nf * (n + 1))
                            for t in range(QT_B):
                                i = n * QT_B + t
                                if i >= 4:
                                    pe.wait_ge(s["added"], i - 3)
                                for f in range(nf):
                                    mm = pe.matmul(c.PS[:, 4 + i % 4, 0:D], hid[:, f, t * P:(t + 1) * P], Sd[:, f, :],
                                                   start=(f == 0), stop=(f == nf - 1))
                                mm.then_inc(s["out"], 1)

                    @block.scalar
                    def _(act):
                        for i in range(B * nf):
                            act.wait_ge(s["gate"], i + 1)
                            if i >= 2:
                                act.wait_ge(s["hid"], i - 1)
                            act.activation(silu[:, i % 2, :], c.PS[:, 2 * (i % 2), :], ACT.Silu).then_inc(s["silu"], 1)

                    @block.vector
                    def _(dve):
                        for n in range(B):
                            for f in range(nf):
                                i = n * nf + f
                                dve.wait_ge(s["silu"], i + 1)
                                if n >= 1 and f == 0:
                                    dve.wait_ge(s["out"], QT_B * n)
                                dve.tensor_tensor(hid[:, f, :], c.PS[:, 2 * (i % 2) + 1, :], silu[:, i % 2, :],
                                                  ALU.mult).then_inc(s["hid"], 1)
                            for t in range(QT_B):
                                i = n * QT_B + t
                                dve.wait_ge(s["out"], i + 1)
                                add_scaled(dve, c, 4, c.X[:, i, :], c.PS[:, 4 + i % 4, 0:D]).then_inc(s["added"], 1)
        finish_loads(c, experts)
        expert_tiles(c, "f0_e", ctx, tile_expert, xs, ys, (Wg, Wu), Wd, FF0, True)
        collect(c, "f0_c", place, ys, 4)



FF2 = 1024
CAPACITY = -(-T * 5 // (E * 4))


def layer2_ffn(c, w, consts, xs, ys):
    nc = c.nc
    with ExitStack() as ctx:
        sb = lambda n, shape, dt=F32: c.sb(ctx, "f2_" + n, shape, dt)
        W1a, W1b = sb("W1a", [P, DK, E, 512]), sb("W1b", [P, DK, E, 512])
        place, tile_expert = sb("place", [P, NT], I32), sb("tile_expert", [P, SLOT_TILES], I32)
        c.XN, expert = sb("XN", [P, NT, D]), sb("expert", [P, NT])
        with ExitStack() as early:
            tb = lambda n, shape, dt=F32: c.sb(early, "f2_" + n, shape, dt)
            c.XNT = tb("XNT", [P, DK, T])
            router, earlier, numbers = tb("router", [P, DK, E]), tb("earlier", [P, P]), tb("numbers", [P, NT, E])
            logits, best = tb("logits", [P, NT, E]), tb("best", [P, NT])
            tot, eq, rank, keep = tb("tot", [P, NT]), tb("eq", [P, NT, E]), tb("rank", [P, NT]), tb("keep", [P, NT])
            p_rows, e_rows = tb("p_rows", [P, T]), tb("e_rows", [P, T])
            part = tb("part", [P, NT, 4])
            small = start_loads(c, "f2", [(router[:, :, :], w["router_T"]), (earlier[:, :], consts["earlier"]),
                                          (numbers[:, :, :], consts["numbers"])])
            firsts = start_loads(c, "f2_w1", [
                (dst[:, k, :, :], w["W1"][:, k * P:(k + 1) * P, 512 * i:512 * (i + 1)].rearrange("e p n -> p e n"))
                for i, dst in enumerate((W1a, W1b)) for k in range(DK)])
            normalise(c, "f2_ln", c.X, c.XN, turned_into=c.XNT)
            finish_loads(c, small)
            token_logits(c, "f2_route", router, E, logits[:, :, :])
            v, exped = Tally(c.sem("f2_r_dve")), c.sem("f2_exped")
            wide = lambda ap: ap.unsqueeze(2).to_broadcast([P, NT, E])
            with nc.Block() as block:
                @block.vector
                def _(dve):
                    def then(ins):
                        dve.wait_ge(v.sem, v.mark(ins))
                    lg = logits[:, :, :]
                    then(dve.tensor_reduce(best[:, :], lg, X_AXIS, ALU.max))
                    then(dve.tensor_tensor(lg, lg, wide(best[:, :]), ALU.subtract))
                    dve.wait_ge(exped, 1)
                    then(dve.tensor_reduce(tot[:, :], lg, X_AXIS, ALU.add))
                    then(dve.reciprocal(tot[:, :], tot[:, :]))
                    then(dve.tensor_tensor(lg, lg, wide(tot[:, :]), ALU.mult))
                    then(dve.tensor_reduce(best[:, :], lg, X_AXIS, ALU.max))
                    first_best(c, dve, then, lg, best[:, :], expert[:, :], eq[:, :, :], numbers[:, :, :])

                @block.scalar
                def _(act):
                    act.wait_ge(v.sem, 2)
                    act.activation(logits[:, :, :], logits[:, :, :], ACT.Exp).then_inc(exped, 1)
            with ExitStack() as tmp:
                rows_of_columns(c, "f2_p", tmp, best, p_rows)
            with ExitStack() as tmp:
                rows_of_columns(c, "f2_e", tmp, expert, e_rows)
            with ExitStack() as tmp:
                same, junk = c.sb(tmp, "f2_same", [P, 2, T], BF16), c.sb(tmp, "f2_junk", [P, 2, T], BF16)
                diag, junk2 = c.sb(tmp, "f2_diag", [P, 2, P]), c.sb(tmp, "f2_junk2", [P, 2, P])
                k = Tally(c.sem("f2_k_dve"))
                with nc.Block() as block:
                    @block.vector
                    def _(dve):
                        then = lambda ins: k.mark(ins)
                        then(dve.memset(part[:, :, :], 0.0))
                        dve.wait_ge(k.sem, 1)
                        for t in range(NT):
                            r2 = t % 2
                            key = best[:, t:t + 1]
                            if t >= 2:
                                dve.wait_ge(k.sem, k.n - 5 if t != 2 and t != NT - 1 else k.n)
                            then(dve.tensor_scalar(same[:, r2, :], e_rows[:, :], expert[:, t:t + 1], None, ALU.is_equal))
                            dve.wait_ge(k.sem, k.n)
                            then(dve.tensor_tensor(diag[:, r2, :], earlier[:, :], same[:, r2, t * P:(t + 1) * P], ALU.mult))
                            dve.wait_ge(k.sem, k.n)
                            for i, (lo, hi, op) in enumerate(((0, t * P, ALU.is_ge), (t * P, T, ALU.is_gt))):
                                if lo < hi:
                                    then(dve.scalar_tensor_tensor(
                                        out=junk[:, r2, lo:hi], in0=p_rows[:, lo:hi], scalar=key,
                                        in1=same[:, r2, lo:hi], op0=op, op1=ALU.mult, accum_out=part[:, t, i:i + 1]))
                            then(dve.scalar_tensor_tensor(
                                out=junk2[:, r2, :], in0=p_rows[:, t * P:(t + 1) * P], scalar=key,
                                in1=diag[:, r2, :], op0=ALU.is_equal, op1=ALU.mult, accum_out=part[:, t, 2:3]))
                        dve.wait_ge(k.sem, k.n)
                        then(dve.tensor_reduce(rank[:, :], part[:, :, :], X_AXIS, ALU.add))
                        dve.wait_ge(k.sem, k.n)
                        then(dve.tensor_scalar(keep[:, :], rank[:, :], float(CAPACITY), None, ALU.is_lt))
                        dve.wait_ge(k.sem, k.n)
                        then(dve.tensor_tensor(expert[:, :], expert[:, :], keep[:, :], ALU.mult))
        W2 = sb("W2", [P, FF2 // P, E, D])
        seconds = []
        dispatch(c, "f2_d", place, tile_expert, expert[:, :], c.XN, consts, xs, meanwhile=lambda: seconds.extend(
            start_loads(c, "f2_w2", [(W2[:, k, :, :], w["W2"][:, k * P:(k + 1) * P, :].rearrange("e p n -> p e n"))
                                     for k in range(FF2 // P)])))
        finish_loads(c, firsts, seconds)
        expert_tiles(c, "f2_e", ctx, tile_expert, xs, ys, (W1a, W1b), W2, FF2, False, (w["b1"], w["b2"]))
        collect(c, "f2_c", place, ys, 6)


def store(c, out):
    stored = c.sem("stored")
    with c.nc.Block() as block:
        @block.sync
        def _(sp):
            sp.dma_start(out.rearrange("b (t p) d -> p (b t) d", p=P), c.X[:, :, :]).then_inc(stored, 16)
            sp.wait_ge(stored, 16)


def build(nc, a, out):
    with ExitStack() as ctx:
        c = Core(nc, ctx)
        scratch = {n: nc.dram_tensor("parts_" + n, (3, D, T), BF16).ap() for n in ("q", "k", "c")}
        xs = nc.dram_tensor("expert_in", (SLOT_TILES * P, D), F32).ap()
        ys = nc.dram_tensor("expert_out", (SLOT_TILES * P, D), F32).ap()
        prologue(c, a["x"], a["g_xattn"], a["g_ffn"])
        part = lambda prefix: {k[len(prefix):]: v for k, v in a.items() if k.startswith(prefix)}
        stages = [
            lambda: layer0_attention(c, a["ctx_T"], a["seg_T"], part("L0_xattn_"), a["rope_tables"],
                                     nc.dram_tensor("near_keys", (B * TABLE_ROWS, NEAR * P), F32).ap(), xs),
            lambda: layer0_ffn(c, part("L0_ffn_"), part("const_"), xs, ys),
            lambda: layer1_attention(c, a["ctx_T"], a["ctx_rows"], part("L1_xattn_")),
            lambda: layer1_ffn(c, part("L1_ffn_"), part("const_"), scratch),
            lambda: layer2_attention(c, a["ctx_T"], a["ctx_rows"], a["mask_BxS2_ik0"], part("L2_xattn_"),
                                     part("const_"), scratch),
            lambda: layer2_ffn(c, part("L2_ffn_"), part("const_"), xs, ys),
            lambda: layer3_attention(c, a["ctx_T"], part("L3_xattn_"), scratch),
            lambda: layer3_ffn(c, part("L3_ffn_")),
        ]
        for st in stages:
            st()
            c.end_stage()
        store(c, out)




def rope_tables():
    half = HD // 2
    inv = (1.0 / 10000.0 ** (np.arange(half, dtype=np.float32) / np.float32(half))).astype(np.float32)
    ang = (np.arange(S, dtype=np.float32)[:, None] * inv[None, :]).astype(np.float32)
    cos, sin = np.cos(ang), np.sin(ang)
    tabs = np.stack([np.concatenate([cos, cos], axis=1), np.concatenate([-sin, sin], axis=1)], axis=1)
    return tabs.reshape(QT_B, P, 2, HD).transpose(1, 0, 2, 3).astype(np.float32)


def head_slots(v):
    out = np.zeros((4, SLOT, 4, v.shape[1]), np.float32)
    out[:, :DH] = v.reshape(4, 4, DH, -1).transpose(1, 2, 0, 3)
    return out.reshape(P, 4, -1)


def kernel(**inputs):
    import concourse.bacc as _bacc
    from concourse.bass_utils import run_bass_kernel_spmd as _run

    nc = _bacc.Bacc("TRN2", target_bir_lowering=False, num_devices=1)
    arrays, args = {}, {}
    given = dict(inputs)
    given["rope_tables"] = rope_tables()
    rows_first = lambda v: v.reshape(DK, P, -1).transpose(1, 0, 2)
    width_first = lambda v: np.transpose(np.reshape(v, (-1, DK, P)), (2, 1, 0))
    heads_T = lambda v: np.transpose(np.reshape(v, (v.shape[0], H, -1)), (2, 1, 0))
    given["ctx_T"] = width_first(np.asarray(inputs["ctx_1024"]))
    given["seg_T"] = np.asarray(inputs["itok_BxS_0_511"]).reshape(NT, P).T
    for name in ("w_q_up", "w_k_up", "w_v_up"):
        given[f"L0_xattn_{name}_T"] = heads_T(np.asarray(inputs[f"L0_xattn_{name}"]))
    given["ctx_rows"] = np.asarray(inputs["ctx_1024"]).reshape(NT, P, D).transpose(1, 0, 2)
    given["L1_xattn_W_l_T"] = np.asarray(inputs["L1_xattn_W_l"]).T.reshape(4, DK, P, D).transpose(2, 0, 1, 3)
    given["L1_xattn_vecs"] = np.stack([np.asarray(inputs["L1_xattn_" + n]).reshape(DK, P).T
                                       for n in ("w_cq", "w_c", "w_q")], axis=1)
    given["L1_ffn_Wg_cols"] = rows_first(np.asarray(inputs["L1_ffn_Wg"]))
    given["L1_ffn_Wo_slots"] = head_slots(np.asarray(inputs["L1_ffn_Wo"]))
    A2 = {k: np.asarray(inputs["L2_xattn_" + k]) for k in ("Wq", "Wk", "Wv", "bq", "bk", "bv")}
    for n in "qk":
        given[f"L2_xattn_W{n}T"] = A2["W" + n].reshape(D, HID).T
        given[f"L2_xattn_W{n}_rows"] = rows_first(A2["W" + n].reshape(D, HID))
        given[f"L2_xattn_b{n}_rows"] = rows_first(np.repeat(A2["b" + n], DH, axis=0))
    slots = np.zeros((HID, H, P), np.float32)
    for h in range(H):
        slots[:, h, SLOT * (h % 4):SLOT * (h % 4) + DH] = A2["Wv"][h].T
    given["L2_xattn_Wv_slots"] = slots
    given["L2_xattn_bvT"] = A2["bv"].T
    for n in "qkv":
        given[f"L3_xattn_W{n}_T"] = rows_first(np.asarray(inputs[f"L3_xattn_W{n}"]).T)
    for n in "qk":
        given[f"L3_xattn_b{n}_cols"] = np.asarray(inputs[f"L3_xattn_b{n}"]).reshape(DK, P).T
    given["L3_xattn_Wo_slots"] = head_slots(np.asarray(inputs["L3_xattn_Wo"]).T)
    given["L3_ffn_W1_T"] = rows_first(np.asarray(inputs["L3_ffn_W1"]).T)
    given["L3_ffn_W2_T"] = np.asarray(inputs["L3_ffn_W2"]).T.reshape(FF3 // P, P, D).transpose(1, 0, 2)
    given["L3_ffn_b1_cols"] = np.asarray(inputs["L3_ffn_b1"]).reshape(FF3 // P, P).T
    p = np.arange(P)
    given["const_blocks"] = (p[:, None] // DH == p[None, :] // DH).astype(np.float32)
    given["const_heads"] = rows_first((np.arange(D)[:, None] // DH == np.arange(H)[None, :]).astype(np.float32))
    given["const_later"] = (p[None, :] > p[:, None]).astype(np.float32)
    given["const_numbers"] = np.broadcast_to(np.arange(E, dtype=np.float32), (P, NT, E))
    given["const_tile_numbers"] = np.broadcast_to(np.arange(SLOT_TILES, dtype=np.float32)[:, None],
                                                  (P, SLOT_TILES, E))
    given["L2_ffn_router_T"] = rows_first(np.asarray(inputs["L2_ffn_router_w"]).T)
    given["const_earlier"] = (p[None, :] < p[:, None]).astype(np.float32)
    for name, value in given.items():
        v = np.ascontiguousarray(value)
        if v.ndim == 0:
            v = v.reshape(1)
        arrays[f"in_{name}_dram"] = v
        args[name] = nc.dram_tensor(f"in_{name}_dram", v.shape, mybir.dt.from_np(v.dtype), kind="ExternalInput").ap()
    out = nc.dram_tensor("out_0_dram", (B, S, D), F32, kind="ExternalOutput").ap()
    build(nc, args, out)
    r = _run(nc, [arrays], core_ids=[0])
    return r.results[0]["out_0_dram"]
```
